# Optimizing a Trainium2 kernel written in Bass

```python
import numpy as np
import jax
import jax.numpy as jnp

def _softmax(x, axis=-1):
    return jax.nn.softmax(x, axis=axis)

def _gelu(x):
    return jax.nn.gelu(x, approximate=True)

def _silu(x):
    return jax.nn.silu(x)

def _sigmoid(x):
    return jax.nn.sigmoid(x)

def _layernorm(x, axis=-1, eps=1e-05):
    m = jnp.mean(x, axis=axis, keepdims=True)
    v = jnp.var(x, axis=axis, keepdims=True)
    return (x - m) / jnp.sqrt(v + eps)

def _scatter_add(tgt, idx, src, axis=0):
    return tgt.at[idx].add(src)

def _segment_sum(src, seg, n):
    return jax.ops.segment_sum(src, seg, n)
kernel_name = 'mk_flamingo_gated_d4_seqx_r4_a2fc7a'

def setup_inputs(seed: int=0):
    np.random.seed(seed)
    _w = jnp.asarray

    def _rec_inputs():
        import jax
        import jax.numpy as jnp
        _rk = jax.random.key(seed)
        x = -0.0002928 + 1 * jax.random.normal(jax.random.fold_in(_rk, 1), (8, 256, 256), jnp.float32)
        _lenS = 256 - jax.random.randint(jax.random.fold_in(_rk, 7), (8,), 0, max(1, 256 // 4) + 1, jnp.int32)
        _lenS2 = 256 - jax.random.randint(jax.random.fold_in(_rk, 8), (8,), 0, max(1, 256 // 4) + 1, jnp.int32)
        _ctx_1024P = jax.random.normal(jax.random.fold_in(_rk, 11), (8, 16, 256), jnp.float32)
        _ctx_1024c = jax.random.dirichlet(jax.random.fold_in(_rk, 511), 0.3 * jnp.ones((16,), jnp.float32), (8, 256))
        _ctx_1024t = jnp.einsum('bsk,bkd->bsd', _ctx_1024c, _ctx_1024P)
        _ctx_1024t = _ctx_1024t * jax.lax.rsqrt(jnp.mean(jnp.square(_ctx_1024t)) + 1e-12) * 0.953939
        ctx_1024 = -1.39393e-06 + 0.999914 * (_ctx_1024t + 0.3 * jax.random.normal(jax.random.fold_in(_rk, 611), (8, 256, 256), jnp.float32))
        fside_SxS2_0 = 0.00086875 + 0.999764 * jax.random.normal(jax.random.fold_in(_rk, 13), (256, 256), jnp.float32)
        _validS = jnp.arange(256)[None, :] < _lenS[:, None]
        _validS2 = jnp.arange(256)[None, :] < _lenS2[:, None]
        _causal = jnp.tril(jnp.ones((256, 256), dtype=bool))
        mask_BxS2_bf1 = jnp.ones((8, 256), dtype=bool)
        _g = jax.random.normal(jax.random.fold_in(_rk, 9001), (2, 4), jnp.float32)
        _g = jnp.sign(_g) * jnp.maximum(jnp.abs(_g), 1.0) + (_g == 0) * 1.0
        g_xattn = _g[0]
        g_ffn = _g[1]
        return (x, ctx_1024, fside_SxS2_0, mask_BxS2_bf1, g_xattn, g_ffn)
    x, ctx_1024, fside_SxS2_0, mask_BxS2_bf1, g_xattn, g_ffn = _rec_inputs()

    def _L0_xattn_setup():
        import jax, jax.numpy as jnp
        import numpy as np
        HEADS = 16
        CAUSAL = True
        NEG_BIAS = 999999.0
        key = jax.random.key(seed)
        k1, k2, k3 = jax.random.split(key, 3)
        B, Sq, Sk, C = (2, 512, 512, 256)
        return {'queries': jax.random.normal(k1, (B, Sq, C), dtype=jnp.float32), 'keys': jax.random.normal(k2, (B, Sk, C), dtype=jnp.float32), 'values': jax.random.normal(k3, (B, Sk, C), dtype=jnp.float32), 'queries_mask': jnp.ones((B, Sq), dtype=bool), 'values_mask': jnp.ones((B, Sk), dtype=bool)}
    _L0_xattn_all = _L0_xattn_setup()
    _L0_xattn_in = {k: v for k, v in _L0_xattn_all.items() if k in ()}
    del _L0_xattn_all

    def _L0_ffn_setup():
        import jax, jax.numpy as jnp
        import numpy as np
        S, B, D, H, DH = (1024, 8, 256, 16, 64)

        def _forward(x, Wg, Wq, bq, Wkv, bkv, Wo, bo, ln_g, ln_b):
            s_len, bsz, d_model = x.shape
            n_head, _, d_head = Wq.shape
            cap = s_len // n_head
            scale = 1.0 / d_head ** 0.5
            h = jnp.transpose(x, (1, 0, 2))
            t = h
            probs = jax.nn.softmax(h @ Wg, axis=-1)
            scores = jnp.transpose(probs, (0, 2, 1))
            _, idx = jax.lax.top_k(scores, cap)
            idx = jnp.sort(idx, axis=-1)
            hg = jnp.take_along_axis(h[:, None, :, :], idx[..., None], axis=2)
            hg = jnp.transpose(hg, (1, 0, 2, 3))
            q = jnp.einsum('hbcd,hde->hbce', hg, Wq) + bq[:, None, None, :]
            kv = jnp.einsum('hbcd,hde->hbce', hg, Wkv) + bkv[:, None, None, :]
            k, v = jnp.split(kv, 2, axis=-1)
            att = jnp.einsum('hbid,hbjd->hbij', q, k) * scale
            p = jax.nn.softmax(att, axis=1)
            av = jnp.einsum('hbij,hbjd->hbid', p, v)
            ao = jnp.einsum('hbid,hde->hbie', av, Wo) + bo
            tok = jnp.transpose(idx, (1, 0, 2))
            b_ids = jnp.arange(bsz)[None, :, None]
            outs = jnp.zeros_like(t).at[b_ids, tok].add(ao)
            y = t + outs
            mu = jnp.mean(y, axis=-1, keepdims=True)
            var = jnp.var(y, axis=-1, keepdims=True)
            yn = (y - mu) * jax.lax.rsqrt(var + 1e-05) * ln_g + ln_b
            return jnp.transpose(yn, (1, 0, 2))
        key = jax.random.key(seed)
        ks = jax.random.split(key, 6)
        s = 0.02
        return {'x': jax.random.normal(ks[0], (S, B, D), jnp.float32), 'attn_mask': jnp.zeros((S, S), jnp.bool_), 'Wg': jax.random.normal(ks[1], (D, H), jnp.float32) * s, 'Wq': jax.random.normal(ks[2], (H, D, DH), jnp.float32) * s, 'bq': jnp.zeros((H, DH), jnp.float32), 'Wkv': jax.random.normal(ks[3], (H, D, 2 * DH), jnp.float32) * s, 'bkv': jnp.zeros((H, 2 * DH), jnp.float32), 'Wo': jax.random.normal(ks[4], (H, DH, D), jnp.float32) * s, 'bo': jnp.zeros((D,), jnp.float32), 'ln_g': jnp.ones((D,), jnp.float32), 'ln_b': jnp.zeros((D,), jnp.float32)}
    _L0_ffn_all = _L0_ffn_setup()
    _L0_ffn_in = {k: v for k, v in _L0_ffn_all.items() if k in ('attn_mask', 'Wg', 'Wq', 'bq', 'Wkv', 'bkv', 'Wo', 'bo', 'ln_g', 'ln_b')}
    del _L0_ffn_all

    def _L1_xattn_setup():
        import jax, jax.numpy as jnp
        import numpy as np
        EMBED_PHI = 256
        EMBED_F = 256
        HIDDEN_F = 256
        N_HEADS = 16
        B, S = (2, 512)
        key = jax.random.key(seed)
        ks = jax.random.split(key, 9)
        sphi = 1.0 / np.sqrt(EMBED_PHI)
        sf = 1.0 / np.sqrt(EMBED_F)
        sh = 1.0 / np.sqrt(HIDDEN_F)
        return {'q': jax.random.normal(ks[0], (B, S, EMBED_PHI), jnp.float32), 'k': jax.random.normal(ks[1], (B, S, EMBED_PHI), jnp.float32), 'v': jax.random.normal(ks[2], (B, S, EMBED_F), jnp.float32), 'Wq': jax.random.normal(ks[3], (HIDDEN_F, EMBED_PHI), jnp.float32) * sphi, 'Wk': jax.random.normal(ks[4], (HIDDEN_F, EMBED_PHI), jnp.float32) * sphi, 'Wv': jax.random.normal(ks[5], (HIDDEN_F, EMBED_F), jnp.float32) * sf, 'bv': jax.random.normal(ks[6], (HIDDEN_F,), jnp.float32) * sf, 'Wo': jax.random.normal(ks[7], (EMBED_F, HIDDEN_F), jnp.float32) * sh, 'bo': jax.random.normal(ks[8], (EMBED_F,), jnp.float32) * sh}
    _L1_xattn_all = _L1_xattn_setup()
    _L1_xattn_in = {k: v for k, v in _L1_xattn_all.items() if k in ('Wq', 'Wk', 'Wv', 'bv', 'Wo', 'bo')}
    del _L1_xattn_all

    def _L1_ffn_setup():
        import jax, jax.numpy as jnp
        import numpy as np
        DIM = 256
        HID = 704
        N_ROUTED = 7
        TOPK = 2
        B, S = (4, 512)

        def _expert(x, wg, wu, wd):
            return jax.nn.silu(x @ wg) * (x @ wu) @ wd
        key = jax.random.key(seed)
        ks = jax.random.split(key, 9)
        s = 0.02
        x = jax.random.normal(ks[0], (B, S, DIM), jnp.float32)
        shared_gate = jax.random.normal(ks[1], (DIM, HID), jnp.float32) * s
        shared_up = jax.random.normal(ks[2], (DIM, HID), jnp.float32) * s
        shared_down = jax.random.normal(ks[3], (HID, DIM), jnp.float32) * s
        routed_gate = jax.random.normal(ks[4], (N_ROUTED, DIM, HID), jnp.float32) * s
        routed_up = jax.random.normal(ks[5], (N_ROUTED, DIM, HID), jnp.float32) * s
        routed_down = jax.random.normal(ks[6], (N_ROUTED, HID, DIM), jnp.float32) * s
        Wr = jax.random.normal(ks[7], (DIM, N_ROUTED), jnp.float32) * s
        routing_bias = jax.random.normal(ks[8], (N_ROUTED,), jnp.float32)
        return dict(x=x, shared_gate=shared_gate, shared_up=shared_up, shared_down=shared_down, routed_gate=routed_gate, routed_up=routed_up, routed_down=routed_down, Wr=Wr, routing_bias=routing_bias)
    _L1_ffn_all = _L1_ffn_setup()
    _L1_ffn_in = {k: v for k, v in _L1_ffn_all.items() if k in ('shared_gate', 'shared_up', 'shared_down', 'routed_gate', 'routed_up', 'routed_down', 'Wr', 'routing_bias')}
    del _L1_ffn_all

    def _L2_xattn_setup():
        import jax, jax.numpy as jnp
        import numpy as np
        N_HEAD, MODEL_DIM, KEY_DIM, VALUE_DIM = (16, 256, 64, 64)
        B, S = (4, 512)
        EPS = 1e-05
        TEMP = float(np.sqrt(KEY_DIM))
        key = jax.random.key(seed)
        ks = jax.random.split(key, 12)
        d = {'query': jax.random.normal(ks[0], (B, S, MODEL_DIM), jnp.float32), 'key': jax.random.normal(ks[1], (B, S, MODEL_DIM), jnp.float32), 'value': jax.random.normal(ks[2], (B, S, MODEL_DIM), jnp.float32), 'Wq': jax.random.normal(ks[3], (MODEL_DIM, N_HEAD * KEY_DIM), jnp.float32) * np.sqrt(2.0 / (MODEL_DIM + KEY_DIM)), 'bq': jnp.zeros((N_HEAD * KEY_DIM,), jnp.float32), 'Wk': jax.random.normal(ks[4], (MODEL_DIM, N_HEAD * KEY_DIM), jnp.float32) * np.sqrt(2.0 / (MODEL_DIM + KEY_DIM)), 'bk': jnp.zeros((N_HEAD * KEY_DIM,), jnp.float32), 'Wv': jax.random.normal(ks[5], (MODEL_DIM, N_HEAD * VALUE_DIM), jnp.float32) * np.sqrt(2.0 / (MODEL_DIM + VALUE_DIM)), 'bv': jnp.zeros((N_HEAD * VALUE_DIM,), jnp.float32), 'Wo': jax.random.normal(ks[6], (N_HEAD * VALUE_DIM, MODEL_DIM), jnp.float32) * np.sqrt(2.0 / (N_HEAD * VALUE_DIM + MODEL_DIM)), 'bo': jnp.zeros((MODEL_DIM,), jnp.float32), 'ln_gamma': jnp.ones((MODEL_DIM,), jnp.float32), 'ln_beta': jnp.zeros((MODEL_DIM,), jnp.float32)}
        return d
    _L2_xattn_all = _L2_xattn_setup()
    _L2_xattn_in = {k: v for k, v in _L2_xattn_all.items() if k in ('Wq', 'bq', 'Wk', 'bk', 'Wv', 'bv', 'Wo', 'bo', 'ln_gamma', 'ln_beta')}
    del _L2_xattn_all

    def _L2_ffn_setup():
        import jax, jax.numpy as jnp
        import numpy as np
        B, S, D, F, O = (4, 512, 256, 1024, 256)
        E, NS, K = (4, 2, 2)
        key = jax.random.key(seed)
        ks = jax.random.split(key, 6)

        def w(k, shape, fan_in):
            return jax.random.normal(k, shape, jnp.float32) * fan_in ** (-0.5)
        return {'x': jax.random.normal(ks[0], (B, S, D), jnp.float32), 'gate_w': w(ks[1], (D, E), D), 'gate_b': jnp.zeros((E,), jnp.float32), 'sw1': w(ks[2], (NS, D, F), D), 'sb1': jnp.zeros((NS, F), jnp.float32), 'sw2': w(ks[3], (NS, F, O), F), 'sb2': jnp.zeros((NS, O), jnp.float32), 'rw1': w(ks[4], (E, D, F), D), 'rb1': jnp.zeros((E, F), jnp.float32), 'rw2': w(ks[5], (E, F, O), F), 'rb2': jnp.zeros((E, O), jnp.float32)}
    _L2_ffn_all = _L2_ffn_setup()
    _L2_ffn_in = {k: v for k, v in _L2_ffn_all.items() if k in ('gate_w', 'gate_b', 'sw1', 'sb1', 'sw2', 'sb2', 'rw1', 'rb1', 'rw2', 'rb2')}
    del _L2_ffn_all

    def _L3_xattn_setup():
        import jax, jax.numpy as jnp
        import numpy as np
        NUM_HEADS = 16
        EPS = 1e-12
        MAX_SCALE_MUL = float(np.log(100.0))

        def _l2norm(t):
            n = jnp.sqrt(jnp.sum(t * t, axis=-1, keepdims=True))
            return t / jnp.maximum(n, EPS)
        key = jax.random.key(seed)
        ks = jax.random.split(key, 10)
        B, Lq, Ly, C = (4, 256, 512, 256)
        s = 1.0 / np.sqrt(C)
        return {'x': jax.random.normal(ks[0], (B, Lq, C), jnp.float32), 'y': jax.random.normal(ks[1], (B, Ly, C), jnp.float32), 'attn_bias': jax.random.normal(ks[2], (Lq, Ly), jnp.float32), 'Wq': jax.random.normal(ks[3], (C, C), jnp.float32) * s, 'bq': jnp.zeros((C,), jnp.float32), 'Wk': jax.random.normal(ks[4], (C, C), jnp.float32) * s, 'Wv': jax.random.normal(ks[5], (C, C), jnp.float32) * s, 'Wo': jax.random.normal(ks[6], (C, C), jnp.float32) * s, 'bo': jnp.zeros((C,), jnp.float32), 'scale_mul_log': jnp.full((1, NUM_HEADS, 1, 1), np.log(4.0), jnp.float32)}
    _L3_xattn_all = _L3_xattn_setup()
    _L3_xattn_in = {k: v for k, v in _L3_xattn_all.items() if k in ('Wq', 'bq', 'Wk', 'Wv', 'Wo', 'bo', 'scale_mul_log')}
    del _L3_xattn_all

    def _L3_ffn_setup():
        import jax, jax.numpy as jnp
        import numpy as np
        B, C, D = (2, 512, 256)
        I = 512
        E, K = (8, 2)
        CF = 1.25
        key = jax.random.key(seed)
        k1, k2, k3, k4 = jax.random.split(key, 4)
        scale = 0.02
        return {'hidden_states': jax.random.normal(k1, (B, C, D), jnp.float32), 'Wg': jax.random.normal(k2, (E, D), jnp.float32) * scale, 'W1': jax.random.normal(k3, (E, D, 2 * I), jnp.float32) * scale, 'W2': jax.random.normal(k4, (E, I, D), jnp.float32) * scale}
    _L3_ffn_all = _L3_ffn_setup()
    _L3_ffn_in = {k: v for k, v in _L3_ffn_all.items() if k in ('Wg', 'W1', 'W2')}
    del _L3_ffn_all
    return {'x': x, 'ctx_1024': ctx_1024, 'fside_SxS2_0': fside_SxS2_0, 'mask_BxS2_bf1': mask_BxS2_bf1, 'g_xattn': g_xattn, 'g_ffn': g_ffn, 'L0_ffn_attn_mask': _L0_ffn_in['attn_mask'], 'L0_ffn_Wg': _L0_ffn_in['Wg'], 'L0_ffn_Wq': _L0_ffn_in['Wq'], 'L0_ffn_bq': _L0_ffn_in['bq'], 'L0_ffn_Wkv': _L0_ffn_in['Wkv'], 'L0_ffn_bkv': _L0_ffn_in['bkv'], 'L0_ffn_Wo': _L0_ffn_in['Wo'], 'L0_ffn_bo': _L0_ffn_in['bo'], 'L0_ffn_ln_g': _L0_ffn_in['ln_g'], 'L0_ffn_ln_b': _L0_ffn_in['ln_b'], 'L1_xattn_Wq': _L1_xattn_in['Wq'], 'L1_xattn_Wk': _L1_xattn_in['Wk'], 'L1_xattn_Wv': _L1_xattn_in['Wv'], 'L1_xattn_bv': _L1_xattn_in['bv'], 'L1_xattn_Wo': _L1_xattn_in['Wo'], 'L1_xattn_bo': _L1_xattn_in['bo'], 'L1_ffn_shared_gate': _L1_ffn_in['shared_gate'], 'L1_ffn_shared_up': _L1_ffn_in['shared_up'], 'L1_ffn_shared_down': _L1_ffn_in['shared_down'], 'L1_ffn_routed_gate': _L1_ffn_in['routed_gate'], 'L1_ffn_routed_up': _L1_ffn_in['routed_up'], 'L1_ffn_routed_down': _L1_ffn_in['routed_down'], 'L1_ffn_Wr': _L1_ffn_in['Wr'], 'L1_ffn_routing_bias': _L1_ffn_in['routing_bias'], 'L2_xattn_Wq': _L2_xattn_in['Wq'], 'L2_xattn_bq': _L2_xattn_in['bq'], 'L2_xattn_Wk': _L2_xattn_in['Wk'], 'L2_xattn_bk': _L2_xattn_in['bk'], 'L2_xattn_Wv': _L2_xattn_in['Wv'], 'L2_xattn_bv': _L2_xattn_in['bv'], 'L2_xattn_Wo': _L2_xattn_in['Wo'], 'L2_xattn_bo': _L2_xattn_in['bo'], 'L2_xattn_ln_gamma': _L2_xattn_in['ln_gamma'], 'L2_xattn_ln_beta': _L2_xattn_in['ln_beta'], 'L2_ffn_gate_w': _L2_ffn_in['gate_w'], 'L2_ffn_gate_b': _L2_ffn_in['gate_b'], 'L2_ffn_sw1': _L2_ffn_in['sw1'], 'L2_ffn_sb1': _L2_ffn_in['sb1'], 'L2_ffn_sw2': _L2_ffn_in['sw2'], 'L2_ffn_sb2': _L2_ffn_in['sb2'], 'L2_ffn_rw1': _L2_ffn_in['rw1'], 'L2_ffn_rb1': _L2_ffn_in['rb1'], 'L2_ffn_rw2': _L2_ffn_in['rw2'], 'L2_ffn_rb2': _L2_ffn_in['rb2'], 'L3_xattn_Wq': _L3_xattn_in['Wq'], 'L3_xattn_bq': _L3_xattn_in['bq'], 'L3_xattn_Wk': _L3_xattn_in['Wk'], 'L3_xattn_Wv': _L3_xattn_in['Wv'], 'L3_xattn_Wo': _L3_xattn_in['Wo'], 'L3_xattn_bo': _L3_xattn_in['bo'], 'L3_xattn_scale_mul_log': _L3_xattn_in['scale_mul_log'], 'L3_ffn_Wg': _L3_ffn_in['Wg'], 'L3_ffn_W1': _L3_ffn_in['W1'], 'L3_ffn_W2': _L3_ffn_in['W2']}

def reference(x, ctx_1024, fside_SxS2_0, mask_BxS2_bf1, g_xattn, g_ffn, L0_ffn_attn_mask, L0_ffn_Wg, L0_ffn_Wq, L0_ffn_bq, L0_ffn_Wkv, L0_ffn_bkv, L0_ffn_Wo, L0_ffn_bo, L0_ffn_ln_g, L0_ffn_ln_b, L1_xattn_Wq, L1_xattn_Wk, L1_xattn_Wv, L1_xattn_bv, L1_xattn_Wo, L1_xattn_bo, L1_ffn_shared_gate, L1_ffn_shared_up, L1_ffn_shared_down, L1_ffn_routed_gate, L1_ffn_routed_up, L1_ffn_routed_down, L1_ffn_Wr, L1_ffn_routing_bias, L2_xattn_Wq, L2_xattn_bq, L2_xattn_Wk, L2_xattn_bk, L2_xattn_Wv, L2_xattn_bv, L2_xattn_Wo, L2_xattn_bo, L2_xattn_ln_gamma, L2_xattn_ln_beta, L2_ffn_gate_w, L2_ffn_gate_b, L2_ffn_sw1, L2_ffn_sb1, L2_ffn_sw2, L2_ffn_sb2, L2_ffn_rw1, L2_ffn_rb1, L2_ffn_rw2, L2_ffn_rb2, L3_xattn_Wq, L3_xattn_bq, L3_xattn_Wk, L3_xattn_Wv, L3_xattn_Wo, L3_xattn_bo, L3_xattn_scale_mul_log, L3_ffn_Wg, L3_ffn_W1, L3_ffn_W2):
    import jax
    import jax.numpy as jnp

    def _L0_xattn_ref(queries, keys, values, queries_mask, values_mask):
        import jax, jax.numpy as jnp
        import numpy as np
        HEADS = 16
        CAUSAL = True
        NEG_BIAS = 999999.0
        B, Sq, C = queries.shape
        Sk = keys.shape[1]
        H = HEADS
        d = C // H
        q = queries.reshape(B, Sq, H, d).transpose(2, 0, 1, 3)
        k = keys.reshape(B, Sk, H, d).transpose(2, 0, 1, 3)
        v = values.reshape(B, Sk, H, d).transpose(2, 0, 1, 3)
        scale = jnp.sqrt(jnp.float32(d))
        scores = jnp.einsum('hbqd,hbkd->hbqk', q, k) / scale
        mask = values_mask[None, :, None, :]
        if CAUSAL:
            causal = jnp.arange(Sq)[:, None] >= jnp.arange(Sk)[None, :]
            mask = jnp.logical_and(mask, causal[None, None])
        weights = jax.nn.softmax(scores - NEG_BIAS * mask.astype(jnp.float32), axis=-1)
        out = jnp.einsum('hbqk,hbkd->hbqd', weights, v)
        out = out.transpose(1, 2, 0, 3).reshape(B, Sq, C)
        return jnp.where(queries_mask[:, :, None], out, jnp.zeros_like(out))

    def _L0_ffn_ref(x, attn_mask, Wg, Wq, bq, Wkv, bkv, Wo, bo, ln_g, ln_b):
        import jax, jax.numpy as jnp
        import numpy as np
        S, B, D, H, DH = (1024, 8, 256, 16, 64)

        def _forward(x, Wg, Wq, bq, Wkv, bkv, Wo, bo, ln_g, ln_b):
            s_len, bsz, d_model = x.shape
            n_head, _, d_head = Wq.shape
            cap = s_len // n_head
            scale = 1.0 / d_head ** 0.5
            h = jnp.transpose(x, (1, 0, 2))
            t = h
            probs = jax.nn.softmax(h @ Wg, axis=-1)
            scores = jnp.transpose(probs, (0, 2, 1))
            _, idx = jax.lax.top_k(scores, cap)
            idx = jnp.sort(idx, axis=-1)
            hg = jnp.take_along_axis(h[:, None, :, :], idx[..., None], axis=2)
            hg = jnp.transpose(hg, (1, 0, 2, 3))
            q = jnp.einsum('hbcd,hde->hbce', hg, Wq) + bq[:, None, None, :]
            kv = jnp.einsum('hbcd,hde->hbce', hg, Wkv) + bkv[:, None, None, :]
            k, v = jnp.split(kv, 2, axis=-1)
            att = jnp.einsum('hbid,hbjd->hbij', q, k) * scale
            p = jax.nn.softmax(att, axis=1)
            av = jnp.einsum('hbij,hbjd->hbid', p, v)
            ao = jnp.einsum('hbid,hde->hbie', av, Wo) + bo
            tok = jnp.transpose(idx, (1, 0, 2))
            b_ids = jnp.arange(bsz)[None, :, None]
            outs = jnp.zeros_like(t).at[b_ids, tok].add(ao)
            y = t + outs
            mu = jnp.mean(y, axis=-1, keepdims=True)
            var = jnp.var(y, axis=-1, keepdims=True)
            yn = (y - mu) * jax.lax.rsqrt(var + 1e-05) * ln_g + ln_b
            return jnp.transpose(yn, (1, 0, 2))
        return _forward(x, Wg, Wq, bq, Wkv, bkv, Wo, bo, ln_g, ln_b)

    def _L1_xattn_ref(q, k, v, Wq, Wk, Wv, bv, Wo, bo):
        import jax, jax.numpy as jnp
        import numpy as np
        EMBED_PHI = 256
        EMBED_F = 256
        HIDDEN_F = 256
        N_HEADS = 16
        B, S = (2, 512)
        Bq, Sq, _ = q.shape
        hd = HIDDEN_F // N_HEADS
        scale = 1.0 / np.sqrt(hd)
        qh = (q @ Wq.T).reshape(Bq, Sq, N_HEADS, hd).transpose(0, 2, 1, 3)
        kh = (k @ Wk.T).reshape(Bq, Sq, N_HEADS, hd).transpose(0, 2, 1, 3)
        vh = (v @ Wv.T + bv).reshape(Bq, Sq, N_HEADS, hd).transpose(0, 2, 1, 3)
        scores = jnp.einsum('bhsd,bhtd->bhst', qh, kh) * scale
        mask = jnp.triu(jnp.ones((Sq, Sq), dtype=bool), k=0).at[0, 0].set(False)
        scores = jnp.where(mask, -jnp.inf, scores)
        probs = jax.nn.softmax(scores, axis=-1)
        out = jnp.einsum('bhst,bhtd->bhsd', probs, vh)
        out = out.transpose(0, 2, 1, 3).reshape(Bq, Sq, HIDDEN_F)
        return out @ Wo.T + bo

    def _L1_ffn_ref(x, shared_gate, shared_up, shared_down, routed_gate, routed_up, routed_down, Wr, routing_bias):
        import jax, jax.numpy as jnp
        import numpy as np
        DIM = 256
        HID = 704
        N_ROUTED = 7
        TOPK = 2
        B, S = (4, 512)

        def _expert(x, wg, wu, wd):
            return jax.nn.silu(x @ wg) * (x @ wu) @ wd
        b, s, d = x.shape
        n_exp = routed_gate.shape[0]
        shared_out = _expert(x, shared_gate, shared_up, shared_down)
        logits = x @ Wr * routing_bias
        probs = jax.nn.sigmoid(logits)
        scores, idx = jax.lax.top_k(probs, TOPK)
        scores = scores / scores.sum(-1, keepdims=True)
        t = b * s
        xf = x.reshape(t, d)
        weights = jnp.zeros((t, n_exp), x.dtype).at[jnp.arange(t)[:, None], idx.reshape(t, TOPK)].add(scores.reshape(t, TOPK))
        combined = jnp.zeros_like(xf)
        for e in range(n_exp):
            combined = combined + _expert(xf, routed_gate[e], routed_up[e], routed_down[e]) * weights[:, e:e + 1]
        return shared_out + combined.reshape(b, s, d)

    def _L2_xattn_ref(query, key, value, Wq, bq, Wk, bk, Wv, bv, Wo, bo, ln_gamma, ln_beta):
        import jax, jax.numpy as jnp
        import numpy as np
        N_HEAD, MODEL_DIM, KEY_DIM, VALUE_DIM = (16, 256, 64, 64)
        B, S = (4, 512)
        EPS = 1e-05
        TEMP = float(np.sqrt(KEY_DIM))
        b, sq, _ = query.shape
        residual = query
        q = (query @ Wq + bq).reshape(b, sq, N_HEAD, KEY_DIM)
        k = (key @ Wk + bk).reshape(b, key.shape[1], N_HEAD, KEY_DIM)
        v = (value @ Wv + bv).reshape(b, value.shape[1], N_HEAD, VALUE_DIM)
        scores = jnp.einsum('bqhd,bkhd->bhqk', q, k) / TEMP
        attn = jax.nn.softmax(scores, axis=-1)
        out = jnp.einsum('bhqk,bkhd->bqhd', attn, v).reshape(b, sq, N_HEAD * VALUE_DIM)
        out = out @ Wo + bo + residual
        mu = jnp.mean(out, axis=-1, keepdims=True)
        var = jnp.var(out, axis=-1, keepdims=True)
        return (out - mu) * jax.lax.rsqrt(var + EPS) * ln_gamma + ln_beta

    def _L2_ffn_ref(x, gate_w, gate_b, sw1, sb1, sw2, sb2, rw1, rb1, rw2, rb2):
        import jax, jax.numpy as jnp
        import numpy as np
        B, S, D, F, O = (4, 512, 256, 1024, 256)
        E, NS, K = (4, 2, 2)
        weights = jax.nn.softmax(x @ gate_w + gate_b, axis=-1)
        topk_w, topk_i = jax.lax.top_k(weights, K)
        sh = jax.nn.relu(jnp.einsum('bsd,ndf->bsnf', x, sw1) + sb1)
        shared = (jnp.einsum('bsnf,nfo->bsno', sh, sw2) + sb2).sum(axis=2) / NS
        rh = jax.nn.relu(jnp.einsum('bsd,edf->bsef', x, rw1) + rb1)
        eo = jnp.einsum('bsef,efo->bseo', rh, rw2) + rb2
        gathered = jnp.take_along_axis(eo, topk_i[..., None], axis=2)
        routed = (gathered * topk_w[..., None]).sum(axis=2)
        return shared + routed

    def _L3_xattn_ref(x, y, attn_bias, Wq, bq, Wk, Wv, Wo, bo, scale_mul_log):
        import jax, jax.numpy as jnp
        import numpy as np
        NUM_HEADS = 16
        EPS = 1e-12
        MAX_SCALE_MUL = float(np.log(100.0))

        def _l2norm(t):
            n = jnp.sqrt(jnp.sum(t * t, axis=-1, keepdims=True))
            return t / jnp.maximum(n, EPS)
        B, Lq, C = x.shape
        Ly = y.shape[1]
        H = NUM_HEADS
        D = C // H
        q = (x @ Wq + bq).reshape(B, Lq, H, D).transpose(0, 2, 1, 3)
        k = (y @ Wk).reshape(B, Ly, H, D).transpose(0, 2, 1, 3)
        v = (y @ Wv).reshape(B, Ly, H, D).transpose(0, 2, 1, 3)
        scale_mul = jnp.exp(jnp.minimum(scale_mul_log, MAX_SCALE_MUL))
        q = _l2norm(q) * scale_mul
        k = _l2norm(k)
        attn = jnp.einsum('bhqd,bhkd->bhqk', q, k) + attn_bias
        attn = jax.nn.softmax(attn, axis=-1)
        oup = jnp.einsum('bhqk,bhkd->bhqd', attn, v)
        oup = oup.transpose(0, 2, 1, 3).reshape(B, Lq, C)
        return oup @ Wo + bo

    def _L3_ffn_ref(hidden_states, Wg, W1, W2):
        import jax, jax.numpy as jnp
        import numpy as np
        B, C, D = (2, 512, 256)
        I = 512
        E, K = (8, 2)
        CF = 1.25
        Bx, Cx, d = hidden_states.shape
        N = Bx * Cx
        cap = int(N * K * CF / E)
        x = hidden_states.reshape(N, d)
        logits = x @ Wg.T
        top_v, top_i = jax.lax.top_k(logits, K)
        gates = jax.nn.softmax(top_v, axis=-1)
        flat_e = top_i.reshape(N * K)
        gates_f = gates.reshape(N * K)
        tok = jnp.repeat(jnp.arange(N), K)
        onehot = jax.nn.one_hot(flat_e, E, dtype=jnp.int32)
        pos = jnp.cumsum(onehot, axis=0) - 1
        pos_f = jnp.take_along_axis(pos, flat_e[:, None], axis=1)[:, 0]
        keep = pos_f < cap
        pos_safe = jnp.where(keep, pos_f, cap)
        exp_batches = jnp.zeros((E, cap, d), x.dtype).at[flat_e, pos_safe].set(x[tok], mode='drop')
        h = jnp.einsum('ecd,edf->ecf', exp_batches, W1)
        inp, gate = jnp.split(h, 2, axis=-1)
        h = jax.nn.gelu(inp, approximate=False) * gate
        exp_out = jnp.einsum('eci,eid->ecd', h, W2)
        gathered = exp_out[flat_e, jnp.minimum(pos_safe, cap - 1)]
        contrib = jnp.where(keep, gates_f, 0.0)[:, None] * gathered
        out = jax.ops.segment_sum(contrib, tok, num_segments=N)
        return out.reshape(Bx, Cx, d)
    x = x + jnp.tanh(g_xattn[0]) * _L0_xattn_ref(_layernorm(x, axis=-1), ctx_1024, ctx_1024, mask_BxS2_bf1, mask_BxS2_bf1)
    x = x + jnp.tanh(g_ffn[0]) * _L0_ffn_ref(_layernorm(x, axis=-1), L0_ffn_attn_mask, L0_ffn_Wg, L0_ffn_Wq, L0_ffn_bq, L0_ffn_Wkv, L0_ffn_bkv, L0_ffn_Wo, L0_ffn_bo, L0_ffn_ln_g, L0_ffn_ln_b)
    x = x + jnp.tanh(g_xattn[1]) * _L1_xattn_ref(_layernorm(x, axis=-1), ctx_1024, ctx_1024, L1_xattn_Wq, L1_xattn_Wk, L1_xattn_Wv, L1_xattn_bv, L1_xattn_Wo, L1_xattn_bo)
    x = x + jnp.tanh(g_ffn[1]) * _L1_ffn_ref(_layernorm(x, axis=-1), L1_ffn_shared_gate, L1_ffn_shared_up, L1_ffn_shared_down, L1_ffn_routed_gate, L1_ffn_routed_up, L1_ffn_routed_down, L1_ffn_Wr, L1_ffn_routing_bias)
    x = x + jnp.tanh(g_xattn[2]) * _L2_xattn_ref(_layernorm(x, axis=-1), ctx_1024, ctx_1024, L2_xattn_Wq, L2_xattn_bq, L2_xattn_Wk, L2_xattn_bk, L2_xattn_Wv, L2_xattn_bv, L2_xattn_Wo, L2_xattn_bo, L2_xattn_ln_gamma, L2_xattn_ln_beta)
    x = x + jnp.tanh(g_ffn[2]) * _L2_ffn_ref(_layernorm(x, axis=-1), L2_ffn_gate_w, L2_ffn_gate_b, L2_ffn_sw1, L2_ffn_sb1, L2_ffn_sw2, L2_ffn_sb2, L2_ffn_rw1, L2_ffn_rb1, L2_ffn_rw2, L2_ffn_rb2)
    x = x + jnp.tanh(g_xattn[3]) * _L3_xattn_ref(_layernorm(x, axis=-1), ctx_1024, fside_SxS2_0, L3_xattn_Wq, L3_xattn_bq, L3_xattn_Wk, L3_xattn_Wv, L3_xattn_Wo, L3_xattn_bo, L3_xattn_scale_mul_log)
    x = x + jnp.tanh(g_ffn[3]) * _L3_ffn_ref(_layernorm(x, axis=-1), L3_ffn_Wg, L3_ffn_W1, L3_ffn_W2)
    return x

_drawn_inputs = setup_inputs


def setup_inputs(seed=0):
    import zlib

    import numpy as np

    out = dict(_drawn_inputs(seed))
    spreads = {'L0_ffn_bq': (0.0, 0.1),
     'L0_ffn_bkv': (0.0, 0.1),
     'L0_ffn_bo': (0.0, 0.1),
     'L0_ffn_ln_g': (1.0, 0.2),
     'L0_ffn_ln_b': (0.0, 0.1),
     'L2_xattn_bq': (0.0, 0.1),
     'L2_xattn_bk': (0.0, 0.8),
     'L2_xattn_bv': (0.0, 0.1),
     'L2_xattn_bo': (0.0, 0.1),
     'L2_xattn_ln_gamma': (1.0, 0.2),
     'L2_xattn_ln_beta': (0.0, 0.1),
     'L2_ffn_gate_b': (0.0, 0.1),
     'L2_ffn_sb1': (0.0, 0.1),
     'L2_ffn_sb2': (0.0, 0.1),
     'L2_ffn_rb1': (0.0, 0.1),
     'L2_ffn_rb2': (0.0, 0.1),
     'L3_xattn_bq': (0.0, 0.408),
     'L3_xattn_bo': (0.0, 0.1),
     'L3_xattn_scale_mul_log': (1.3862943649291992, 0.2)}
    factors = {'g_ffn': 8.0,
     'L1_ffn_Wr': 2.777,
     'L1_ffn_routing_bias': 3.048,
     'L3_ffn_Wg': 3.735,
     'L3_ffn_W1': 3.42,
     'L3_ffn_W2': 3.436}
    for name, (base, spread) in spreads.items():
        noise = np.random.default_rng([zlib.crc32(name.encode()), seed]).standard_normal(out[name].shape)
        drawn = base * np.exp(spread * noise) if base else spread * noise
        out[name] = jnp.asarray(drawn.astype(out[name].dtype))
    for name, factor in factors.items():
        out[name] = (out[name] * factor).astype(out[name].dtype)
    return out
```

```python
from contextlib import ExitStack

import concourse.bass as bass
from concourse import mybir

F32 = mybir.dt.float32
U8 = mybir.dt.uint8
ALU = mybir.AluOpType
ACT = mybir.ActivationFunctionType
AX = mybir.AxisListType

P = 128
BATCH, SEQ, D = 8, 256, 256
TOK = BATCH * SEQ
TT = TOK // P
TPB = SEQ // P
DC = D // P
CH = 512
NCH = TOK // CH
TPC = CH // P
NH = 16
WE = 8
NEG_BIAS = 999999.0
MASKED = -1.0e30
BIG = 1.0e30
EPS = 1e-5
NORM_EPS2 = 1e-24
LOG_MAX_SCALE = 4.605170185988092
SS = 4
TS = 2
T_LAG, AV_LAG = 2, 3
FIN_AT = 5

F1, F1_LAST = 6, 64
F2 = 8
F3 = 4
E1, E2, E3 = 8, 6, 8
CAP = int(TOK * 2 * 1.25 / E3)


def build(nc, a, out, stop_after=8):
    with ExitStack() as ctx:
        def sb(name, shape, dt=F32):
            return ctx.enter_context(nc.sbuf_tensor(name, shape, dt))

        def sem(name):
            return ctx.enter_context(nc.semaphore(name))

        X = sb("X", [P, TT, D])
        Hn = sb("Hn", [P, TT, D])
        HT = sb("HT", [P, DC, TOK])
        CT = sb("CT", [P, DC, TOK])
        ACC = sb("ACC", [P, TT, D])
        arena = sb("arena", [P, 20480])
        ident = sb("ident", [P, P])
        ones = sb("ones", [P, P])
        tril = sb("tril", [P, P])
        headsum = sb("headsum", [P, P])
        rev = sb("rev", [P, TT, WE])
        maskE = sb("maskE", [P, 1])
        maskO = sb("maskO", [P, 1])
        eps = sb("eps", [P, 1])
        causal0 = sb("causal0", [P, TPB, SEQ])
        causal1 = sb("causal1", [P, TPB, SEQ])
        biasL = sb("biasL", [P, TPB, SEQ])
        fside = sb("fside", [P, TPB, SEQ])
        bo_bc = sb("bo_bc", [P, 3, D])
        graw = sb("graw", [P, 8])
        tg = sb("tg", [P, 8])
        lnst = sb("lnst", [P, TT, 6])
        lnmv = sb("lnmv", [P, TT, 2])
        lnsd = sb("lnsd", [P, TT])
        lnrs = sb("lnrs", [P, TT])
        qm8 = sb("qm8", [P, TT], U8)
        qm = sb("qm", [P, TT])
        Ssb = sb("Ssb", [P, SS, TPB, SEQ])
        Pb = sb("Pb", [P, SS, TPB, SEQ])
        PTb = sb("PTb", [P, TS, TPB, SEQ])
        nmax = sb("nmax", [P, SS, TPB])
        rsum = sb("rsum", [P, BATCH, TPB, NH])
        rrec = sb("rrec", [P, TPB, NH])
        xtmp = sb("xtmp", [P, TPB, D])
        wr = sb("wr", [P, 3, DC, WE])
        rbias = sb("rbias", [P, 2, WE])
        lg = sb("lg", [P, TT, WE])
        rt = sb("rt", [P, 4, TT, WE])
        oh1 = sb("oh1", [P, TT, WE])
        oh2 = sb("oh2", [P, TT, WE])
        r1 = sb("r1", [P, 4, TT])
        wts = sb("wts", [P, WE, TT])
        bqk = sb("bqk", [P, 2, 8])
        bq8 = sb("bq8", [P, 8])
        bq3 = sb("bq3", [P, DC])
        smul = sb("smul", [P, DC])
        psum = ctx.enter_context(nc.psum_tensor("psum", [P, 8, 512], F32))

        QTa = arena[:, 0:4096].rearrange("p (c t) -> p c t", c=DC)
        KTa = arena[:, 4096:8192].rearrange("p (c t) -> p c t", c=DC)
        Va = arena[:, 8192:12288].rearrange("p (t d) -> p t d", t=TT)
        Qs = arena[:, 12288:12800].rearrange("p (c t) -> p c t", c=DC)
        KE = arena[:, 12800:13312].rearrange("p (c t) -> p c t", c=DC)
        KO = arena[:, 13312:13824].rearrange("p (c t) -> p c t", c=DC)
        Vb = arena[:, 13824:14336].rearrange("p (t d) -> p t d", t=TPB)
        Osb = arena[:, 14336:14848].rearrange("p (t d) -> p t d", t=TPB)
        OTs = arena[:, 14848:15360].rearrange("p (c t) -> p c t", c=DC)
        Wsm = arena[:, 15360:17408].rearrange("p (w c n) -> p w c n", w=4, c=DC)
        mask8 = arena[:, 17408:17920].bitcast(U8)
        maskf = arena[:, 17920:19968]
        bv1 = arena[:, 19968:20224]
        lng = arena[:, 0:256]
        lnb = arena[:, 256:512]
        Wqkv = arena[:, 0:6144].rearrange("p (w c n) -> p w c n", w=3, c=DC)
        Wo2 = arena[:, 6144:8192].rearrange("p (c n) -> p c n", c=8)
        Q2 = arena[:, 8192:10240].rearrange("p (m t) -> p m t", m=8)
        K2 = arena[:, 10240:12288].rearrange("p (m t) -> p m t", m=8)
        V2 = arena[:, 12288:14336].rearrange("p (t n) -> p t n", t=TPB)
        O2 = arena[:, 14336:16384].rearrange("p (t n) -> p t n", t=TPB)
        OT2 = arena[:, 16384:18432].rearrange("p (m t) -> p m t", m=8)
        CTb = arena[:, 18432:18944].rearrange("p (c t) -> p c t", c=DC)
        bv2 = arena[:, 18944:19968]
        lng2 = arena[:, 19968:20224]
        lnb2 = arena[:, 20224:20480]
        WS = 4368
        wslot = [arena[:, s * WS:(s + 1) * WS] for s in range(2)]
        hid = arena[:, 2 * WS:2 * WS + 8192].rearrange("p (s f t) -> p s f t", s=2, f=8)
        sg = arena[:, 2 * WS + 8192:2 * WS + 9216].rearrange("p (s t) -> p s t", s=2)
        dtmp = arena[:, 2 * WS + 9216:2 * WS + 9728].rearrange("p (s d) -> p s d", s=2)
        b2bc = arena[:, 2 * WS + 9728:2 * WS + 10240].rearrange("p (s d) -> p s d", s=2)
        b1c = arena[:, 2 * WS + 10240:2 * WS + 10256].rearrange("p (s f) -> p s f", s=2)

        ld_x, ld_ctx, ld_small = sem("ld_x"), sem("ld_ctx"), sem("ld_small")
        ld_att = [sem(f"ld_att{i}") for i in range(4)]
        consts, dve_consts = sem("consts"), sem("dve_consts")
        tg_done = sem("tg_done")
        st_done, ag_done, sd_done, rs_done, h_done = (sem(n) for n in ("st_done", "ag_done", "sd_done", "rs_done", "h_done"))
        tp_done = [sem("tp_done0"), sem("tp_done1")]
        tpe_done = [sem("tpe_done0"), sem("tpe_done1")]
        x_upd = sem("x_upd")
        chain = sem("chain")
        act_chain = sem("act_chain")
        pj_mm = [sem("pj_mm0"), sem("pj_mm1")]
        pj_ev = [sem("pj_ev0"), sem("pj_ev1")]
        out_done = sem("out_done")

        class AttSems:
            def __init__(s, n):
                s.prep, s.vcopy, s.s, s.sm, s.p, s.t, s.pt, s.av, s.on, s.ot, s.oe, s.wo, s.ch, s.proj = (
                    sem(f"a{n}_{w}") for w in ("prep", "vcopy", "scores", "max", "probs", "ptrans", "pcopy", "pv",
                                               "onorm", "otrans", "ocopy", "wo", "chain", "proj"))
        att = [AttSems(n) for n in range(4)]
        mf = [sem("l2_filled6"), sem("l2_filled7")]
        me = [sem("l2_emptied6"), sem("l2_emptied7")]

        class FfnSems:
            def __init__(s, n):
                s.w = [sem(f"f{n}_w0"), sem(f"f{n}_w1")]
                s.up, s.act, s.hid, s.down, s.acc, s.lg, s.init = (
                    sem(f"f{n}_{w}") for w in ("up", "act", "hid", "down", "acc", "logits", "init"))
                s.tmp = sem(f"f{n}_tmp") if n == 2 else None
        ffn = [None] + [FfnSems(n) for n in (1, 2, 3)]
        pfx = sem("prefix")
        waited = sem("waited")

        def x_after(layer, ff):
            return 12 * layer + (12 if ff else 8)

        block = ctx.enter_context(nc.Block())

        def bs(b, n=SEQ):
            return slice(b * n, b * n + n) if isinstance(b, int) else bass.ds(b * n, n)

        def norm_stats(dve, m, src, ready=None):
            if ready is not None:
                dve.wait_ge(*ready)
            for t in range(TT):
                dve.bn_stats(lnst[:, t, :], src[:, t, :]).then_inc(st_done, 1)
            dve.wait_ge(st_done, TT * (m + 1))
            for t in range(TT):
                dve.bn_aggr(lnmv[:, t, :], lnst[:, t, :]).then_inc(ag_done, 1)

        def norm_sqrt(act, m):
            act.wait_ge(ag_done, TT * (m + 1))
            act.activation(lnsd[:, :], lnmv[:, :, 1], ACT.Sqrt, bias=eps[:, 0:1]).then_inc(sd_done, 1)

        def norm_apply(dve, m, src, dst):
            dve.wait_ge(sd_done, m + 1)
            dve.reciprocal(lnrs[:, :], lnsd[:, :]).then_inc(rs_done, 1)
            dve.wait_ge(rs_done, 5 * m + 1)
            dve.tensor_tensor(lnsd[:, :], lnrs[:, :], lnrs[:, :], ALU.mult).then_inc(rs_done, 1)
            dve.wait_ge(rs_done, 5 * m + 2)
            dve.scalar_tensor_tensor(out=lnsd[:, :], in0=lnmv[:, :, 1], scalar=eps[:, 0:1], in1=lnsd[:, :],
                                     op0=ALU.add, op1=ALU.mult).then_inc(rs_done, 1)
            dve.wait_ge(rs_done, 5 * m + 3)
            dve.tensor_scalar(lnsd[:, :], lnsd[:, :], -0.5, 1.5, ALU.mult, ALU.add).then_inc(rs_done, 1)
            dve.wait_ge(rs_done, 5 * m + 4)
            dve.tensor_tensor(lnrs[:, :], lnrs[:, :], lnsd[:, :], ALU.mult).then_inc(rs_done, 1)
            dve.wait_ge(rs_done, 5 * m + 5)
            for t in range(TT):
                dve.tensor_scalar(dst[:, t, :], src[:, t, :], lnmv[:, t, 0:1], lnrs[:, t:t + 1],
                                  ALU.subtract, ALU.mult).then_inc(h_done, 1)

        def transposes_pe(pe, n, src, ready):
            for g in range(TT // 4):
                ready(g)
                for c in range(DC):
                    if n or g:
                        pe.wait_ge(tpe_done[c], 4 * n + g)
                    for j in range(4):
                        mm = pe.transpose(psum[:, c, j * P:(j + 1) * P], src[:, 4 * g + j, c * P:(c + 1) * P],
                                          ident[:, :])
                    mm.then_inc(tp_done[c], 1)

        def transposes_copy_dve(dve, n, dst):
            for g in range(TT // 4):
                dve.wait_ge(tp_done[0], 4 * n + g + 1)
                dve.tensor_copy(dst[:, 0, g * 512:(g + 1) * 512], psum[:, 0, :]).then_inc(tpe_done[0], 1)

        def transposes_copy_act(act, n, dst):
            for g in range(TT // 4):
                act.wait_ge(tp_done[1], 4 * n + g + 1)
                act.activation(dst[:, 1, g * 512:(g + 1) * 512], psum[:, 1, :], ACT.Copy).then_inc(tpe_done[1], 1)

        def prepare_dve(dve, layer, b):
            s = att[layer]
            dve.wait_ge(s.s, b * NH + 1)
            scale = 1.0 if layer == 3 else 0.25
            QT, KT = (HT, CT) if layer == 0 else (QTa, KTa)
            for c in range(DC):
                dve.tensor_scalar(Qs[:, c, :], QT[:, c, bs(b)], scale, None, ALU.mult)
                dve.tensor_scalar(KE[:, c, :], KT[:, c, bs(b)], maskE[:, 0:1], None, ALU.mult)
                last = dve.tensor_scalar(KO[:, c, :], KT[:, c, bs(b)], maskO[:, 0:1], None, ALU.mult)
            if layer == 0:
                for qt in range(TPB):
                    last = dve.tensor_tensor(biasL[:, qt, :], causal0[:, qt, :], maskf[:, bs(b)], ALU.mult)
            last.then_inc(s.prep, 1)
            dve.wait_ge(s.prep, b + 1)
        def prepare_pool(pool, layer, b):
            s = att[layer]
            pool.wait_ge(s.av, b * NH + TS)
            pool.tensor_copy(Vb[:, :, :], Va[:, bs(b, TPB), :]).then_inc(s.vcopy, 1)

        def head_view(layer, h):
            if layer == 2:
                o, m = 64 * (h % 2), h // 2
                return (lambda x: x[o:o + 64, m, :]), Q2, K2
            o, m = 32 * ((h // 2) % 4), h // 8
            return (lambda x: x[o:o + 32, m, :]), Qs, (KE, KO)[h % 2]

        def score_bank(layer, h):
            return h % 2 if layer == 2 else (0, 1, 5, 6)[h % 4]

        def scores_pe(pe, layer, b, h):
            s = att[layer]
            if layer == 2:
                pe.wait_ge(s.p, b * NH + h + 1 - 2 + SS)
            else:
                pe.wait_ge(s.sm, b * NH + h + 1)
            part, q, k = head_view(layer, h)
            for qt in range(TPB):
                mm = pe.matmul(psum[:, score_bank(layer, h), qt * SEQ:(qt + 1) * SEQ],
                               part(q)[:, qt * P:(qt + 1) * P], part(k), start=True, stop=True)
            mm.then_inc(s.s, 1)

        def max_dve(dve, layer, b, h):
            s, k, bank = att[layer], h % SS, score_bank(layer, h)
            dve.wait_ge(s.s, b * NH + h + 2)
            dve.wait_ge(s.p, b * NH + h + 1)
            bias = {0: biasL, 1: causal1, 3: fside}.get(layer)
            if layer == 2:
                dve.tensor_reduce(nmax[:, k, :], psum[:, bank, :].rearrange("p (q k) -> p q k", q=TPB), AX.X, ALU.max,
                                  negate=True).then_inc(s.sm, 1)
                return
            dve.sem_inc(waited, 1)
            for qt in range(TPB):
                ins = dve.tensor_tensor_reduce(Ssb[:, k, qt, :], psum[:, bank, qt * SEQ:(qt + 1) * SEQ], bias[:, qt, :],
                                               -1.0, 3.0e38, ALU.add, ALU.min, nmax[:, k, qt:qt + 1])
            ins.then_inc(s.sm, 1)

        def exp_act(act, layer, b, h):
            s, k, bank = att[layer], h % SS, score_bank(layer, h)
            act.wait_ge(s.sm, b * NH + h + 1 + SS)
            act.wait_ge(s.t, b * NH + h + 1)
            for qt in range(TPB):
                src, sc = (psum[:, bank, qt * SEQ:(qt + 1) * SEQ], 1.0) if layer == 2 else (Ssb[:, k, qt, :], -1.0)
                acc = rsum[:, b, qt, h:h + 1] if isinstance(b, int) else rsum[:, bass.ds(b, 1), qt, h:h + 1]
                ins = act.activation(Pb[:, k, qt, :], src, ACT.Exp, bias=nmax[:, k, qt:qt + 1], scale=sc,
                                     accum_out=acc)
            ins.then_inc(s.p, 1)

        def ptrans_pe(pe, layer, b, h):
            s, j, k = att[layer], h % SS, 2 + h % TS
            pe.wait_ge(s.p, b * NH + h + 1 + SS)
            pe.wait_ge(s.pt, b * NH + h + 1)
            for kt in range(TPB):
                for qt in range(TPB):
                    mm = pe.transpose(psum[:, k, kt * SEQ + qt * P:kt * SEQ + (qt + 1) * P],
                                      Pb[:, j, qt, kt * P:(kt + 1) * P], ident[:, :])
            mm.then_inc(s.t, 1)

        def pcopy_dve(dve, layer, b, h):
            s, k = att[layer], h % TS
            dve.wait_ge(s.t, b * NH + h + 1 + SS)
            dve.wait_ge(s.av, b * NH + h + 1)
            dve.tensor_copy(PTb[:, k, :, :], psum[:, 2 + k, :].rearrange("p (k q) -> p k q", k=TPB)).then_inc(s.pt, 1)

        def pv_pe(pe, layer, b, h):
            s, k = att[layer], h % TS
            pe.wait_ge(s.pt, b * NH + h + 1 + TS)
            if layer == 2:
                if h % 4 == 0:
                    pe.wait_ge(s.on, b * 4 + h // 4 + 1)
                V, w, o = V2, 64, 64 * (h % 4)
            else:
                if h == 0:
                    pe.wait_ge(s.vcopy, b + 1)
                    pe.wait_ge(s.on, b + 1)
                V, w, o = Vb, 16, 16 * h
            c = 64 * h if layer == 2 else o
            for qt in range(TPB):
                for kt in range(TPB):
                    mm = pe.matmul(psum[:, 4, qt * SEQ + o:qt * SEQ + o + w], PTb[:, k, kt, qt * P:(qt + 1) * P],
                                   V[:, kt, c:c + w], start=(kt == 0), stop=(kt == TPB - 1))
            mm.then_inc(s.av, 1)

        def onorm_dve(dve, layer, b, g=0):
            s = att[layer]
            n, heads, w = (4, 4, 64) if layer == 2 else (1, NH, 16)
            h0 = heads * g
            dve.wait_ge(s.av, b * NH + h0 + heads + TS)
            if layer == 2:
                rs = rsum[:, b, :, h0:h0 + 4] if isinstance(b, int) else rsum[:, bass.ds(b, 1), :, h0:h0 + 4]
            else:
                rs = rsum[:, b, :, :] if isinstance(b, int) else rsum[:, bass.ds(b, 1), :, :]
            if not isinstance(b, int):
                rs = rs.rearrange("p a q h -> p (a q) h")
            dve.reciprocal(rrec[:, :, h0:h0 + heads], rs).then_inc(s.ch, 1)
            per = {0: 2, 1: 2, 2: 5, 3: 2}[layer]
            dve.wait_ge(s.ch, b * per + g + 1)
            if layer == 0:
                m = qm[:, bs(b, TPB)]
                dve.tensor_tensor(rrec[:, :, :], rrec[:, :, :], m.unsqueeze(2).broadcast_to([P, TPB, NH]),
                                  ALU.mult).then_inc(s.ch, 1)
                dve.wait_ge(s.ch, b * per + 2)
            dst = O2[:, :, 256 * g:256 * g + 256] if layer == 2 else Osb[:, :, :]
            if layer == 2:
                dve.wait_ge(s.ot, b + 1)
            for qt in range(TPB):
                ins = dve.tensor_tensor(dst[:, qt, :].rearrange("p (h w) -> p h w", w=w),
                                        psum[:, 4, qt * SEQ:(qt + 1) * SEQ].rearrange("p (h w) -> p h w", w=w),
                                        rrec[:, qt, h0:h0 + heads].unsqueeze(2).broadcast_to([P, heads, w]), ALU.mult)
            ins.then_inc(s.on, 1)

        def final_pe(pe, layer, b):
            s = att[layer]
            pe.wait_ge(s.on, b + 2)
            for c in range(DC):
                for qt in range(TPB):
                    mm = pe.transpose(psum[:, 7, c * SEQ + qt * P:c * SEQ + (qt + 1) * P],
                                      Osb[:, qt, c * P:(c + 1) * P], ident[:, :])
            mm.then_inc(s.ot, 1)

        def final2_pe(pe, layer, b):
            s = att[layer]
            pe.wait_ge(s.oe, b + 1)
            for qt in range(TPB):
                for c in range(DC):
                    mm = pe.matmul(psum[:, 7, qt * D:(qt + 1) * D], OTs[:, c, qt * P:(qt + 1) * P], Wsm[:, 3, c, :],
                                   start=(c == 0), stop=(c == DC - 1))
            mm.then_inc(s.wo, 1)

        def ocopy_act(act, layer, b):
            s = att[layer]
            act.wait_ge(s.ot, b + 1)
            act.activation(OTs[:, :, :], psum[:, 7, :].rearrange("p (c t) -> p c t", c=DC), ACT.Copy).then_inc(s.oe, 1)

        def xadd_dve(dve, layer, b):
            s = att[layer]
            xb = X[:, bs(b, TPB), :]
            if layer == 0:
                dve.wait_ge(s.on, b + 2)
                src = Osb
            else:
                dve.wait_ge(s.wo, b + 1)
                bo = bo_bc[:, {1: 0, 3: 2}[layer], :]
                dve.tensor_tensor(xtmp[:, :, :], psum[:, 7, :].rearrange("p (q d) -> p q d", q=TPB),
                                  bo.unsqueeze(1).broadcast_to([P, TPB, D]), ALU.add).then_inc(s.ch, 1)
                dve.wait_ge(s.ch, 2 * b + 2)
                src = xtmp
            dve.scalar_tensor_tensor(out=xb, in0=src[:, :, :], scalar=tg[:, layer:layer + 1], in1=xb, op0=ALU.mult,
                                     op1=ALU.add).then_inc(x_upd, 1)

        def att_body_pe(pe, layer, b, first):
            s = att[layer]
            if layer == 2:
                project2_pe(pe, b)
            else:
                pe.wait_ge(s.prep, b + 1)
            for k in range(NH + AV_LAG):
                if k < NH:
                    scores_pe(pe, layer, b, k)
                if k >= T_LAG and k - T_LAG < NH:
                    ptrans_pe(pe, layer, b, k - T_LAG)
                if k >= AV_LAG:
                    pv_pe(pe, layer, b, k - AV_LAG)
                if not first and layer != 0:
                    if layer == 2:
                        if k == 1:
                            otrans2_pe(pe, b, 6)
                        if k == 3:
                            wo2_pe(pe, b, 6)
                    else:
                        if k == 1:
                            final_pe(pe, layer, b - 1)
                        if k == 3:
                            final2_pe(pe, layer, b - 1)

        def att_pe(pe, layer):
            att_body_pe(pe, layer, 0, True)
            with pe.Fori(1, BATCH) as b:
                att_body_pe(pe, layer, b, False)
            if layer == 2:
                otrans2_pe(pe, BATCH, 0)
                wo2_pe(pe, BATCH, 0)
            elif layer:
                final_pe(pe, layer, BATCH - 1)
                final2_pe(pe, layer, BATCH - 1)

        def att_body_dve(dve, layer, b, first):
            if layer == 2:
                project2_dve(dve, b)
            else:
                prepare_dve(dve, layer, b)
            for k in range(NH + AV_LAG):
                if k < NH:
                    max_dve(dve, layer, b, k)
                if k >= T_LAG and k - T_LAG < NH:
                    pcopy_dve(dve, layer, b, k - T_LAG)
                if not first and layer != 0:
                    if layer == 2 and k == 1:
                        ocopy2_dve(dve, b, 6)
                    if k == FIN_AT - 1:
                        if layer == 2:
                            y2_dve(dve, b, 6)
                        else:
                            xadd_dve(dve, layer, b - 1)
                if layer == 2 and k >= AV_LAG + 4 and (k - AV_LAG) % 4 == 0:
                    onorm_dve(dve, layer, b, (k - AV_LAG) // 4 - 1)
            onorm_dve(dve, layer, b, 3 if layer == 2 else 0)
            if layer == 0:
                xadd_dve(dve, 0, b)

        def att_dve(dve, layer):
            att_body_dve(dve, layer, 0, True)
            with dve.Fori(1, BATCH) as b:
                att_body_dve(dve, layer, b, False)
            if layer == 2:
                ocopy2_dve(dve, BATCH, 0)
                y2_dve(dve, BATCH, 0)
            elif layer:
                xadd_dve(dve, layer, BATCH - 1)

        def att_body_act(act, layer, b, first):
            if layer == 2:
                project2_act(act, b)
            for k in range(NH):
                exp_act(act, layer, b, k)
                if k == 1 and not first and layer != 0:
                    if layer == 2:
                        ocopy2_act(act, b, 6)
                    else:
                        ocopy_act(act, layer, b - 1)

        def att_act(act, layer):
            att_body_act(act, layer, 0, True)
            with act.Fori(1, BATCH) as b:
                att_body_act(act, layer, b, False)
            if layer == 2:
                ocopy2_act(act, BATCH, 0)
            elif layer:
                ocopy_act(act, layer, BATCH - 1)

        def att_pool(pool, layer):
            prepare_pool(pool, layer, 0)
            with pool.Fori(1, BATCH) as b:
                prepare_pool(pool, layer, b)

        def proj_steps(layer):
            st = [("q", m, n) for m in range(DC) for n in range(NCH)]
            st += [("k", m, n) for m in range(DC) for n in range(NCH)]
            return st + [("v", t, 0) for t in range(TT // 2)]

        N_PJ = len(proj_steps(1)) // 2

        def proj_pe(pe, layer):
            pe.wait_ge(ld_att[layer], 16 * {1: 5, 3: 4}[layer])
            pe.wait_ge(tpe_done[0], 4 * tn(layer, False) + 4)
            pe.wait_ge(tpe_done[1], 4 * tn(layer, False) + 4)
            base = 0 if layer == 1 else N_PJ
            for i, (kind, m, n) in enumerate(proj_steps(layer)):
                bk = i % 2
                if base + i // 2:
                    pe.wait_ge(pj_ev[bk], base + i // 2)
                bank = psum[:, 2 + bk, :]
                if kind == "v":
                    for j in range(2):
                        t = 2 * m + j
                        for c in range(DC):
                            mm = pe.matmul(bank[:, j * D:(j + 1) * D], CT[:, c, t * P:(t + 1) * P], Wsm[:, 2, c, :],
                                           start=(c == 0), stop=(c == DC - 1))
                else:
                    src = HT if kind == "q" else CT
                    for c in range(DC):
                        mm = pe.matmul(bank, Wsm[:, 0 if kind == "q" else 1, c, m * P:(m + 1) * P],
                                       src[:, c, n * CH:(n + 1) * CH], start=(c == 0), stop=(c == DC - 1))
                mm.then_inc(pj_mm[bk], 1)

        def proj_copy(layer, dve=None, act=None):
            base = 0 if layer == 1 else N_PJ
            for i, (kind, m, n) in enumerate(proj_steps(layer)):
                bk = i % 2
                eng = dve if bk == 0 or kind == "v" else act
                if eng is None:
                    continue
                eng.wait_ge(pj_mm[bk], base + i // 2 + 1)
                bank = psum[:, 2 + bk, :]
                if kind == "v":
                    dst, src = Va[:, 2 * m:2 * m + 2, :], bank.rearrange("p (t d) -> p t d", t=2)
                    if layer == 1:
                        ins = dve.tensor_tensor(dst, src, bv1.unsqueeze(1).broadcast_to([P, 2, D]), ALU.add)
                    else:
                        ins = dve.tensor_copy(dst, src)
                else:
                    dst, src = (QTa if kind == "q" else KTa)[:, m, n * CH:(n + 1) * CH], bank
                    if eng is act and kind == "q" and layer == 3:
                        ins = act.activation(dst, src, ACT.Identity, bias=bq3[:, m:m + 1])
                    elif eng is act:
                        ins = act.activation(dst, src, ACT.Copy)
                    elif kind == "q" and layer == 3:
                        ins = dve.tensor_scalar(dst, src, bq3[:, m:m + 1], None, ALU.add)
                    else:
                        ins = dve.tensor_copy(dst, src)
                ins.then_inc(pj_ev[bk], 1)

        l2_sq, l2_mm, l2_sd, l2_mx, l2_rc, l2_sc = (sem(n) for n in ("l2_sq", "l2_sum", "l2_sqrt", "l2_max", "l2_rec", "l2_scaled"))
        sm_x = sem("scale_mul")

        def l2_steps():
            return [(k, m, n) for k in range(2) for m in range(DC) for n in range(NCH)]

        def l2norm_pool(pool):
            pool.wait_ge(pj_ev[0], 2 * N_PJ)
            pool.wait_ge(pj_ev[1], 2 * N_PJ)
            for i, (k, m, n) in enumerate(l2_steps()):
                x = (QTa, KTa)[k][:, m, n * CH:(n + 1) * CH]
                if i >= 4:
                    pool.wait_ge(l2_mm, i - 3)
                pool.tensor_tensor(ACCf(i % 4), x, x, ALU.mult).then_inc(l2_sq, 1)

        def ACCf(i):
            return ACC[:, 2 * i:2 * i + 2, :].rearrange("p t d -> p (t d)")

        def l2norm_pe(pe):
            for i in range(16):
                pe.wait_ge(l2_sq, i + 1)
                if i >= 4:
                    pe.wait_ge(l2_mx, i - 3)
                pe.matmul(psum[:, 4 + i % 4, :], headsum[:, :], ACCf(i % 4), start=True, stop=True).then_inc(l2_mm, 1)

        def l2norm_act(act):
            for i in range(16):
                act.wait_ge(l2_mx, i + 1)
                act.activation(ACCf(4 + i % 4), ACCf(4 + i % 4), ACT.Sqrt).then_inc(l2_sd, 1)

        def l2norm_dve(dve):
            def floor(i):
                dve.wait_ge(l2_mm, i + 1)
                if i >= 4:
                    dve.wait_ge(l2_sc, i - 3)
                dve.tensor_scalar(ACCf(4 + i % 4), psum[:, 4 + i % 4, :], NORM_EPS2, None, ALU.max).then_inc(l2_mx, 1)

            def scale(i):
                k, m, n = l2_steps()[i]
                x = (QTa, KTa)[k][:, m, n * CH:(n + 1) * CH]
                dve.wait_ge(l2_sd, i + 1)
                dve.reciprocal(ACCf(4 + i % 4), ACCf(4 + i % 4)).then_inc(l2_rc, 1)
                dve.wait_ge(l2_rc, i + 1)
                if k == 0:
                    dve.scalar_tensor_tensor(out=x, in0=x, scalar=smul[:, m:m + 1], in1=ACCf(4 + i % 4),
                                             op0=ALU.mult, op1=ALU.mult).then_inc(l2_sc, 1)
                else:
                    dve.tensor_tensor(x, x, ACCf(4 + i % 4), ALU.mult).then_inc(l2_sc, 1)
            dve.wait_ge(sm_x, 2)
            for i in range(16 + 2):
                if i < 16:
                    floor(i)
                if i >= 2:
                    scale(i - 2)
            dve.wait_ge(l2_sc, 16)

        def base2(b, bk):
            if isinstance(b, int) and b == 0:
                return 0
            return b * 9 - 3 if bk == 0 else b * 8 - 2

        def empty2(pe, b, bk, i):
            pe.wait_ge(me[bk], base2(b, bk) + i + 1)

        def full2(eng, b, bk, i):
            eng.wait_ge(mf[bk], base2(b, bk) + i + 1)

        def stage2_pool(pool, b):
            s = att[2]
            pool.wait_ge(s.s, b * NH + 1)
            pool.tensor_copy(CTb[:, :, :], CT[:, :, bs(b)]).then_inc(s.vcopy, 1)

        def att2_pool(pool):
            pool.wait_ge(x_upd, x_after(1, True))
            stage2_pool(pool, 0)
            with pool.Fori(1, BATCH) as b:
                stage2_pool(pool, b)

        def project2_pe(pe, b):
            s = att[2]
            for w, src in ((0, HT), (1, CT)):
                for j in range(4):
                    bk = j % 2
                    empty2(pe, b, bk, 2 * w + j // 2)
                    for n in range(2):
                        m = 2 * j + n
                        for c in range(DC):
                            mm = pe.matmul(psum[:, 6 + bk, n * SEQ:(n + 1) * SEQ], Wqkv[:, w, c, m * P:(m + 1) * P],
                                           src[:, c, bs(b)], start=(c == 0), stop=(c == DC - 1))
                    mm.then_inc(mf[bk], 1)
            pe.wait_ge(s.vcopy, b + 1)
            for t in range(TPB):
                for bk in range(2):
                    empty2(pe, b, bk, 4 + t)
                    for c in range(DC):
                        mm = pe.matmul(psum[:, 6 + bk, :], CTb[:, c, t * P:(t + 1) * P],
                                       Wqkv[:, 2, c, bk * 512:(bk + 1) * 512], start=(c == 0), stop=(c == DC - 1))
                    mm.then_inc(mf[bk], 1)
            for bk in range(2):
                empty2(pe, b, bk, 6)

        def project2_dve(dve, b):
            s = att[2]
            dve.wait_ge(s.s, b * NH + 1)
            for w in range(2):
                for j in (0, 2):
                    full2(dve, b, 0, 2 * w + j // 2)
                    for n in range(2):
                        m = 2 * j + n
                        src = psum[:, 6, n * SEQ:(n + 1) * SEQ]
                        if w == 0:
                            ins = dve.tensor_scalar(Q2[:, m, :], src, bqk[:, 0, m:m + 1], 0.125, ALU.add, ALU.mult)
                        else:
                            ins = dve.tensor_scalar(K2[:, m, :], src, bqk[:, 1, m:m + 1], None, ALU.add)
                    ins.then_inc(me[0], 1)
            dve.wait_ge(s.av, b * NH + TS)
            for t in range(TPB):
                for bk in range(2):
                    full2(dve, b, bk, 4 + t)
                    half = slice(bk * 512, (bk + 1) * 512)
                    dve.tensor_tensor(V2[:, t, half], psum[:, 6 + bk, :], bv2[:, half], ALU.add).then_inc(me[bk], 1)

        def project2_act(act, b):
            s = att[2]
            act.wait_ge(s.s, b * NH + 1)
            for w in range(2):
                for j in (1, 3):
                    full2(act, b, 1, 2 * w + j // 2)
                    for n in range(2):
                        m = 2 * j + n
                        src = psum[:, 7, n * SEQ:(n + 1) * SEQ]
                        if w == 0:
                            ins = act.activation(Q2[:, m, :], src, ACT.Identity, bias=bq8[:, m:m + 1], scale=0.125)
                        else:
                            ins = act.activation(K2[:, m, :], src, ACT.Identity, bias=bqk[:, 1, m:m + 1])
                    ins.then_inc(me[1], 1)

        def otrans2_pe(pe, nb, i0):
            s = att[2]
            pe.wait_ge(s.on, nb * 4 + 1)
            for j in range(4):
                bk = j % 2
                empty2(pe, nb, bk, i0 + j // 2)
                for n in range(2):
                    m = 2 * j + n
                    for qt in range(TPB):
                        mm = pe.transpose(psum[:, 6 + bk, n * SEQ + qt * P:n * SEQ + (qt + 1) * P],
                                          O2[:, qt, m * P:(m + 1) * P], ident[:, :])
                mm.then_inc(mf[bk], 1)
            pe.drain().then_inc(s.ot, 1)

        def wo2_pe(pe, nb, i0):
            empty2(pe, nb, 0, i0 + 2)
            empty2(pe, nb, 1, i0 + 2)
            for qt in range(TPB):
                for m in range(8):
                    mm = pe.matmul(psum[:, 6, qt * D:(qt + 1) * D], OT2[:, m, qt * P:(qt + 1) * P], Wo2[:, m, :],
                                   start=(m == 0), stop=(m == 7))
            mm.then_inc(mf[0], 1)

        def ocopy2(nb, i0, bk, copy):
            for j in (bk, bk + 2):
                copy(OT2[:, 2 * j:2 * j + 2, :], psum[:, 6 + bk, :].rearrange("p (m t) -> p m t", m=2), j)

        def ocopy2_dve(dve, nb, i0):
            for j in (0, 2):
                full2(dve, nb, 0, i0 + j // 2)
                dve.tensor_copy(OT2[:, 2 * j:2 * j + 2, :],
                                psum[:, 6, :].rearrange("p (m t) -> p m t", m=2)).then_inc(me[0], 1)

        def ocopy2_act(act, nb, i0):
            for j in (1, 3):
                full2(act, nb, 1, i0 + j // 2)
                act.activation(OT2[:, 2 * j:2 * j + 2, :],
                               psum[:, 7, :].rearrange("p (m t) -> p m t", m=2), ACT.Copy).then_inc(me[1], 1)

        def y2_dve(dve, nb, i0):
            s = att[2]
            full2(dve, nb, 0, i0 + 2)
            dve.tensor_tensor(xtmp[:, :, :], psum[:, 6, :].rearrange("p (q d) -> p q d", q=TPB),
                              bo_bc[:, 1, :].unsqueeze(1).broadcast_to([P, TPB, D]), ALU.add).then_inc(me[0], 1)
            dve.wait_ge(me[0], base2(nb, 0) + i0 + 4)
            dve.tensor_tensor(ACC[:, bs(nb - 1, TPB), :], xtmp[:, :, :], Hn[:, bs(nb - 1, TPB), :],
                              ALU.add).then_inc(s.ch, 1)

        def logits_pe(pe, layer, n):
            f = ffn[layer]
            pe.wait_ge(tpe_done[0], 4 * tn(layer, True) + 4)
            pe.wait_ge(tpe_done[1], 4 * tn(layer, True) + 4)
            for t in range(TT):
                for c in range(DC):
                    mm = pe.matmul(psum[:, 4, t * WE:t * WE + n], HT[:, c, t * P:(t + 1) * P], wr[:, layer - 1, c, 0:n],
                                   start=(c == 0), stop=(c == DC - 1))
            mm.then_inc(f.lg, 1)

        steps = [0]

        def routing_dve(dve, layer, n, shared):
            f = ffn[layer]

            def link(ins):
                steps[0] += 1
                ins.then_inc(chain, 1)
                dve.wait_ge(chain, steps[0])

            def row(x):
                return x.unsqueeze(2).broadcast_to([P, TT, n])

            z = lg[:, :, 0:n]
            t0, t1, pr, msk = (rt[:, i, :, 0:n] for i in range(4))
            o1, o2, rv = oh1[:, :, 0:n], oh2[:, :, 0:n], rev[:, :, 0:n]
            dve.wait_ge(f.lg, 1)
            ps = psum[:, 4, 0:TT * WE].rearrange("p (t e) -> p t e", e=WE)[:, :, 0:n]
            if layer == 1:
                link(dve.tensor_tensor(z, ps, rbias[:, 0, 0:n].unsqueeze(1).broadcast_to([P, TT, n]), ALU.mult))
                dve.sem_inc(rt_in, 1)
                dve.wait_ge(rt_out, 1)
                val = pr
            elif layer == 2:
                link(dve.tensor_tensor(z, ps, rbias[:, 1, 0:n].unsqueeze(1).broadcast_to([P, TT, n]), ALU.add))
                link(dve.tensor_reduce(r1[:, 0, :], z, AX.X, ALU.max))
                link(dve.tensor_tensor(z, z, row(r1[:, 0, :]), ALU.subtract))
                dve.sem_inc(rt_in, 1)
                dve.wait_ge(rt_out, 2)
                link(dve.tensor_reduce(r1[:, 0, :], pr, AX.X, ALU.add))
                link(dve.reciprocal(r1[:, 1, :], r1[:, 0, :]))
                link(dve.tensor_tensor(pr, pr, row(r1[:, 1, :]), ALU.mult))
                val = pr
            else:
                link(dve.tensor_copy(z, ps))
                val = z

            def pick(values, best, onehot):
                link(dve.tensor_reduce(best, values, AX.X, ALU.max))
                link(dve.tensor_tensor(t0, values, row(best), ALU.is_equal))
                link(dve.tensor_tensor(t0, t0, rv, ALU.mult))
                link(dve.tensor_reduce(r1[:, 3, :], t0, AX.X, ALU.max))
                link(dve.tensor_tensor(onehot, t0, row(r1[:, 3, :]), ALU.is_equal))

            pick(val, r1[:, 0, :], o1)
            link(dve.scalar_tensor_tensor(out=t1, in0=o1, scalar=-BIG, in1=val, op0=ALU.mult, op1=ALU.add))
            pick(t1, r1[:, 1, :], o2)
            link(dve.tensor_tensor(msk, o1, o2, ALU.add))
            if layer == 1:
                link(dve.tensor_tensor(r1[:, 2, :], r1[:, 0, :], r1[:, 1, :], ALU.add))
                link(dve.reciprocal(r1[:, 3, :], r1[:, 2, :]))
                link(dve.tensor_tensor(t0, pr, msk, ALU.mult))
                link(dve.tensor_tensor(t0, t0, row(r1[:, 3, :]), ALU.mult))
            elif layer == 2:
                link(dve.tensor_tensor(t0, pr, msk, ALU.mult))
            else:
                link(dve.tensor_tensor(r1[:, 2, :], r1[:, 1, :], r1[:, 0, :], ALU.subtract))
                dve.sem_inc(rt_in, 1)
                dve.wait_ge(rt_out, 3)
                link(dve.tensor_scalar(r1[:, 2, :], r1[:, 1, :], 1.0, None, ALU.add))
                link(dve.reciprocal(r1[:, 0, :], r1[:, 2, :]))
                link(dve.tensor_tensor(r1[:, 1, :], r1[:, 1, :], r1[:, 0, :], ALU.mult))
                link(dve.tensor_tensor(t0, o1, row(r1[:, 0, :]), ALU.mult))
                link(dve.tensor_tensor(t1, o2, row(r1[:, 1, :]), ALU.mult))
                link(dve.tensor_tensor(t0, t0, t1, ALU.add))
                dve.sem_inc(pfx, 1)
                dve.wait_ge(pfx, 2)
                link(dve.tensor_scalar(t1, psum[:, 5, 0:TT * WE].rearrange("p (t e) -> p t e", e=WE),
                                       CAP + 0.5, None, ALU.is_le))
                link(dve.tensor_tensor(t0, t0, t1, ALU.mult))
            for e in range(shared):
                link(dve.memset(wts[:, e, :], 1.0 / shared))
            link(dve.tensor_copy(wts[:, shared:shared + n, :].rearrange("p e t -> p t e"), t0))

        def routing_act(act, layer):
            if layer == 1:
                act.wait_ge(rt_in, 1)
                act.activation(rt[:, 2, :, 0:7], lg[:, :, 0:7], ACT.Sigmoid).then_inc(rt_out, 1)
            elif layer == 2:
                act.wait_ge(rt_in, 2)
                act.activation(rt[:, 2, :, 0:4], lg[:, :, 0:4], ACT.Exp).then_inc(rt_out, 1)
            else:
                act.wait_ge(rt_in, 3)
                act.activation(r1[:, 1, :], r1[:, 2, :], ACT.Exp).then_inc(rt_out, 1)

        def ranks_pe(pe):
            pe.wait_ge(pfx, 1)
            pe.matmul(psum[:, 5, 0:TT * WE], tril[:, :], rt[:, 3, :, :].rearrange("p t e -> p (t e)"),
                      start=True, stop=False, skip_group_check=True)
            for t in range(TT - 1):
                mm = pe.matmul(psum[:, 5, (t + 1) * WE:TT * WE], ones[:, :],
                               rt[:, 3, t, :].unsqueeze(1).broadcast_to([P, TT - 1 - t, WE]),
                               start=False, stop=(t == TT - 2), skip_group_check=True)
            mm.then_inc(pfx, 1)

        def ffn_shape(layer):
            return {1: (E1, F1, F1_LAST, True), 2: (E2, F2, P, False), 3: (E3, F3, P, True)}[layer]

        def wviews(layer, s):
            w = wslot[s]
            if layer == 1:
                g = w[:, 0:1408].rearrange("p (c n) -> p c n", c=DC)
                u = w[:, 1408:2816].rearrange("p (c n) -> p c n", c=DC)
                return g, u, w[:, 2816:4352].rearrange("p (f n) -> p f n", f=F1)
            if layer == 2:
                return (w[:, 0:2048].rearrange("p (c n) -> p c n", c=DC), None,
                        w[:, 2048:4096].rearrange("p (f n) -> p f n", f=F2))
            w1 = w[:, 0:2048].rearrange("p (c n) -> p c n", c=DC)
            return w1[:, :, 0:512], w1[:, :, 512:1024], w[:, 2048:3072].rearrange("p (f n) -> p f n", f=F3)

        LOADS = {1: 4, 2: 4, 3: 2}

        def load_expert(sp, layer, i, s):
            f = ffn[layer]
            e = 2 * i + s
            g, u, d = wviews(layer, s)

            def ex(name):
                return a[name][e] if isinstance(e, int) else a[name][bass.ds(e, 1)].squeeze(0)
            if layer == 1:
                sp.dma_start(g, ex("f1g").rearrange("(c p) n -> p c n", p=P)).then_inc(f.w[s], 16)
                sp.dma_start(u, ex("f1u").rearrange("(c p) n -> p c n", p=P)).then_inc(f.w[s], 16)
                sp.dma_start(d[:, 0:F1 - 1, :], ex("f1d")[0:(F1 - 1) * P, :].rearrange("(f p) n -> p f n", p=P)
                             ).then_inc(f.w[s], 16)
                sp.dma_start(d[0:F1_LAST, F1 - 1, :], ex("f1d")[(F1 - 1) * P:, :]).then_inc(f.w[s], 16)
            elif layer == 2:
                sp.dma_start(g, ex("f2w1").rearrange("(c p) n -> p c n", p=P)).then_inc(f.w[s], 16)
                sp.dma_start(d, ex("f2w2").rearrange("(f p) n -> p f n", p=P)).then_inc(f.w[s], 16)
                sp.dma_start(b1c[:, s, :], ex("f2b1")).then_inc(f.w[s], 16)
                sp.dma_start(b2bc[:, s, :], ex("f2b2").partition_broadcast(P)).then_inc(f.w[s], 16)
            else:
                sp.dma_start(wslot[s][:, 0:2048].rearrange("p (c n) -> p c n", c=DC),
                             ex("f3w1").rearrange("(c p) n -> p c n", p=P)).then_inc(f.w[s], 16)
                sp.dma_start(d, ex("f3w2").rearrange("(f p) n -> p f n", p=P)).then_inc(f.w[s], 16)

        def ffn_loads(sp, layer):
            f = ffn[layer]
            n_e = ffn_shape(layer)[0]
            sp.wait_ge(x_upd, x_after(layer, False))
            for s in range(2):
                load_expert(sp, layer, 0, s)
            with sp.Fori(1, n_e // 2) as i:
                for s in range(2):
                    sp.wait_ge(f.acc, i * 32 + (16 * (s - 1) + 4))
                    load_expert(sp, layer, i, s)

        def ffn_pe(pe, layer):
            f = ffn[layer]
            n_e, nf, last_w, gated = ffn_shape(layer)
            with pe.Fori(0, n_e // 2) as i:
                for s in range(2):
                    g, u, d = wviews(layer, s)
                    pe.wait_ge(f.w[s], (i + 1) * (16 * LOADS[layer]))
                    for c in range(NCH):
                        ch = i * 8 + (s * 4 + c)
                        for k in range(nf):
                            w = last_w if k == nf - 1 else P
                            bank = (s * 4 * nf + c * nf + k) % 2
                            pe.wait_ge(f.hid, i * (8 * nf) + ((s * 4 + c) * nf + k + 1))
                            for wv, base in ((g, 0), (u, 2)):
                                if wv is None:
                                    continue
                                for kc in range(DC):
                                    mm = pe.matmul(psum[0:w, base + bank, :], wv[:, kc, k * P:k * P + w],
                                                   HT[:, kc, c * CH:(c + 1) * CH], start=(kc == 0), stop=(kc == DC - 1))
                            mm.then_inc(f.up, 1)
                        for tt in range(TPC):
                            pe.wait_ge(f.acc, ch * 4 + (tt + 1))
                            for k in range(nf):
                                if tt == 0:
                                    pe.wait_ge(f.hid, i * (8 * nf) + ((s * 4 + c) * nf + k + 3))
                                w = last_w if k == nf - 1 else P
                                mm = pe.matmul(psum[:, 4 + tt, 0:D],
                                               hid[0:w, c % 2, k, tt * P:(tt + 1) * P], d[0:w, k, :],
                                               start=(k == 0), stop=(k == nf - 1))
                            mm.then_inc(f.down, 1)

        def ffn_act(act, layer):
            f = ffn[layer]
            n_e, nf, last_w, gated = ffn_shape(layer)
            with act.Fori(0, n_e // 2) as i:
                for s in range(2):
                    if layer == 2:
                        act.wait_ge(f.w[s], (i + 1) * (16 * LOADS[layer]))
                    for c in range(NCH):
                        if layer == 2:
                            act.wait_ge(f.down, i * 32 + 4 * (s * 4 + c) + 4)
                        for k in range(nf):
                            w = last_w if k == nf - 1 else P
                            n = (s * 4 + c) * nf + k
                            act.wait_ge(f.up, i * (8 * nf) + (n + 1))
                            if layer == 2:
                                act.activation(hid[:, c % 2, k, :], psum[:, n % 2, :], ACT.Relu,
                                               bias=b1c[:, s, k:k + 1]).then_inc(f.hid, 1)
                            else:
                                act.wait_ge(f.hid, i * (8 * nf) + (n + 1))
                                act.activation(sg[0:w, n % 2, :], psum[0:w, n % 2, :],
                                               ACT.Silu if layer == 1 else ACT.Gelu).then_inc(f.act, 1)

        def ffn_dve(dve, layer):
            f = ffn[layer]
            n_e, nf, last_w, gated = ffn_shape(layer)
            dve.wait_ge(f.init, 1)
            with dve.Fori(0, n_e // 2) as i:
                for s in range(2):
                    if layer == 2:
                        dve.wait_ge(f.w[s], (i + 1) * (16 * LOADS[layer]))
                    for c in range(NCH):
                        if gated:
                            dve.wait_ge(f.down, i * 32 + 4 * (s * 4 + c) + 4)
                            for k in range(nf):
                                w = last_w if k == nf - 1 else P
                                n = (s * 4 + c) * nf + k
                                dve.wait_ge(f.act, i * (8 * nf) + (n + 1))
                                dve.tensor_tensor(hid[0:w, c % 2, k, :], sg[0:w, n % 2, :], psum[0:w, 2 + n % 2, :],
                                                  ALU.mult).then_inc(f.hid, 1)
                        for tt in range(TPC):
                            t = c * TPC + tt
                            dve.wait_ge(f.down, i * 32 + (4 * (s * 4 + c) + tt + 9))
                            y = psum[:, 4 + tt, 0:D]
                            if layer == 2:
                                dve.tensor_tensor(dtmp[:, tt % 2, :], y, b2bc[:, s, :], ALU.add).then_inc(f.tmp, 1)
                                dve.wait_ge(f.tmp, i * 32 + (4 * (s * 4 + c) + tt + 1))
                                y = dtmp[:, tt % 2, :]
                            dve.scalar_tensor_tensor(out=ACC[:, t, :], in0=y, scalar=wts_at(i, s, t), in1=ACC[:, t, :],
                                                     op0=ALU.mult, op1=ALU.add).then_inc(f.acc, 1)
            dve.wait_ge(f.acc, 16 * n_e + 4)

        def wts_at(i, s, t):
            return wts[:, bass.ds(i * 2 + s, 1), t]

        def xadd_all(dve, n, src, gate, per):
            for g in range(n):
                t = slice(g * per, (g + 1) * per)
                dve.scalar_tensor_tensor(out=X[:, t, :], in0=src[:, t, :], scalar=tg[:, gate:gate + 1], in1=X[:, t, :],
                                         op0=ALU.mult, op1=ALU.add).then_inc(x_upd, 1)

        def affine_dve(dve, src, g, b):
            for i, (vec, op) in enumerate(((g, ALU.mult), (b, ALU.add))):
                for q in range(4):
                    t = slice(4 * q, 4 * q + 4)
                    ins = dve.tensor_tensor(src[:, t, :], src[:, t, :], vec.unsqueeze(1).broadcast_to([P, 4, D]), op)
                steps[0] += 1
                ins.then_inc(chain, 1)
                dve.wait_ge(chain, steps[0])

        def tn(layer, ff):
            return {(0, False): 1, (1, False): 2, (1, True): 3, (2, False): 4, (2, True): 5, (3, False): 6, (3, True): 7}[
                (layer, ff)]
        ST = {(0, False): 0, (0, True): 1, (1, False): 3, (1, True): 4, (2, False): 5, (2, True): 7, (3, False): 8,
              (3, True): 9}

        rt_in, rt_out = sem("rt_in"), sem("rt_out")
        SUB = [(l, ff) for l in range(4) for ff in (False, True)][:stop_after]
        N_SMALL = 18
        N_CONST = 24

        @block.sync
        def _(sp):
            xv = a["x"].rearrange("(t p) d -> p t d", p=P)
            sp.dma_start(Va[:, :, :], a["ctx"].rearrange("(t p) d -> p t d", p=P)).then_inc(ld_ctx, 16)
            sp.dma_start(X[:, :, :], xv).then_inc(ld_x, 16)
            small = [(mask8[:, 0:TOK], a["mask"].partition_broadcast(P)), (qm8[:, :], a["maskT"]),
                     (graw[:, :], a["gates"].partition_broadcast(P)),
                     (fside[:, :, :], a["fside"].rearrange("(t p) k -> p t k", p=P)),
                     (lng, a["ln_g0"].partition_broadcast(P)), (lnb, a["ln_b0"].partition_broadcast(P)),
                     (bo_bc[:, 0, :], a["bo1"].partition_broadcast(P)), (bo_bc[:, 1, :], a["bo2"].partition_broadcast(P)),
                     (bo_bc[:, 2, :], a["bo3"].partition_broadcast(P)),
                     (rbias[:, 0, 0:7], a["rbias"].partition_broadcast(P)),
                     (rbias[:, 1, 0:4], a["gate_b"].partition_broadcast(P)),
                     (wr[:, 0, :, 0:7], a["wr1"].rearrange("(c p) e -> p c e", p=P)),
                     (wr[:, 1, :, 0:4], a["wr2"].rearrange("(c p) e -> p c e", p=P)),
                     (wr[:, 2, :, 0:8], a["wr3"].rearrange("(c p) e -> p c e", p=P)),
                     (bqk[:, 0, :], a["bq2"]), (bqk[:, 1, :], a["bk2"]), (bq3[:, :], a["bq3"]), (smul[:, :], a["smul"])]
            assert len(small) == N_SMALL
            for dst, src in small:
                sp.dma_start(dst, src).then_inc(ld_small, 16)

            for layer, ff in SUB:
                if ff and layer:
                    ffn_loads(sp, layer)
                elif layer in (1, 3) and not ff:
                    if layer == 3:
                        sp.wait_ge(x_upd, x_after(2, True))
                    for w in range(4):
                        sp.dma_start(Wsm[:, w, :, :], a[f"w{layer}"][w].rearrange("(c p) n -> p c n", p=P)
                                     ).then_inc(ld_att[layer], 16)
                    if layer == 1:
                        sp.dma_start(bv1, a["bv1"].partition_broadcast(P)).then_inc(ld_att[1], 16)
                elif layer == 2 and not ff:
                    sp.wait_ge(x_upd, x_after(1, True))
                    for w in range(3):
                        sp.dma_start(Wqkv[:, w, :, :], a["w2"][w].rearrange("(c p) n -> p c n", p=P)
                                     ).then_inc(ld_att[2], 16)
                    sp.dma_start(Wo2[:, :, :], a["wo2"].rearrange("(c p) n -> p c n", p=P)).then_inc(ld_att[2], 16)
                    for dst, name in ((bv2, "bv2"), (lng2, "ln_g2"), (lnb2, "ln_b2")):
                        sp.dma_start(dst, a[name].partition_broadcast(P)).then_inc(ld_att[2], 16)
            sp.wait_ge(x_upd, x_after(*SUB[-1]))
            sp.dma_start(out.rearrange("(t p) d -> p t d", p=P), X[:, :, :]).then_inc(out_done, 16)
            sp.wait_ge(out_done, 16)

        @block.gpsimd
        def _(pool):
            n = [0]

            def step(ins, wait=True):
                n[0] += 1
                ins.then_inc(consts, 1)
                if wait:
                    pool.wait_ge(consts, n[0])
            pool.memset(ident[:, :], 0.0).then_inc(consts, 1)
            pool.memset(ones[:, :], 1.0).then_inc(consts, 1)
            pool.memset(tril[:, :], 1.0).then_inc(consts, 1)
            pool.memset(headsum[:, :], 1.0).then_inc(consts, 1)
            pool.memset(causal0[:, :, :], -NEG_BIAS).then_inc(consts, 1)
            pool.memset(causal1[:, :, :], 0.0).then_inc(consts, 1)
            n[0] = 6
            for e in range(WE):
                step(pool.memset(rev[:, :, e], float(WE - e)), wait=False)
            step(pool.memset(eps[:, :], EPS))
            step(pool.affine_select(out=ident[:, :], in_=ident[:, :], compare_op=ALU.not_equal, fill=1.0, base=0,
                                    pattern=[[-1, P]], channel_multiplier=1))
            step(pool.affine_select(out=tril[:, :], in_=tril[:, :], compare_op=ALU.is_ge, fill=0.0, base=0,
                                    pattern=[[1, P]], channel_multiplier=-1))
            hs = headsum[:, :].rearrange("p (b w) -> p b w", w=16)
            step(pool.affine_select(out=hs, in_=hs, compare_op=ALU.is_ge, fill=0.0, base=0,
                                    pattern=[[-16, 8], [0, 16]], channel_multiplier=1))
            step(pool.affine_select(out=hs, in_=hs, compare_op=ALU.is_ge, fill=0.0, base=15,
                                    pattern=[[16, 8], [0, 16]], channel_multiplier=-1))
            for qt in range(TPB):
                step(pool.affine_select(out=causal0[:, qt, :], in_=causal0[:, qt, :], compare_op=ALU.is_ge, fill=0.0,
                                        base=P * qt, pattern=[[-1, SEQ]], channel_multiplier=1))
                step(pool.affine_select(out=causal1[:, qt, :], in_=causal1[:, qt, :], compare_op=ALU.is_ge,
                                        fill=MASKED, base=P * qt - 1, pattern=[[-1, SEQ]], channel_multiplier=1))
            step(pool.memset(causal1[0:1, 0, 0:1], 0.0))
            assert n[0] == N_CONST

            for layer, ff in SUB:
                if not ff:
                    if layer == 0:
                        pool.wait_ge(ld_ctx, 16)
                        att_pool(pool, 0)
                    elif layer == 2:
                        att2_pool(pool)
                    else:
                        if layer == 3:
                            l2norm_pool(pool)
                        for bk in range(2):
                            pool.wait_ge(pj_ev[bk], N_PJ * (1 if layer == 1 else 2))
                        att_pool(pool, layer)
                elif layer:
                    pool.wait_ge(x_upd, x_after(layer, False))
                    pool.memset(ACC[:, :, :], 0.0).then_inc(ffn[layer].init, 1)

        @block.tensor
        def _(pe):
            pe.wait_ge(consts, N_CONST)
            for n in range(4):
                pe.sem_inc(att[n].s, 1)
                pe.sem_inc(att[n].t, SS)
                pe.sem_inc(att[n].av, TS)
            pe.sem_inc(att[2].ot, 1)
            for n in range(1, 4):
                pe.sem_inc(ffn[n].down, 8)
            pe.wait_ge(ld_ctx, 16)
            transposes_pe(pe, 0, Va, lambda g: None)
            for layer, ff in SUB:
                if (layer, ff) != (0, True):
                    m = ST[(layer, ff)]
                    transposes_pe(pe, tn(layer, ff), Hn, lambda g: pe.wait_ge(h_done, TT * m + 4 * g + 4))
                if not ff:
                    if layer in (1, 3):
                        proj_pe(pe, layer)
                    if layer == 3:
                        l2norm_pe(pe)
                    if layer == 2:
                        pe.wait_ge(ld_att[2], 16 * 7)
                        for c in range(DC):
                            pe.wait_ge(tpe_done[c], 4 * tn(2, False) + 4)
                    att_pe(pe, layer)
                elif layer:
                    logits_pe(pe, layer, {1: 7, 2: 4, 3: 8}[layer])
                    if layer == 3:
                        ranks_pe(pe)
                    ffn_pe(pe, layer)

        @block.scalar
        def _(act):
            for n in range(4):
                act.sem_inc(att[n].p, SS)
            act.wait_ge(ld_small, 16 * N_SMALL)
            act.activation(tg[:, :], graw[:, :], ACT.Tanh).then_inc(tg_done, 1)
            act.mul(bq8[:, :], bqk[:, 0, :], 0.125).then_inc(tg_done, 1)
            act.wait_ge(sm_x, 1)
            act.activation(smul[:, :], smul[:, :], ACT.Exp).then_inc(sm_x, 1)
            act.wait_ge(tg_done, 2)
            transposes_copy_act(act, 0, CT)
            for layer, ff in SUB:
                norm_sqrt(act, ST[(layer, ff)])
                if (layer, ff) == (0, True):
                    norm_sqrt(act, 2)
                else:
                    transposes_copy_act(act, tn(layer, ff), HT)
                if not ff:
                    if layer in (1, 3):
                        proj_copy(layer, act=act)
                    if layer == 3:
                        l2norm_act(act)
                    att_act(act, layer)
                    if layer == 2:
                        norm_sqrt(act, 6)
                elif layer:
                    routing_act(act, layer)
                    ffn_act(act, layer)

        @block.vector
        def _(dve):
            for n in range(4):
                dve.sem_inc(att[n].sm, SS)
                dve.sem_inc(att[n].pt, TS)
                dve.sem_inc(att[n].on, 1)
            for bk in range(2):
                dve.sem_inc(me[bk], 1)
            for n in range(1, 4):
                dve.sem_inc(ffn[n].hid, 2)
                dve.sem_inc(ffn[n].acc, 4)
            dve.wait_ge(consts, N_CONST)
            dve.wait_ge(ld_small, 16 * N_SMALL)
            dve.tensor_scalar(smul[:, :], smul[:, :], LOG_MAX_SCALE, None, ALU.min).then_inc(sm_x, 1)
            dve.tensor_reduce(maskE[:, :], headsum[:, 0:P:32], AX.X, ALU.add)
            dve.tensor_reduce(maskO[:, :], headsum[:, 16:P:32], AX.X, ALU.add)
            dve.tensor_copy(maskf, mask8[:, 0:TOK])
            dve.tensor_copy(qm[:, :], qm8[:, :]).then_inc(dve_consts, 1)
            dve.wait_ge(dve_consts, 1)
            transposes_copy_dve(dve, 0, CT)
            for layer, ff in SUB:
                m = ST[(layer, ff)]
                ready = (ld_x, 16) if m == 0 else (x_upd, x_after(*[(l, q) for l in range(4) for q in (False, True)][
                    2 * layer + int(ff) - 1]))
                norm_stats(dve, m, X, ready)
                norm_apply(dve, m, X, Hn)
                if (layer, ff) == (0, True):
                    norm_stats(dve, 2, Hn, (h_done, TT * 2))
                    norm_apply(dve, 2, Hn, ACC)
                    dve.wait_ge(h_done, TT * 3)
                    affine_dve(dve, ACC, lng, lnb)
                    xadd_all(dve, 4, ACC, 4, 4)
                    continue
                transposes_copy_dve(dve, tn(layer, ff), HT)
                if not ff:
                    if layer == 0:
                        for c in range(DC):
                            dve.wait_ge(tpe_done[c], 4 * tn(0, False) + 4)
                        dve.wait_ge(tg_done, 2)
                    if layer in (1, 3):
                        proj_copy(layer, dve=dve)
                        for bk in range(2):
                            dve.wait_ge(pj_ev[bk], N_PJ * (1 if layer == 1 else 2))
                    if layer == 3:
                        l2norm_dve(dve)
                    if layer == 2:
                        dve.wait_ge(ld_att[2], 16 * 7)
                    att_dve(dve, layer)
                    if layer == 2:
                        norm_stats(dve, 6, ACC, (att[2].ch, 5 * BATCH))
                        norm_apply(dve, 6, ACC, ACC)
                        dve.wait_ge(h_done, TT * 7)
                        affine_dve(dve, ACC, lng2, lnb2)
                        xadd_all(dve, 8, ACC, 2, 2)
                else:
                    routing_dve(dve, layer, {1: 7, 2: 4, 3: 8}[layer], {1: 1, 2: 2, 3: 0}[layer])
                    ffn_dve(dve, layer)
                    xadd_all(dve, 4, ACC, 4 + layer, 4)


def arrays_of(i):
    import numpy as np

    def rows(x, p=128):
        return np.ascontiguousarray(np.asarray(x).reshape(-1, p).T)

    def join(*xs):
        return np.ascontiguousarray(np.concatenate([np.asarray(x) for x in xs], 0))

    def stack(*xs):
        return np.ascontiguousarray(np.stack([np.asarray(x) for x in xs], 0))

    g = {k: np.asarray(v) for k, v in i.items()}
    mask = g["mask_BxS2_bf1"].view(np.uint8).reshape(-1)
    f2b1 = join(g["L2_ffn_sb1"], g["L2_ffn_rb1"])
    return {
        "x": g["x"].reshape(2048, 256), "ctx": g["ctx_1024"].reshape(2048, 256), "fside": g["fside_SxS2_0"],
        "mask": np.ascontiguousarray(mask), "maskT": rows(mask),
        "gates": join(g["g_xattn"], g["g_ffn"]), "ln_g0": g["L0_ffn_ln_g"], "ln_b0": g["L0_ffn_ln_b"],
        "w1": stack(g["L1_xattn_Wq"].T, g["L1_xattn_Wk"].T, g["L1_xattn_Wv"].T, g["L1_xattn_Wo"].T),
        "bv1": g["L1_xattn_bv"], "bo1": g["L1_xattn_bo"],
        "f1g": join(g["L1_ffn_shared_gate"][None], g["L1_ffn_routed_gate"]),
        "f1u": join(g["L1_ffn_shared_up"][None], g["L1_ffn_routed_up"]),
        "f1d": join(g["L1_ffn_shared_down"][None], g["L1_ffn_routed_down"]),
        "wr1": g["L1_ffn_Wr"], "rbias": g["L1_ffn_routing_bias"],
        "w2": stack(g["L2_xattn_Wq"], g["L2_xattn_Wk"], g["L2_xattn_Wv"]), "wo2": g["L2_xattn_Wo"],
        "bq2": rows(g["L2_xattn_bq"]), "bk2": rows(g["L2_xattn_bk"]), "bv2": g["L2_xattn_bv"], "bo2": g["L2_xattn_bo"],
        "ln_g2": g["L2_xattn_ln_gamma"], "ln_b2": g["L2_xattn_ln_beta"],
        "wr2": g["L2_ffn_gate_w"], "gate_b": g["L2_ffn_gate_b"],
        "f2w1": join(g["L2_ffn_sw1"], g["L2_ffn_rw1"]), "f2w2": join(g["L2_ffn_sw2"], g["L2_ffn_rw2"]),
        "f2b1": np.ascontiguousarray(f2b1.reshape(6, 8, 128).transpose(0, 2, 1)),
        "f2b2": join(g["L2_ffn_sb2"], g["L2_ffn_rb2"]),
        "w3": stack(g["L3_xattn_Wq"], g["L3_xattn_Wk"], g["L3_xattn_Wv"], g["L3_xattn_Wo"]),
        "bq3": rows(g["L3_xattn_bq"]), "bo3": g["L3_xattn_bo"],
        "smul": rows(np.repeat(g["L3_xattn_scale_mul_log"].reshape(16), 16)),
        "wr3": np.ascontiguousarray(g["L3_ffn_Wg"].T), "f3w1": g["L3_ffn_W1"], "f3w2": g["L3_ffn_W2"],
    }


def kernel(**inputs):
    import numpy as _np
    import concourse.bacc as _bacc
    from concourse import mybir as _mybir
    from concourse.bass_utils import run_bass_kernel_spmd as _run

    nc = _bacc.Bacc("TRN2", target_bir_lowering=False, num_devices=1)
    arrays, args = {}, {}
    for name, arr in arrays_of(inputs).items():
        arr = _np.ascontiguousarray(arr)
        arrays[f"in_{name}"] = arr
        args[name] = nc.dram_tensor(f"in_{name}", arr.shape, _mybir.dt.from_np(arr.dtype), kind="ExternalInput").ap()
    out = nc.dram_tensor("out_x", (TOK, D), F32, kind="ExternalOutput").ap()
    build(nc, args, out)
    r = _run(nc, [arrays], core_ids=[0])
    return r.results[0]["out_x"].reshape(BATCH, SEQ, D)
```

```python
from contextlib import ExitStack

import concourse.bass as bass
from concourse import mybir

F32 = mybir.dt.float32
U8 = mybir.dt.uint8
ALU = mybir.AluOpType
ACT = mybir.ActivationFunctionType
AX = mybir.AxisListType

P = 128
BATCH, SEQ, D = 8, 256, 256
TOK = BATCH * SEQ
TT = TOK // P
TPB = SEQ // P
DC = D // P
CH = 512
NCH = TOK // CH
TPC = CH // P
NH = 16
WE = 8
NEG_BIAS = 999999.0
MASKED = -1.0e30
BIG = 1.0e30
EPS = 1e-5
NORM_EPS2 = 1e-24
LOG_MAX_SCALE = 4.605170185988092
RS = 2
PS = 4
TS = 8
T_LAG = 2
QUAD = 4

F1, F1_LAST = 6, 64
F2 = 8
F3 = 4
E1, E2, E3 = 8, 6, 8
CAP = int(TOK * 2 * 1.25 / E3)


def build(nc, a, out, stop_after=8):
    with ExitStack() as ctx:
        def sb(name, shape, dt=F32):
            return ctx.enter_context(nc.sbuf_tensor(name, shape, dt))

        def sem(name):
            return ctx.enter_context(nc.semaphore(name))

        X = sb("X", [P, TT, D])
        Hn = sb("Hn", [P, TT, D])
        HT = sb("HT", [P, DC, TOK])
        HTf = HT[:, :, :].rearrange("p c t -> p (c t)")
        CT = sb("CT", [P, DC, TOK])
        ACC = sb("ACC", [P, TT, D])
        arena = sb("arena", [P, 20992])
        ident = sb("ident", [P, P])
        ones = sb("ones", [P, P])
        tril = sb("tril", [P, P])
        headsum = sb("headsum", [P, P])
        rev = sb("rev", [P, TT, WE])
        eps = sb("eps", [P, 1])
        causal0 = sb("causal0", [P, TPB, SEQ])
        biasL = sb("biasL", [P, TPB, SEQ])
        bo_bc = sb("bo_bc", [P, 3, D])
        graw = sb("graw", [P, 8])
        tg = sb("tg", [P, 8])
        lnst = sb("lnst", [P, TT, 6])
        lnmv = sb("lnmv", [P, TT, 2])
        lnsd = sb("lnsd", [P, TT])
        lnrs = sb("lnrs", [P, TT])
        qm8 = sb("qm8", [P, TT], U8)
        qm = sb("qm", [P, TT])
        Ssb = sb("Ssb", [P, RS, TPB, SEQ])
        Pb = sb("Pb", [P, PS, TPB, SEQ])
        PTb = sb("PTb", [P, TS, TPB, SEQ])
        nmax = sb("nmax", [P, PS, TPB])
        rsum = sb("rsum", [P, BATCH, TPB, NH])
        rrec = sb("rrec", [P, TPB, NH])
        xtmp = sb("xtmp", [P, TPB, D])
        wr = sb("wr", [P, 3, DC, WE])
        rbias = sb("rbias", [P, 2, WE])
        r1 = sb("r1", [P, 4, TT])
        wts = sb("wts", [P, WE, TT])
        bqk = sb("bqk", [P, 2, 8])
        bq8 = sb("bq8", [P, 8])
        bq3 = sb("bq3", [P, DC])
        smul = sb("smul", [P, DC])
        psum = ctx.enter_context(nc.psum_tensor("psum", [P, 8, 512], F32))

        Pf = Pb[:, :, :, :].rearrange("p s t k -> p (s t k)")
        rt = Pf[:, 0:4 * TT * WE].rearrange("p (i t e) -> p i t e", i=4, t=TT)
        lg, oh1, oh2 = (Pf[:, (4 + i) * TT * WE:(5 + i) * TT * WE].rearrange("p (t e) -> p t e", t=TT)
                        for i in range(3))

        KTa = arena[:, 0:4096].rearrange("p (c t) -> p c t", c=DC)
        Va = arena[:, 4096:8192].rearrange("p (t d) -> p t d", t=TT)
        Kpad = arena[:, 8192:16384].rearrange("p (r j m t) -> p r j m t", r=2, j=8, m=DC)
        Qs = arena[:, 16384:17408].rearrange("p (r c t) -> p r c t", r=2, c=DC)
        Vpad = arena[:, 17408:18432].rearrange("p (k h w) -> p k h w", k=TPB, h=NH)
        OTs = arena[:, 18432:18944].rearrange("p (c t) -> p c t", c=DC)
        Rsb = arena[:, 18944:19456].rearrange("p (c t) -> p c t", c=DC)
        Wo = arena[:, 19456:19968].rearrange("p (c n) -> p c n", c=DC)
        bv1 = arena[:, 19968:20224]
        lng = arena[:, 20224:20480]
        lnb = arena[:, 20480:20736]
        QTa = Hn[:, :, :].rearrange("p t d -> p (t d)").rearrange("p (c t) -> p c t", c=DC)
        Wsm = PTb[:, 0:3, :, :]
        mask8 = HTf[:, 0:512].bitcast(U8)
        maskf = ACC[:, :, :].rearrange("p t d -> p (t d)")[:, 0:TOK]
        Wqkv = arena[:, 0:6144].rearrange("p (w c n) -> p w c n", w=3, c=DC)
        Wo2 = arena[:, 6144:8192].rearrange("p (c n) -> p c n", c=8)
        Q2 = arena[:, 8192:10240].rearrange("p (m t) -> p m t", m=8)
        K2 = arena[:, 10240:14336].rearrange("p (r m t) -> p r m t", r=2, m=8)
        V2 = arena[:, 14336:16384].rearrange("p (t n) -> p t n", t=TPB)
        OT2 = arena[:, 16384:18432].rearrange("p (m t) -> p m t", m=8)
        Rsb2 = arena[:, 18432:18944].rearrange("p (c t) -> p c t", c=DC)
        CTb = arena[:, 18944:19456].rearrange("p (c t) -> p c t", c=DC)
        bv2 = arena[:, 19456:20480]
        lng2 = arena[:, 20480:20736]
        lnb2 = arena[:, 20736:20992]
        WS = 4368
        wslot = [arena[:, s * WS:(s + 1) * WS] for s in range(2)]
        hid = arena[:, 2 * WS:2 * WS + 8192].rearrange("p (s f t) -> p s f t", s=2, f=8)
        sg = arena[:, 2 * WS + 8192:2 * WS + 9216].rearrange("p (s t) -> p s t", s=2)
        dtmp = arena[:, 2 * WS + 9216:2 * WS + 9728].rearrange("p (s d) -> p s d", s=2)
        b2bc = arena[:, 2 * WS + 9728:2 * WS + 10240].rearrange("p (s d) -> p s d", s=2)
        b1c = arena[:, 2 * WS + 10240:2 * WS + 10256].rearrange("p (s f) -> p s f", s=2)

        ld_x, ld_ctx, ld_small = sem("ld_x"), sem("ld_ctx"), sem("ld_small")
        ld_att = [sem(f"ld_att{i}") for i in range(4)]
        consts, dve_consts = sem("consts"), sem("dve_consts")
        tg_done = sem("tg_done")
        st_done, ag_done, sd_done, rs_done, h_done = (sem(n) for n in ("st_done", "ag_done", "sd_done", "rs_done", "h_done"))
        tp_done = [sem("tp_done0"), sem("tp_done1")]
        tpe_done = [sem("tpe_done0"), sem("tpe_done1")]
        x_upd = sem("x_upd")
        chain = sem("chain")
        act_chain = sem("act_chain")
        pj_mm = [sem("pj_mm0"), sem("pj_mm1")]
        pj_ev = [sem("pj_ev0"), sem("pj_ev1")]
        out_done = sem("out_done")

        class AttSems:
            def __init__(s, n):
                s.s, s.sm, s.p, s.t, s.pt, s.av, s.v, s.rr, s.rx, s.r, s.rc, s.on, s.wo, s.fin, s.ch = (
                    sem(f"a{n}_{w}") for w in ("scores", "max", "probs", "ptrans", "pcopy", "pv", "values", "rsum",
                                               "widened", "spread", "spreadcopy", "onorm", "wo", "fin", "chain"))
                s.kq = [sem(f"a{n}_kq0"), sem(f"a{n}_kq1")] if n != 2 else None
        att = [AttSems(n) for n in range(4)]
        mf = [sem("l2_filled6"), sem("l2_filled7")]
        me = [sem("l2_emptied6"), sem("l2_emptied7")]
        zeroed = sem("zeroed")

        class FfnSems:
            def __init__(s, n):
                s.w = [sem(f"f{n}_w0"), sem(f"f{n}_w1")]
                s.up, s.act, s.hid, s.down, s.acc, s.lg, s.init = (
                    sem(f"f{n}_{w}") for w in ("up", "act", "hid", "down", "acc", "logits", "init"))
                s.tmp = sem(f"f{n}_tmp") if n == 2 else None
        ffn = [None] + [FfnSems(n) for n in (1, 2, 3)]
        pfx = sem("prefix")
        waited = sem("waited")

        def x_after(layer, ff):
            return 12 * layer + (12 if ff else 8)

        block = ctx.enter_context(nc.Block())

        def bs(b, n=SEQ):
            return slice(b * n, b * n + n) if isinstance(b, int) else bass.ds(b * n, n)

        def norm_stats(dve, m, src, ready=None):
            if ready is not None:
                dve.wait_ge(*ready)
            for t in range(TT):
                dve.bn_stats(lnst[:, t, :], src[:, t, :]).then_inc(st_done, 1)
            dve.wait_ge(st_done, TT * (m + 1))
            for t in range(TT):
                dve.bn_aggr(lnmv[:, t, :], lnst[:, t, :]).then_inc(ag_done, 1)

        def norm_sqrt(act, m):
            act.wait_ge(ag_done, TT * (m + 1))
            act.activation(lnsd[:, :], lnmv[:, :, 1], ACT.Sqrt, bias=eps[:, 0:1]).then_inc(sd_done, 1)

        def norm_apply(dve, m, src, dst):
            dve.wait_ge(sd_done, m + 1)
            dve.reciprocal(lnrs[:, :], lnsd[:, :]).then_inc(rs_done, 1)
            dve.wait_ge(rs_done, 5 * m + 1)
            dve.tensor_tensor(lnsd[:, :], lnrs[:, :], lnrs[:, :], ALU.mult).then_inc(rs_done, 1)
            dve.wait_ge(rs_done, 5 * m + 2)
            dve.scalar_tensor_tensor(out=lnsd[:, :], in0=lnmv[:, :, 1], scalar=eps[:, 0:1], in1=lnsd[:, :],
                                     op0=ALU.add, op1=ALU.mult).then_inc(rs_done, 1)
            dve.wait_ge(rs_done, 5 * m + 3)
            dve.tensor_scalar(lnsd[:, :], lnsd[:, :], -0.5, 1.5, ALU.mult, ALU.add).then_inc(rs_done, 1)
            dve.wait_ge(rs_done, 5 * m + 4)
            dve.tensor_tensor(lnrs[:, :], lnrs[:, :], lnsd[:, :], ALU.mult).then_inc(rs_done, 1)
            dve.wait_ge(rs_done, 5 * m + 5)
            for t in range(TT):
                dve.tensor_scalar(dst[:, t, :], src[:, t, :], lnmv[:, t, 0:1], lnrs[:, t:t + 1],
                                  ALU.subtract, ALU.mult).then_inc(h_done, 1)

        def transposes_pe(pe, n, src, ready):
            for g in range(TT // 4):
                ready(g)
                for c in range(DC):
                    if n or g:
                        pe.wait_ge(tpe_done[c], 4 * n + g)
                    for j in range(4):
                        mm = pe.transpose(psum[:, c, j * P:(j + 1) * P], src[:, 4 * g + j, c * P:(c + 1) * P],
                                          ident[:, :])
                    mm.then_inc(tp_done[c], 1)

        def transposes_copy_dve(dve, n, dst, scale=1.0):
            for g in range(TT // 4):
                dve.wait_ge(tp_done[0], 4 * n + g + 1)
                dve.tensor_scalar(dst[:, 0, g * 512:(g + 1) * 512], psum[:, 0, :], scale, None,
                                  ALU.mult).then_inc(tpe_done[0], 1)

        def transposes_copy_act(act, n, dst, scale=1.0):
            for g in range(TT // 4):
                act.wait_ge(tp_done[1], 4 * n + g + 1)
                act.activation(dst[:, 1, g * 512:(g + 1) * 512], psum[:, 1, :], ACT.Copy,
                               scale=scale).then_inc(tpe_done[1], 1)

        HEADS = [8 * m + 2 * j + n for m in range(DC) for n in range(2) for j in range(QUAD)]
        SBANK = (0, 1, 5, 6)

        def att_load_sp(sp, layer, b, r, first):
            s = att[layer]
            if not first:
                sp.wait_ge(s.s, b * NH - (NH - 1))
            qsrc, ksrc = (HT, CT) if layer == 0 else (QTa, KTa)
            sp.dma_start(Qs[:, r, :, :], qsrc[:, :, bs(b)]).then_inc(s.kq[r], 16)
            for j in range(8):
                sp.dma_start(Kpad[16 * j:16 * j + 16, r, j, :, :], ksrc[16 * j:16 * j + 16, :, bs(b)]
                             ).then_inc(s.kq[r], 16)

        def att_sp(sp, layer):
            for r in range(2):
                att_load_sp(sp, layer, r, r, True)
            with sp.Fori(1, BATCH // 2) as i:
                for r in range(2):
                    att_load_sp(sp, layer, i * 2 + r, r, False)

        def values_pool(pool, layer, b):
            s = att[layer]
            pool.wait_ge(s.av, b * QUAD + 2)
            v = Va[:, bs(b, TPB), :].rearrange("p k (a w) -> p k a w", w=32)
            o = Vpad[:, :, :, :].rearrange("p k (a n) w -> p k a n w", n=2)
            for n in range(2):
                for kt in range(TPB):
                    ins = pool.tensor_copy(o[:, kt, :, n, 16 * n:16 * n + 16], v[:, kt, :, 16 * n:16 * n + 16])
            ins.then_inc(s.v, 1)

        def att_pool(pool, layer):
            with pool.Fori(0, BATCH) as b:
                values_pool(pool, layer, b)

        def scores_pe(pe, layer, b, k, r=0):
            s = att[layer]
            if layer == 2:
                pe.wait_ge(s.p, b * NH + k + 1 - 2 + PS)
                bank, q, kk = k % 2, Q2[:, k // 2, :], K2[:, k % 2, k // 2, :]
            else:
                pe.wait_ge(s.sm, b * NH + k + 1)
                h = HEADS[k]
                bank, q, kk = SBANK[k % 4], Qs[:, r, h // 8, :], Kpad[:, r, h % 8, h // 8, :]
            for qt in range(TPB):
                mm = pe.matmul(psum[:, bank, qt * SEQ:(qt + 1) * SEQ], q[:, qt * P:(qt + 1) * P], kk,
                               start=True, stop=True)
            mm.then_inc(s.s, 1)

        def max_dve(dve, layer, b, k):
            s = att[layer]
            dve.wait_ge(s.s, b * NH + k + 2)
            if layer == 2:
                dve.wait_ge(s.p, b * NH + k + 1)
                dve.tensor_reduce(nmax[:, k % PS, :], psum[:, k % 2, :].rearrange("p (q k) -> p q k", q=TPB), AX.X,
                                  ALU.max, negate=True).then_inc(s.sm, 1)
                return
            dve.wait_ge(s.p, b * NH + k + 1 - RS + PS)
            dve.sem_inc(waited, 1)
            for qt in range(TPB):
                ins = dve.tensor_tensor_reduce(Ssb[:, k % RS, qt, :], psum[:, SBANK[k % 4], qt * SEQ:(qt + 1) * SEQ],
                                               biasL[:, qt, :], -1.0, 3.0e38, ALU.add, ALU.min,
                                               nmax[:, k % PS, qt:qt + 1])
            ins.then_inc(s.sm, 1)

        def exp_act(act, layer, b, k):
            s = att[layer]
            act.wait_ge(s.sm, b * NH + k + 1 + 4)
            act.wait_ge(s.t, b * NH + k + 1)
            h = k if layer == 2 else HEADS[k]
            for qt in range(TPB):
                src, sc = (psum[:, k % 2, qt * SEQ:(qt + 1) * SEQ], 1.0) if layer == 2 else (Ssb[:, k % RS, qt, :], -1.0)
                acc = rsum[:, b, qt, h:h + 1] if isinstance(b, int) else rsum[:, bass.ds(b, 1), qt, h:h + 1]
                ins = act.activation(Pb[:, k % PS, qt, :], src, ACT.Exp, bias=nmax[:, k % PS, qt:qt + 1], scale=sc,
                                     accum_out=acc)
            ins.then_inc(s.p, 1)

        def ptrans_pe(pe, layer, b, k):
            s = att[layer]
            pe.wait_ge(s.p, b * NH + k + 1 + PS)
            pe.wait_ge(s.pt, b * NH + k + 1)
            for kt in range(TPB):
                for qt in range(TPB):
                    mm = pe.transpose(psum[:, 2 + k % 2, kt * SEQ + qt * P:kt * SEQ + (qt + 1) * P],
                                      Pb[:, k % PS, qt, kt * P:(kt + 1) * P], ident[:, :])
            mm.then_inc(s.t, 1)

        def pcopy_dve(dve, layer, b, k):
            s = att[layer]
            dve.wait_ge(s.t, b * NH + k + 1 + PS)
            if k % QUAD == 0:
                dve.wait_ge(s.av, b * QUAD + k // QUAD + 1)
            dve.tensor_copy(PTb[:, k % TS, :, :], psum[:, 2 + k % 2, :].rearrange("p (k q) -> p k q", k=TPB)
                            ).then_inc(s.pt, 1)

        def pv_pe(pe, layer, b, g):
            s = att[layer]
            pe.wait_ge(s.pt, b * NH + QUAD * (g + 1) + 2)
            if g == 0:
                pe.wait_ge(s.v, b + 1)
                pe.wait_ge(s.on, b + 1)
            m, n = g // 2, g % 2
            for kt in range(TPB):
                for j in range(QUAD):
                    k = QUAD * g + j
                    mm = pe.matmul(psum[32 * j:32 * j + 32, 4, m * SEQ:(m + 1) * SEQ], Vpad[:, kt, HEADS[k], :],
                                   PTb[:, k % TS, kt, :], start=(n == 0 and kt == 0),
                                   stop=(n == 1 and kt == TPB - 1))
            mm.then_inc(s.av, 1)

        def rsums(b, h0, n):
            if isinstance(b, int):
                return rsum[:, b, :, h0:h0 + n]
            return rsum[:, bass.ds(b, 1), :, h0:h0 + n].rearrange("p a q h -> p (a q) h")

        def recip_dve(dve, layer, b):
            s = att[layer]
            dve.wait_ge(s.p, b * NH + NH + PS)
            if layer:
                dve.reciprocal(rrec[:, :, :], rsums(b, 0, NH)).then_inc(s.rr, 1)
                return
            dve.reciprocal(rrec[:, :, :], rsums(b, 0, NH)).then_inc(s.ch, 1)
            dve.wait_ge(s.ch, b + 1)
            dve.tensor_tensor(rrec[:, :, :], rrec[:, :, :],
                              qm[:, bs(b, TPB)].unsqueeze(2).broadcast_to([P, TPB, NH]), ALU.mult).then_inc(s.rr, 1)

        def spread_pe(pe, layer, b):
            s = att[layer]
            pe.wait_ge(s.rx, b + 1)
            pe.wait_ge(s.fin, b + 1)
            for m in range(DC):
                for qt in range(TPB):
                    mm = pe.transpose(psum[:, 7, m * SEQ + qt * P:m * SEQ + (qt + 1) * P],
                                      Rsb[:, qt, m * P:(m + 1) * P], ident[:, :])
            mm.then_inc(s.r, 1)

        def widen_act(act, layer, b):
            s = att[layer]
            act.wait_ge(s.rr, b + 1)
            act.activation(Rsb[:, :, :].rearrange("p q (h w) -> p q h w", w=16),
                           rrec[:, :, :].unsqueeze(3).broadcast_to([P, TPB, NH, 16]), ACT.Copy).then_inc(s.rx, 1)

        def spread_act(act, layer, b):
            s = att[layer]
            act.wait_ge(s.r, b + 1)
            act.activation(Rsb[:, :, :], psum[:, 7, :].rearrange("p (c t) -> p c t", c=DC), ACT.Copy).then_inc(s.rc, 1)

        def onorm_dve(dve, layer, b):
            s = att[layer]
            dve.wait_ge(s.av, b * QUAD + QUAD + 2)
            dve.wait_ge(s.rc, b + 1)
            dve.tensor_tensor(OTs[:, :, :], psum[:, 4, :].rearrange("p (c t) -> p c t", c=DC), Rsb[:, :, :],
                              ALU.mult).then_inc(s.on, 1)

        def final_pe(pe, layer, b):
            s = att[layer]
            pe.wait_ge(s.on, b + 2)
            for qt in range(TPB):
                for c in range(DC):
                    if layer:
                        mm = pe.matmul(psum[:, 7, qt * D:(qt + 1) * D], OTs[:, c, qt * P:(qt + 1) * P], Wo[:, c, :],
                                       start=(c == 0), stop=(c == DC - 1))
                    else:
                        mm = pe.transpose(psum[:, 7, qt * D + c * P:qt * D + (c + 1) * P],
                                          OTs[:, c, qt * P:(qt + 1) * P], ident[:, :])
            mm.then_inc(s.wo, 1)

        def xadd_dve(dve, layer, b):
            s = att[layer]
            xb = X[:, bs(b, TPB), :]
            dve.wait_ge(s.wo, b + 1)
            y = psum[:, 7, :].rearrange("p (q d) -> p q d", q=TPB)
            if layer:
                bo = bo_bc[:, {1: 0, 3: 2}[layer], :]
                dve.tensor_tensor(xtmp[:, :, :], y, bo.unsqueeze(1).broadcast_to([P, TPB, D]), ALU.add
                                  ).then_inc(s.fin, 1)
                dve.wait_ge(s.fin, b + 2)
                dve.scalar_tensor_tensor(out=xb, in0=xtmp[:, :, :], scalar=tg[:, layer:layer + 1], in1=xb,
                                         op0=ALU.mult, op1=ALU.add).then_inc(x_upd, 1)
            else:
                dve.scalar_tensor_tensor(out=xb, in0=y, scalar=tg[:, 0:1], in1=xb, op0=ALU.mult,
                                         op1=ALU.add).then_inc(s.fin, 1)

        def att_step_pe(pe, layer, b, pair, r, k, cur, prev):
            if cur:
                if k == 0:
                    pe.wait_ge(att[layer].kq[r], pair * 144 + 144)
                scores_pe(pe, layer, b, k, r)
            if k < T_LAG:
                if prev:
                    ptrans_pe(pe, layer, b - 1, NH + k - T_LAG)
            elif cur:
                ptrans_pe(pe, layer, b, k - T_LAG)
            if prev and k == 2:
                pv_pe(pe, layer, b - 1, 3)
            elif cur and k in (6, 10, 14):
                pv_pe(pe, layer, b, (k - 6) // 4)
            if prev and k == 3:
                spread_pe(pe, layer, b - 1)
            if prev and k == 6:
                final_pe(pe, layer, b - 1)

        def att_step_act(act, layer, b, pair, r, k, cur, prev):
            if cur:
                exp_act(act, layer, b, k)
            if prev and k == 1:
                widen_act(act, layer, b - 1)
            if prev and k == 3:
                spread_act(act, layer, b - 1)

        def att_step_dve(dve, layer, b, pair, r, k, cur, prev):
            if cur:
                if layer == 0 and k == 0:
                    dve.wait_ge(att[0].sm, b * NH + 4)
                    for qt in range(TPB):
                        ins = dve.tensor_tensor(biasL[:, qt, :], causal0[:, qt, :], maskf[:, bs(b)], ALU.mult)
                    ins.then_inc(own_bias, 1)
                    dve.wait_ge(own_bias, b + 1)
                max_dve(dve, layer, b, k)
            if k < T_LAG:
                if prev:
                    pcopy_dve(dve, layer, b - 1, NH + k - T_LAG)
                    if k == T_LAG - 1:
                        recip_dve(dve, layer, b - 1)
            elif cur:
                pcopy_dve(dve, layer, b, k - T_LAG)
            if prev and k == 4:
                onorm_dve(dve, layer, b - 1)
            if prev and k == 7:
                xadd_dve(dve, layer, b - 1)

        own_bias = sem("bias0")

        def att_loop(eng, layer, step, last=8):
            for r in range(2):
                for k in range(NH):
                    step(eng, layer, r, 0, r, k, True, r > 0)
            with eng.Fori(1, BATCH // 2) as i:
                for r in range(2):
                    for k in range(NH):
                        step(eng, layer, i * 2 + r, i, r, k, True, True)
            for k in range(last):
                step(eng, layer, BATCH, 0, 0, k, False, True)

        def att_pe(pe, layer):
            att_loop(pe, layer, att_step_pe)

        def att_act(act, layer):
            att_loop(act, layer, att_step_act)

        def att_dve(dve, layer):
            att_loop(dve, layer, att_step_dve)
            if layer == 0:
                dve.wait_ge(att[0].fin, BATCH + 1)
                dve.sem_inc(x_upd, BATCH)

        def proj_steps(layer):
            st = [("q", m, n) for m in range(DC) for n in range(NCH)]
            st += [("k", m, n) for m in range(DC) for n in range(NCH)]
            return st + [("v", t, 0) for t in range(TT // 2)]

        N_PJ = len(proj_steps(1)) // 2

        def proj_pe(pe, layer):
            pe.wait_ge(ld_att[layer], 16 * {1: 5, 3: 5}[layer])
            pe.wait_ge(tpe_done[0], 4 * tn(layer, False) + 4)
            pe.wait_ge(tpe_done[1], 4 * tn(layer, False) + 4)
            base = 0 if layer == 1 else N_PJ
            for i, (kind, m, n) in enumerate(proj_steps(layer)):
                bk = i % 2
                if base + i // 2:
                    pe.wait_ge(pj_ev[bk], base + i // 2)
                bank = psum[:, 2 + bk, :]
                if kind == "v":
                    for j in range(2):
                        t = 2 * m + j
                        for c in range(DC):
                            mm = pe.matmul(bank[:, j * D:(j + 1) * D], CT[:, c, t * P:(t + 1) * P], Wsm[:, 2, c, :],
                                           start=(c == 0), stop=(c == DC - 1))
                else:
                    src = HT if kind == "q" else CT
                    for c in range(DC):
                        mm = pe.matmul(bank, Wsm[:, 0 if kind == "q" else 1, c, m * P:(m + 1) * P],
                                       src[:, c, n * CH:(n + 1) * CH], start=(c == 0), stop=(c == DC - 1))
                mm.then_inc(pj_mm[bk], 1)

        def proj_copy(layer, dve=None, act=None):
            base = 0 if layer == 1 else N_PJ
            for i, (kind, m, n) in enumerate(proj_steps(layer)):
                bk = i % 2
                eng = dve if bk == 0 or kind == "v" else act
                if eng is None:
                    continue
                eng.wait_ge(pj_mm[bk], base + i // 2 + 1)
                bank = psum[:, 2 + bk, :]
                if kind == "v":
                    dst, src = Va[:, 2 * m:2 * m + 2, :], bank.rearrange("p (t d) -> p t d", t=2)
                    if layer == 1:
                        ins = dve.tensor_tensor(dst, src, bv1.unsqueeze(1).broadcast_to([P, 2, D]), ALU.add)
                    else:
                        ins = dve.tensor_copy(dst, src)
                else:
                    dst, src = (QTa if kind == "q" else KTa)[:, m, n * CH:(n + 1) * CH], bank
                    if kind == "q" and layer == 1:
                        if eng is act:
                            ins = act.activation(dst, src, ACT.Copy, scale=0.25)
                        else:
                            ins = dve.tensor_scalar(dst, src, 0.25, None, ALU.mult)
                    elif eng is act and kind == "q" and layer == 3:
                        ins = act.activation(dst, src, ACT.Identity, bias=bq3[:, m:m + 1])
                    elif eng is act:
                        ins = act.activation(dst, src, ACT.Copy)
                    elif kind == "q" and layer == 3:
                        ins = dve.tensor_scalar(dst, src, bq3[:, m:m + 1], None, ALU.add)
                    else:
                        ins = dve.tensor_copy(dst, src)
                ins.then_inc(pj_ev[bk], 1)

        l2_sq, l2_mm, l2_sd, l2_mx, l2_rc, l2_sc = (sem(n) for n in ("l2_sq", "l2_sum", "l2_sqrt", "l2_max", "l2_rec", "l2_scaled"))
        sm_x = sem("scale_mul")

        def l2_steps():
            return [(k, m, n) for k in range(2) for m in range(DC) for n in range(NCH)]

        def l2norm_pool(pool):
            pool.wait_ge(pj_ev[0], 2 * N_PJ)
            pool.wait_ge(pj_ev[1], 2 * N_PJ)
            for i, (k, m, n) in enumerate(l2_steps()):
                x = (QTa, KTa)[k][:, m, n * CH:(n + 1) * CH]
                if i >= 4:
                    pool.wait_ge(l2_mm, i - 3)
                pool.tensor_tensor(ACCf(i % 4), x, x, ALU.mult).then_inc(l2_sq, 1)

        def ACCf(i):
            return ACC[:, 2 * i:2 * i + 2, :].rearrange("p t d -> p (t d)")

        def l2norm_pe(pe):
            for i in range(16):
                pe.wait_ge(l2_sq, i + 1)
                if i >= 4:
                    pe.wait_ge(l2_mx, i - 3)
                pe.matmul(psum[:, 4 + i % 4, :], headsum[:, :], ACCf(i % 4), start=True, stop=True).then_inc(l2_mm, 1)

        def l2norm_act(act):
            for i in range(16):
                act.wait_ge(l2_mx, i + 1)
                act.activation(ACCf(4 + i % 4), ACCf(4 + i % 4), ACT.Sqrt).then_inc(l2_sd, 1)

        def l2norm_dve(dve):
            def floor(i):
                dve.wait_ge(l2_mm, i + 1)
                if i >= 4:
                    dve.wait_ge(l2_sc, i - 3)
                dve.tensor_scalar(ACCf(4 + i % 4), psum[:, 4 + i % 4, :], NORM_EPS2, None, ALU.max).then_inc(l2_mx, 1)

            def scale(i):
                k, m, n = l2_steps()[i]
                x = (QTa, KTa)[k][:, m, n * CH:(n + 1) * CH]
                dve.wait_ge(l2_sd, i + 1)
                dve.reciprocal(ACCf(4 + i % 4), ACCf(4 + i % 4)).then_inc(l2_rc, 1)
                dve.wait_ge(l2_rc, i + 1)
                if k == 0:
                    dve.scalar_tensor_tensor(out=x, in0=x, scalar=smul[:, m:m + 1], in1=ACCf(4 + i % 4),
                                             op0=ALU.mult, op1=ALU.mult).then_inc(l2_sc, 1)
                else:
                    dve.tensor_tensor(x, x, ACCf(4 + i % 4), ALU.mult).then_inc(l2_sc, 1)
            dve.wait_ge(sm_x, 2)
            for i in range(16 + 2):
                if i < 16:
                    floor(i)
                if i >= 2:
                    scale(i - 2)
            dve.wait_ge(l2_sc, 16)

        def base2(b, bk):
            if bk:
                return b * 8
            return 0 if isinstance(b, int) and b == 0 else b * 9 - 1

        def fill_of(b, g):
            if g % 2 == 0:
                return 1, 6 + g // 2
            return 0, (6 if isinstance(b, int) and b == 0 else 7) + g // 2

        def empty2(pe, b, bk, i):
            pe.wait_ge(me[bk], base2(b, bk) + i + 1)

        def full2(eng, b, bk, i):
            eng.wait_ge(mf[bk], base2(b, bk) + i + 1)

        def stage2_pool(pool, b):
            s = att[2]
            pool.wait_ge(s.s, b * NH + 1)
            pool.tensor_copy(CTb[:, :, :], CT[:, :, bs(b)]).then_inc(s.v, 1)

        def att2_pool(pool):
            with pool.Fori(0, BATCH) as b:
                stage2_pool(pool, b)

        def project2_pe(pe, b):
            s = att[2]
            for w, src in ((0, HT), (1, CT)):
                for j in range(4):
                    bk = j % 2
                    empty2(pe, b, bk, 2 * w + j // 2)
                    for n in range(2):
                        m = 2 * j + n
                        for c in range(DC):
                            mm = pe.matmul(psum[:, 6 + bk, n * SEQ:(n + 1) * SEQ], Wqkv[:, w, c, m * P:(m + 1) * P],
                                           src[:, c, bs(b)], start=(c == 0), stop=(c == DC - 1))
                    mm.then_inc(mf[bk], 1)
            pe.wait_ge(s.v, b + 1)
            for t in range(TPB):
                for bk in range(2):
                    empty2(pe, b, bk, 4 + t)
                    for c in range(DC):
                        mm = pe.matmul(psum[:, 6 + bk, :], CTb[:, c, t * P:(t + 1) * P],
                                       Wqkv[:, 2, c, bk * 512:(bk + 1) * 512], start=(c == 0), stop=(c == DC - 1))
                    mm.then_inc(mf[bk], 1)
            for bk in range(2):
                empty2(pe, b, bk, 6)

        def project2_dve(dve, b):
            s = att[2]
            dve.wait_ge(s.s, b * NH + 1)
            for w in range(2):
                for j in (0, 2):
                    full2(dve, b, 0, 2 * w + j // 2)
                    src = psum[:, 6, :].rearrange("p (m t) -> p m t", m=2)
                    if w == 0:
                        ins = dve.scalar_tensor_tensor(
                            out=Q2[:, 2 * j:2 * j + 2, :], in0=src, scalar=0.125,
                            in1=bq8[:, 2 * j:2 * j + 2].unsqueeze(2).broadcast_to([P, 2, SEQ]), op0=ALU.mult, op1=ALU.add)
                    else:
                        for n in range(2):
                            q = slice(64 * n, 64 * n + 64)
                            ins = dve.tensor_tensor(
                                K2[q, n, 2 * j:2 * j + 2, :], src[q], bqk[q, 1, 2 * j:2 * j + 2].unsqueeze(2).broadcast_to(
                                    [64, 2, SEQ]), ALU.add)
                    ins.then_inc(me[0], 1)
            dve.wait_ge(s.av, b * QUAD + 2)
            for t in range(TPB):
                for bk in range(2):
                    full2(dve, b, bk, 4 + t)
                    cols = slice(bk * 512, (bk + 1) * 512)
                    dve.tensor_tensor(V2[:, t, cols], psum[:, 6 + bk, :], bv2[:, cols], ALU.add).then_inc(me[bk], 1)

        def project2_act(act, b):
            s = att[2]
            act.wait_ge(s.s, b * NH + 1)
            for w in range(2):
                for j in (1, 3):
                    full2(act, b, 1, 2 * w + j // 2)
                    for n in range(2):
                        m = 2 * j + n
                        src = psum[:, 7, n * SEQ:(n + 1) * SEQ]
                        if w == 0:
                            ins = act.activation(Q2[:, m, :], src, ACT.Identity, bias=bq8[:, m:m + 1], scale=0.125)
                        else:
                            for o in range(2):
                                q = slice(64 * o, 64 * o + 64)
                                ins = act.activation(K2[q, o, m, :], src[q], ACT.Identity, bias=bqk[q, 1, m:m + 1])
                    ins.then_inc(me[1], 1)

        def pv2_pe(pe, b, g):
            s = att[2]
            pe.wait_ge(s.pt, b * NH + QUAD * (g + 1) + 2)
            pe.wait_ge(s.on, b * QUAD + g + 1)
            for m in range(2):
                for kt in range(TPB):
                    for n in range(2):
                        k = QUAD * g + 2 * m + n
                        mm = pe.matmul(psum[64 * n:64 * n + 64, 4 + g % 2, m * SEQ:(m + 1) * SEQ],
                                       V2[:, kt, 64 * k:64 * k + 64], PTb[:, k % TS, kt, :], start=(kt == 0),
                                       stop=(kt == TPB - 1))
            mm.then_inc(s.av, 1)

        def recip2_dve(dve, b, g):
            s = att[2]
            dve.wait_ge(s.p, b * NH + QUAD * (g + 1) + PS)
            dve.reciprocal(rrec[:, :, QUAD * g:QUAD * (g + 1)], rsums(b, QUAD * g, QUAD)).then_inc(s.rr, 1)

        def spread2_pe(pe, b, g):
            s = att[2]
            bk, i = fill_of(b, g)
            pe.wait_ge(s.rx, b * QUAD + g + 1)
            empty2(pe, b, bk, i)
            for m in range(2):
                for qt in range(TPB):
                    mm = pe.transpose(psum[:, 6 + bk, m * SEQ + qt * P:m * SEQ + (qt + 1) * P],
                                      Rsb2[:, qt, m * P:(m + 1) * P], ident[:, :])
            mm.then_inc(mf[bk], 1)

        def widen2_act(act, b, g):
            s = att[2]
            act.wait_ge(s.rr, b * QUAD + g + 1)
            act.activation(Rsb2[:, :, :].rearrange("p q (h w) -> p q h w", w=64),
                           rrec[:, :, QUAD * g:QUAD * (g + 1)].unsqueeze(3).broadcast_to([P, TPB, QUAD, 64]), ACT.Copy
                           ).then_inc(s.rx, 1)

        def spread2_act(act, b, g):
            s = att[2]
            bk, i = fill_of(b, g)
            full2(act, b, bk, i)
            act.activation(Rsb2[:, :, :], psum[:, 6 + bk, :].rearrange("p (c t) -> p c t", c=DC), ACT.Copy
                           ).then_inc(me[bk], 1)

        def onorm2_dve(dve, b, g):
            s = att[2]
            bk, i = fill_of(b, g)
            dve.wait_ge(s.av, b * QUAD + g + 3)
            dve.wait_ge(me[bk], base2(b, bk) + i + 2)
            dve.tensor_tensor(OT2[:, 2 * g:2 * g + 2, :], psum[:, 4 + g % 2, :].rearrange("p (c t) -> p c t", c=DC),
                              Rsb2[:, :, :], ALU.mult).then_inc(s.on, 1)

        def wo2_pe(pe, nb, i):
            s = att[2]
            pe.wait_ge(s.on, nb * QUAD + 2)
            empty2(pe, nb, 0, i)
            for qt in range(TPB):
                for m in range(8):
                    mm = pe.matmul(psum[:, 6, qt * D:(qt + 1) * D], OT2[:, m, qt * P:(qt + 1) * P], Wo2[:, m, :],
                                   start=(m == 0), stop=(m == 7))
            mm.then_inc(mf[0], 1)

        def y2_dve(dve, nb, i):
            s = att[2]
            full2(dve, nb, 0, i)
            dve.tensor_tensor(xtmp[:, :, :], psum[:, 6, :].rearrange("p (q d) -> p q d", q=TPB),
                              bo_bc[:, 1, :].unsqueeze(1).broadcast_to([P, TPB, D]), ALU.add).then_inc(me[0], 1)
            dve.wait_ge(me[0], base2(nb, 0) + i + 2)
            dve.tensor_tensor(ACC[:, bs(nb - 1, TPB), :], xtmp[:, :, :], Hn[:, bs(nb - 1, TPB), :],
                              ALU.add).then_inc(s.fin, 1)

        TAIL = NH + 5

        def att2_body_pe(pe, b, first):
            project2_pe(pe, b)
            if not first:
                wo2_pe(pe, b, 6)
            for k in range(TAIL):
                if k < NH:
                    scores_pe(pe, 2, b, k)
                if T_LAG <= k < NH + T_LAG:
                    ptrans_pe(pe, 2, b, k - T_LAG)
                if k >= 6 and (k - 6) % 4 == 0:
                    pv2_pe(pe, b, (k - 6) // 4)
                if k >= 7 and (k - 7) % 4 == 0:
                    spread2_pe(pe, b, (k - 7) // 4)

        def att2_body_act(act, b, first):
            project2_act(act, b)
            for k in range(TAIL):
                if k < NH:
                    exp_act(act, 2, b, k)
                if k >= 5 and (k - 5) % 4 == 0 and k < NH + 4:
                    widen2_act(act, b, (k - 5) // 4)
                if k >= 7 and (k - 7) % 4 == 0:
                    spread2_act(act, b, (k - 7) // 4)

        def att2_body_dve(dve, b, first):
            project2_dve(dve, b)
            if not first:
                y2_dve(dve, b, 6)
            for k in range(TAIL):
                if k < NH:
                    max_dve(dve, 2, b, k)
                if T_LAG <= k < NH + T_LAG:
                    pcopy_dve(dve, 2, b, k - T_LAG)
                if k >= 5 and (k - 5) % 4 == 0 and k < NH + 4:
                    recip2_dve(dve, b, (k - 5) // 4)
                if k >= 8 and (k - 8) % 4 == 0:
                    onorm2_dve(dve, b, (k - 8) // 4)

        def att2_pe(pe, layer):
            att2_body_pe(pe, 0, True)
            with pe.Fori(1, BATCH) as b:
                att2_body_pe(pe, b, False)
            wo2_pe(pe, BATCH, 0)

        def att2_act(act, layer):
            att2_body_act(act, 0, True)
            with act.Fori(1, BATCH) as b:
                att2_body_act(act, b, False)

        def att2_dve(dve, layer):
            att2_body_dve(dve, 0, True)
            with dve.Fori(1, BATCH) as b:
                att2_body_dve(dve, b, False)
            y2_dve(dve, BATCH, 0)

        def logits_pe(pe, layer, n):
            f = ffn[layer]
            pe.wait_ge(tpe_done[0], 4 * tn(layer, True) + 4)
            pe.wait_ge(tpe_done[1], 4 * tn(layer, True) + 4)
            for t in range(TT):
                for c in range(DC):
                    mm = pe.matmul(psum[:, 4, t * WE:t * WE + n], HT[:, c, t * P:(t + 1) * P], wr[:, layer - 1, c, 0:n],
                                   start=(c == 0), stop=(c == DC - 1))
            mm.then_inc(f.lg, 1)

        steps = [0]

        def routing_dve(dve, layer, n, shared):
            f = ffn[layer]

            def link(ins):
                steps[0] += 1
                ins.then_inc(chain, 1)
                dve.wait_ge(chain, steps[0])

            def row(x):
                return x.unsqueeze(2).broadcast_to([P, TT, n])

            z = lg[:, :, 0:n]
            t0, t1, pr, msk = (rt[:, i, :, 0:n] for i in range(4))
            o1, o2, rv = oh1[:, :, 0:n], oh2[:, :, 0:n], rev[:, :, 0:n]
            dve.wait_ge(f.lg, 1)
            ps = psum[:, 4, 0:TT * WE].rearrange("p (t e) -> p t e", e=WE)[:, :, 0:n]
            if layer == 1:
                link(dve.tensor_tensor(z, ps, rbias[:, 0, 0:n].unsqueeze(1).broadcast_to([P, TT, n]), ALU.mult))
                dve.sem_inc(rt_in, 1)
                dve.wait_ge(rt_out, 1)
                val = pr
            elif layer == 2:
                link(dve.tensor_tensor(z, ps, rbias[:, 1, 0:n].unsqueeze(1).broadcast_to([P, TT, n]), ALU.add))
                link(dve.tensor_reduce(r1[:, 0, :], z, AX.X, ALU.max))
                link(dve.tensor_tensor(z, z, row(r1[:, 0, :]), ALU.subtract))
                dve.sem_inc(rt_in, 1)
                dve.wait_ge(rt_out, 2)
                link(dve.tensor_reduce(r1[:, 0, :], pr, AX.X, ALU.add))
                link(dve.reciprocal(r1[:, 1, :], r1[:, 0, :]))
                link(dve.tensor_tensor(pr, pr, row(r1[:, 1, :]), ALU.mult))
                val = pr
            else:
                link(dve.tensor_copy(z, ps))
                val = z

            def pick(values, best, onehot):
                link(dve.tensor_reduce(best, values, AX.X, ALU.max))
                link(dve.tensor_tensor(t0, values, row(best), ALU.is_equal))
                link(dve.tensor_tensor(t0, t0, rv, ALU.mult))
                link(dve.tensor_reduce(r1[:, 3, :], t0, AX.X, ALU.max))
                link(dve.tensor_tensor(onehot, t0, row(r1[:, 3, :]), ALU.is_equal))

            pick(val, r1[:, 0, :], o1)
            link(dve.scalar_tensor_tensor(out=t1, in0=o1, scalar=-BIG, in1=val, op0=ALU.mult, op1=ALU.add))
            pick(t1, r1[:, 1, :], o2)
            link(dve.tensor_tensor(msk, o1, o2, ALU.add))
            if layer == 1:
                link(dve.tensor_tensor(r1[:, 2, :], r1[:, 0, :], r1[:, 1, :], ALU.add))
                link(dve.reciprocal(r1[:, 3, :], r1[:, 2, :]))
                link(dve.tensor_tensor(t0, pr, msk, ALU.mult))
                link(dve.tensor_tensor(t0, t0, row(r1[:, 3, :]), ALU.mult))
            elif layer == 2:
                link(dve.tensor_tensor(t0, pr, msk, ALU.mult))
            else:
                link(dve.tensor_tensor(r1[:, 2, :], r1[:, 1, :], r1[:, 0, :], ALU.subtract))
                dve.sem_inc(rt_in, 1)
                dve.wait_ge(rt_out, 3)
                link(dve.tensor_scalar(r1[:, 2, :], r1[:, 1, :], 1.0, None, ALU.add))
                link(dve.reciprocal(r1[:, 0, :], r1[:, 2, :]))
                link(dve.tensor_tensor(r1[:, 1, :], r1[:, 1, :], r1[:, 0, :], ALU.mult))
                link(dve.tensor_tensor(t0, o1, row(r1[:, 0, :]), ALU.mult))
                link(dve.tensor_tensor(t1, o2, row(r1[:, 1, :]), ALU.mult))
                link(dve.tensor_tensor(t0, t0, t1, ALU.add))
                dve.sem_inc(pfx, 1)
                dve.wait_ge(pfx, 2)
                link(dve.tensor_scalar(t1, psum[:, 5, 0:TT * WE].rearrange("p (t e) -> p t e", e=WE),
                                       CAP + 0.5, None, ALU.is_le))
                link(dve.tensor_tensor(t0, t0, t1, ALU.mult))
            for e in range(shared):
                link(dve.memset(wts[:, e, :], 1.0 / shared))
            link(dve.tensor_copy(wts[:, shared:shared + n, :].rearrange("p e t -> p t e"), t0))

        def routing_act(act, layer):
            if layer == 1:
                act.wait_ge(rt_in, 1)
                act.activation(rt[:, 2, :, 0:7], lg[:, :, 0:7], ACT.Sigmoid).then_inc(rt_out, 1)
            elif layer == 2:
                act.wait_ge(rt_in, 2)
                act.activation(rt[:, 2, :, 0:4], lg[:, :, 0:4], ACT.Exp).then_inc(rt_out, 1)
            else:
                act.wait_ge(rt_in, 3)
                act.activation(r1[:, 1, :], r1[:, 2, :], ACT.Exp).then_inc(rt_out, 1)

        def ranks_pe(pe):
            pe.wait_ge(pfx, 1)
            pe.matmul(psum[:, 5, 0:TT * WE], tril[:, :], rt[:, 3, :, :].rearrange("p t e -> p (t e)"),
                      start=True, stop=False, skip_group_check=True)
            for t in range(TT - 1):
                mm = pe.matmul(psum[:, 5, (t + 1) * WE:TT * WE], ones[:, :],
                               rt[:, 3, t, :].unsqueeze(1).broadcast_to([P, TT - 1 - t, WE]),
                               start=False, stop=(t == TT - 2), skip_group_check=True)
            mm.then_inc(pfx, 1)

        def ffn_shape(layer):
            return {1: (E1, F1, F1_LAST, True), 2: (E2, F2, P, False), 3: (E3, F3, P, True)}[layer]

        def wviews(layer, s):
            w = wslot[s]
            if layer == 1:
                g = w[:, 0:1408].rearrange("p (c n) -> p c n", c=DC)
                u = w[:, 1408:2816].rearrange("p (c n) -> p c n", c=DC)
                return g, u, w[:, 2816:4352].rearrange("p (f n) -> p f n", f=F1)
            if layer == 2:
                return (w[:, 0:2048].rearrange("p (c n) -> p c n", c=DC), None,
                        w[:, 2048:4096].rearrange("p (f n) -> p f n", f=F2))
            w1 = w[:, 0:2048].rearrange("p (c n) -> p c n", c=DC)
            return w1[:, :, 0:512], w1[:, :, 512:1024], w[:, 2048:3072].rearrange("p (f n) -> p f n", f=F3)

        LOADS = {1: 4, 2: 4, 3: 2}

        def load_expert(sp, layer, i, s):
            f = ffn[layer]
            e = 2 * i + s
            g, u, d = wviews(layer, s)

            def ex(name):
                return a[name][e] if isinstance(e, int) else a[name][bass.ds(e, 1)].squeeze(0)
            if layer == 1:
                sp.dma_start(g, ex("f1g").rearrange("(c p) n -> p c n", p=P)).then_inc(f.w[s], 16)
                sp.dma_start(u, ex("f1u").rearrange("(c p) n -> p c n", p=P)).then_inc(f.w[s], 16)
                sp.dma_start(d[:, 0:F1 - 1, :], ex("f1d")[0:(F1 - 1) * P, :].rearrange("(f p) n -> p f n", p=P)
                             ).then_inc(f.w[s], 16)
                sp.dma_start(d[0:F1_LAST, F1 - 1, :], ex("f1d")[(F1 - 1) * P:, :]).then_inc(f.w[s], 16)
            elif layer == 2:
                sp.dma_start(g, ex("f2w1").rearrange("(c p) n -> p c n", p=P)).then_inc(f.w[s], 16)
                sp.dma_start(d, ex("f2w2").rearrange("(f p) n -> p f n", p=P)).then_inc(f.w[s], 16)
                sp.dma_start(b1c[:, s, :], ex("f2b1")).then_inc(f.w[s], 16)
                sp.dma_start(b2bc[:, s, :], ex("f2b2").partition_broadcast(P)).then_inc(f.w[s], 16)
            else:
                sp.dma_start(wslot[s][:, 0:2048].rearrange("p (c n) -> p c n", c=DC),
                             ex("f3w1").rearrange("(c p) n -> p c n", p=P)).then_inc(f.w[s], 16)
                sp.dma_start(d, ex("f3w2").rearrange("(f p) n -> p f n", p=P)).then_inc(f.w[s], 16)

        def ffn_loads(sp, layer):
            f = ffn[layer]
            n_e = ffn_shape(layer)[0]
            sp.wait_ge(x_upd, x_after(layer, False))
            for s in range(2):
                load_expert(sp, layer, 0, s)
            with sp.Fori(1, n_e // 2) as i:
                for s in range(2):
                    sp.wait_ge(f.acc, i * 32 + (16 * (s - 1) + 4))
                    load_expert(sp, layer, i, s)

        def ffn_pe(pe, layer):
            f = ffn[layer]
            n_e, nf, last_w, gated = ffn_shape(layer)
            with pe.Fori(0, n_e // 2) as i:
                for s in range(2):
                    g, u, d = wviews(layer, s)
                    pe.wait_ge(f.w[s], (i + 1) * (16 * LOADS[layer]))
                    for c in range(NCH):
                        ch = i * 8 + (s * 4 + c)
                        for k in range(nf):
                            w = last_w if k == nf - 1 else P
                            bank = (s * 4 * nf + c * nf + k) % 2
                            pe.wait_ge(f.hid, i * (8 * nf) + ((s * 4 + c) * nf + k + 1))
                            for wv, base in ((g, 0), (u, 2)):
                                if wv is None:
                                    continue
                                for kc in range(DC):
                                    mm = pe.matmul(psum[0:w, base + bank, :], wv[:, kc, k * P:k * P + w],
                                                   HT[:, kc, c * CH:(c + 1) * CH], start=(kc == 0), stop=(kc == DC - 1))
                            mm.then_inc(f.up, 1)
                        for tt in range(TPC):
                            pe.wait_ge(f.acc, ch * 4 + (tt + 1))
                            for k in range(nf):
                                if tt == 0:
                                    pe.wait_ge(f.hid, i * (8 * nf) + ((s * 4 + c) * nf + k + 3))
                                w = last_w if k == nf - 1 else P
                                mm = pe.matmul(psum[:, 4 + tt, 0:D],
                                               hid[0:w, c % 2, k, tt * P:(tt + 1) * P], d[0:w, k, :],
                                               start=(k == 0), stop=(k == nf - 1))
                            mm.then_inc(f.down, 1)

        def ffn_act(act, layer):
            f = ffn[layer]
            n_e, nf, last_w, gated = ffn_shape(layer)
            with act.Fori(0, n_e // 2) as i:
                for s in range(2):
                    if layer == 2:
                        act.wait_ge(f.w[s], (i + 1) * (16 * LOADS[layer]))
                    for c in range(NCH):
                        if layer == 2:
                            act.wait_ge(f.down, i * 32 + 4 * (s * 4 + c) + 4)
                        for k in range(nf):
                            w = last_w if k == nf - 1 else P
                            n = (s * 4 + c) * nf + k
                            act.wait_ge(f.up, i * (8 * nf) + (n + 1))
                            if layer == 2:
                                act.activation(hid[:, c % 2, k, :], psum[:, n % 2, :], ACT.Relu,
                                               bias=b1c[:, s, k:k + 1]).then_inc(f.hid, 1)
                            else:
                                act.wait_ge(f.hid, i * (8 * nf) + (n + 1))
                                act.activation(sg[0:w, n % 2, :], psum[0:w, n % 2, :],
                                               ACT.Silu if layer == 1 else ACT.Gelu).then_inc(f.act, 1)

        def ffn_dve(dve, layer):
            f = ffn[layer]
            n_e, nf, last_w, gated = ffn_shape(layer)
            dve.wait_ge(f.init, 1)
            with dve.Fori(0, n_e // 2) as i:
                for s in range(2):
                    if layer == 2:
                        dve.wait_ge(f.w[s], (i + 1) * (16 * LOADS[layer]))
                    for c in range(NCH):
                        if gated:
                            dve.wait_ge(f.down, i * 32 + 4 * (s * 4 + c) + 4)
                            for k in range(nf):
                                w = last_w if k == nf - 1 else P
                                n = (s * 4 + c) * nf + k
                                dve.wait_ge(f.act, i * (8 * nf) + (n + 1))
                                dve.tensor_tensor(hid[0:w, c % 2, k, :], sg[0:w, n % 2, :], psum[0:w, 2 + n % 2, :],
                                                  ALU.mult).then_inc(f.hid, 1)
                        for tt in range(TPC):
                            t = c * TPC + tt
                            dve.wait_ge(f.down, i * 32 + (4 * (s * 4 + c) + tt + 9))
                            y = psum[:, 4 + tt, 0:D]
                            if layer == 2:
                                dve.tensor_tensor(dtmp[:, tt % 2, :], y, b2bc[:, s, :], ALU.add).then_inc(f.tmp, 1)
                                dve.wait_ge(f.tmp, i * 32 + (4 * (s * 4 + c) + tt + 1))
                                y = dtmp[:, tt % 2, :]
                            dve.scalar_tensor_tensor(out=ACC[:, t, :], in0=y, scalar=wts_at(i, s, t), in1=ACC[:, t, :],
                                                     op0=ALU.mult, op1=ALU.add).then_inc(f.acc, 1)
            dve.wait_ge(f.acc, 16 * n_e + 4)

        def wts_at(i, s, t):
            return wts[:, bass.ds(i * 2 + s, 1), t]

        def xadd_all(dve, n, src, gate, per):
            for g in range(n):
                t = slice(g * per, (g + 1) * per)
                dve.scalar_tensor_tensor(out=X[:, t, :], in0=src[:, t, :], scalar=tg[:, gate:gate + 1], in1=X[:, t, :],
                                         op0=ALU.mult, op1=ALU.add).then_inc(x_upd, 1)

        def affine_dve(dve, src, g, b):
            for i, (vec, op) in enumerate(((g, ALU.mult), (b, ALU.add))):
                for q in range(4):
                    t = slice(4 * q, 4 * q + 4)
                    ins = dve.tensor_tensor(src[:, t, :], src[:, t, :], vec.unsqueeze(1).broadcast_to([P, 4, D]), op)
                steps[0] += 1
                ins.then_inc(chain, 1)
                dve.wait_ge(chain, steps[0])

        def tn(layer, ff):
            return {(0, False): 1, (1, False): 2, (1, True): 3, (2, False): 4, (2, True): 5, (3, False): 6, (3, True): 7}[
                (layer, ff)]
        ST = {(0, False): 0, (0, True): 1, (1, False): 3, (1, True): 4, (2, False): 5, (2, True): 7, (3, False): 8,
              (3, True): 9}

        rt_in, rt_out = sem("rt_in"), sem("rt_out")
        mask1 = sem("mask1")
        SUB = [(l, ff) for l in range(4) for ff in (False, True)][:stop_after]
        N_SMALL = 17
        N_CONST = 20

        def att_weights(sp, layer):
            for w in range(4):
                dst = Wo[:, :, :] if w == 3 else Wsm[:, w, :, :]
                sp.dma_start(dst, a[f"w{layer}"][w].rearrange("(c p) n -> p c n", p=P)).then_inc(ld_att[layer], 16)
            if layer == 1:
                sp.dma_start(bv1, a["bv1"].partition_broadcast(P)).then_inc(ld_att[1], 16)
            else:
                sp.dma_start(biasL[:, :, :], a["fside"].rearrange("(t p) k -> p t k", p=P)).then_inc(ld_att[3], 16)

        @block.sync
        def _(sp):
            xv = a["x"].rearrange("(t p) d -> p t d", p=P)
            sp.dma_start(Va[:, :, :], a["ctx"].rearrange("(t p) d -> p t d", p=P)).then_inc(ld_ctx, 16)
            sp.dma_start(X[:, :, :], xv).then_inc(ld_x, 16)
            small = [(mask8[:, 0:TOK], a["mask"].partition_broadcast(P)), (qm8[:, :], a["maskT"]),
                     (graw[:, :], a["gates"].partition_broadcast(P)),
                     (lng, a["ln_g0"].partition_broadcast(P)), (lnb, a["ln_b0"].partition_broadcast(P)),
                     (bo_bc[:, 0, :], a["bo1"].partition_broadcast(P)), (bo_bc[:, 1, :], a["bo2"].partition_broadcast(P)),
                     (bo_bc[:, 2, :], a["bo3"].partition_broadcast(P)),
                     (rbias[:, 0, 0:7], a["rbias"].partition_broadcast(P)),
                     (rbias[:, 1, 0:4], a["gate_b"].partition_broadcast(P)),
                     (wr[:, 0, :, 0:7], a["wr1"].rearrange("(c p) e -> p c e", p=P)),
                     (wr[:, 1, :, 0:4], a["wr2"].rearrange("(c p) e -> p c e", p=P)),
                     (wr[:, 2, :, 0:8], a["wr3"].rearrange("(c p) e -> p c e", p=P)),
                     (bqk[:, 0, :], a["bq2"]), (bqk[:, 1, :], a["bk2"]), (bq3[:, :], a["bq3"]), (smul[:, :], a["smul"])]
            assert len(small) == N_SMALL
            for dst, src in small:
                sp.dma_start(dst, src).then_inc(ld_small, 16)

            for layer, ff in SUB:
                if ff and layer:
                    ffn_loads(sp, layer)
                elif ff:
                    sp.wait_ge(x_upd, x_after(0, False))
                    att_weights(sp, 1)
                elif layer == 2:
                    sp.wait_ge(x_upd, x_after(1, True))
                    for w in range(3):
                        sp.dma_start(Wqkv[:, w, :, :], a["w2"][w].rearrange("(c p) n -> p c n", p=P)
                                     ).then_inc(ld_att[2], 16)
                    sp.dma_start(Wo2[:, :, :], a["wo2"].rearrange("(c p) n -> p c n", p=P)).then_inc(ld_att[2], 16)
                    for dst, name in ((bv2, "bv2"), (lng2, "ln_g2"), (lnb2, "ln_b2")):
                        sp.dma_start(dst, a[name].partition_broadcast(P)).then_inc(ld_att[2], 16)
                else:
                    if layer == 3:
                        sp.wait_ge(x_upd, x_after(2, True))
                        att_weights(sp, 3)
                    sp.wait_ge(zeroed, {0: 3, 1: 7, 3: 11}[layer])
                    if layer == 0:
                        for c in range(DC):
                            sp.wait_ge(tpe_done[c], 4 * tn(0, False) + 4)
                    else:
                        for bk in range(2):
                            sp.wait_ge(pj_ev[bk], N_PJ * (1 if layer == 1 else 2))
                    if layer == 3:
                        sp.wait_ge(l2_sc, 16)
                    att_sp(sp, layer)
            sp.wait_ge(x_upd, x_after(*SUB[-1]))
            sp.dma_start(out.rearrange("(t p) d -> p t d", p=P), X[:, :, :]).then_inc(out_done, 16)
            sp.wait_ge(out_done, 16)

        @block.gpsimd
        def _(pool):
            n = [0]

            def step(ins, wait=True):
                n[0] += 1
                ins.then_inc(consts, 1)
                if wait:
                    pool.wait_ge(consts, n[0])
            pool.memset(ident[:, :], 0.0).then_inc(consts, 1)
            pool.memset(ones[:, :], 1.0).then_inc(consts, 1)
            pool.memset(tril[:, :], 1.0).then_inc(consts, 1)
            pool.memset(headsum[:, :], 1.0).then_inc(consts, 1)
            pool.memset(causal0[:, :, :], -NEG_BIAS).then_inc(consts, 1)
            n[0] = 5
            for e in range(WE):
                step(pool.memset(rev[:, :, e], float(WE - e)), wait=False)
            step(pool.memset(eps[:, :], EPS))
            step(pool.affine_select(out=ident[:, :], in_=ident[:, :], compare_op=ALU.not_equal, fill=1.0, base=0,
                                    pattern=[[-1, P]], channel_multiplier=1))
            step(pool.affine_select(out=tril[:, :], in_=tril[:, :], compare_op=ALU.is_ge, fill=0.0, base=0,
                                    pattern=[[1, P]], channel_multiplier=-1))
            hs = headsum[:, :].rearrange("p (b w) -> p b w", w=16)
            step(pool.affine_select(out=hs, in_=hs, compare_op=ALU.is_ge, fill=0.0, base=0,
                                    pattern=[[-16, 8], [0, 16]], channel_multiplier=1))
            step(pool.affine_select(out=hs, in_=hs, compare_op=ALU.is_ge, fill=0.0, base=15,
                                    pattern=[[16, 8], [0, 16]], channel_multiplier=-1))
            for qt in range(TPB):
                step(pool.affine_select(out=causal0[:, qt, :], in_=causal0[:, qt, :], compare_op=ALU.is_ge, fill=0.0,
                                        base=P * qt, pattern=[[-1, SEQ]], channel_multiplier=1))
            assert n[0] == N_CONST

            for layer, ff in SUB:
                if not ff:
                    if layer == 2:
                        pool.wait_ge(x_upd, x_after(1, True))
                        pool.memset(K2[:, :, :, :], 0.0).then_inc(zeroed, 1)
                        att2_pool(pool)
                        continue
                    if layer:
                        pool.wait_ge(x_upd, x_after(layer - 1, True))
                    pool.memset(Kpad[:, 0], 0.0).then_inc(zeroed, 1)
                    pool.memset(Kpad[:, 1], 0.0).then_inc(zeroed, 1)
                    pool.memset(Vpad[:, :, :, :], 0.0).then_inc(zeroed, 1)
                    if layer == 1:
                        pool.memset(biasL[:, :, :], 0.0).then_inc(zeroed, 1)
                        pool.wait_ge(zeroed, 7)
                        for qt in range(TPB):
                            ins = pool.affine_select(out=biasL[:, qt, :], in_=biasL[:, qt, :], compare_op=ALU.is_ge,
                                                     fill=MASKED, base=P * qt - 1, pattern=[[-1, SEQ]],
                                                     channel_multiplier=1)
                            ins.then_inc(mask1, 1)
                        pool.wait_ge(mask1, 2)
                        pool.memset(biasL[0:1, 0, 0:1], 0.0).then_inc(mask1, 1)
                    if layer == 0:
                        pool.wait_ge(ld_ctx, 16)
                    else:
                        if layer == 3:
                            l2norm_pool(pool)
                        for bk in range(2):
                            pool.wait_ge(pj_ev[bk], N_PJ * (1 if layer == 1 else 2))
                    pool.wait_ge(zeroed, {0: 3, 1: 7, 3: 11}[layer])
                    att_pool(pool, layer)
                elif layer:
                    pool.wait_ge(x_upd, x_after(layer, False))
                    pool.memset(ACC[:, :, :], 0.0).then_inc(ffn[layer].init, 1)

        @block.tensor
        def _(pe):
            pe.wait_ge(consts, N_CONST)
            for n in range(4):
                pe.sem_inc(att[n].s, 1)
                pe.sem_inc(att[n].t, PS)
                pe.sem_inc(att[n].av, 2)
            for n in range(1, 4):
                pe.sem_inc(ffn[n].down, 8)
            pe.wait_ge(ld_ctx, 16)
            transposes_pe(pe, 0, Va, lambda g: None)
            for layer, ff in SUB:
                if (layer, ff) != (0, True):
                    m = ST[(layer, ff)]
                    transposes_pe(pe, tn(layer, ff), Hn, lambda g: pe.wait_ge(h_done, TT * m + 4 * g + 4))
                if not ff:
                    if layer in (1, 3):
                        proj_pe(pe, layer)
                    if layer == 3:
                        l2norm_pe(pe)
                    if layer == 2:
                        pe.wait_ge(ld_att[2], 16 * 7)
                        for c in range(DC):
                            pe.wait_ge(tpe_done[c], 4 * tn(2, False) + 4)
                    (att2_pe if layer == 2 else att_pe)(pe, layer)
                elif layer:
                    logits_pe(pe, layer, {1: 7, 2: 4, 3: 8}[layer])
                    if layer == 3:
                        ranks_pe(pe)
                    ffn_pe(pe, layer)

        @block.scalar
        def _(act):
            for n in range(4):
                act.sem_inc(att[n].p, PS)
            act.wait_ge(ld_small, 16 * N_SMALL)
            act.activation(tg[:, :], graw[:, :], ACT.Tanh).then_inc(tg_done, 1)
            act.mul(bq8[:, :], bqk[:, 0, :], 0.125).then_inc(tg_done, 1)
            act.wait_ge(sm_x, 1)
            act.activation(smul[:, :], smul[:, :], ACT.Exp).then_inc(sm_x, 1)
            act.wait_ge(tg_done, 2)
            transposes_copy_act(act, 0, CT)
            for layer, ff in SUB:
                norm_sqrt(act, ST[(layer, ff)])
                if (layer, ff) == (0, True):
                    norm_sqrt(act, 2)
                else:
                    transposes_copy_act(act, tn(layer, ff), HT, 0.25 if (layer, ff) == (0, False) else 1.0)
                if not ff:
                    if layer in (1, 3):
                        proj_copy(layer, act=act)
                    if layer == 3:
                        l2norm_act(act)
                    if layer == 2:
                        act.wait_ge(zeroed, 8)
                    (att2_act if layer == 2 else att_act)(act, layer)
                    if layer == 2:
                        norm_sqrt(act, 6)
                elif layer:
                    routing_act(act, layer)
                    ffn_act(act, layer)

        @block.vector
        def _(dve):
            for n in range(4):
                dve.sem_inc(att[n].sm, 4)
                dve.sem_inc(att[n].pt, 2)
                dve.sem_inc(att[n].on, 1 if n != 2 else 2)
                dve.sem_inc(att[n].fin, 1)
            for bk in range(2):
                dve.sem_inc(me[bk], 1)
            for n in range(1, 4):
                dve.sem_inc(ffn[n].hid, 2)
                dve.sem_inc(ffn[n].acc, 4)
            dve.wait_ge(consts, N_CONST)
            dve.wait_ge(ld_small, 16 * N_SMALL)
            dve.tensor_scalar(smul[:, :], smul[:, :], LOG_MAX_SCALE, None, ALU.min).then_inc(sm_x, 1)
            dve.tensor_copy(maskf, mask8[:, 0:TOK])
            dve.tensor_copy(qm[:, :], qm8[:, :]).then_inc(dve_consts, 1)
            dve.wait_ge(dve_consts, 1)
            transposes_copy_dve(dve, 0, CT)
            for layer, ff in SUB:
                m = ST[(layer, ff)]
                ready = (ld_x, 16) if m == 0 else (x_upd, x_after(*[(l, q) for l in range(4) for q in (False, True)][
                    2 * layer + int(ff) - 1]))
                norm_stats(dve, m, X, ready)
                norm_apply(dve, m, X, Hn)
                if (layer, ff) == (0, True):
                    norm_stats(dve, 2, Hn, (h_done, TT * 2))
                    norm_apply(dve, 2, Hn, ACC)
                    dve.wait_ge(h_done, TT * 3)
                    affine_dve(dve, ACC, lng, lnb)
                    xadd_all(dve, 4, ACC, 4, 4)
                    continue
                transposes_copy_dve(dve, tn(layer, ff), HT, 0.25 if (layer, ff) == (0, False) else 1.0)
                if not ff:
                    if layer == 0:
                        dve.wait_ge(tg_done, 2)
                    if layer in (1, 3):
                        proj_copy(layer, dve=dve)
                        for bk in range(2):
                            dve.wait_ge(pj_ev[bk], N_PJ * (1 if layer == 1 else 2))
                    if layer == 1:
                        dve.wait_ge(mask1, 3)
                    if layer == 3:
                        l2norm_dve(dve)
                    if layer == 2:
                        dve.wait_ge(ld_att[2], 16 * 7)
                        dve.wait_ge(zeroed, 8)
                    (att2_dve if layer == 2 else att_dve)(dve, layer)
                    if layer == 2:
                        norm_stats(dve, 6, ACC, (att[2].fin, BATCH + 1))
                        norm_apply(dve, 6, ACC, ACC)
                        dve.wait_ge(h_done, TT * 7)
                        affine_dve(dve, ACC, lng2, lnb2)
                        xadd_all(dve, 8, ACC, 2, 2)
                else:
                    routing_dve(dve, layer, {1: 7, 2: 4, 3: 8}[layer], {1: 1, 2: 2, 3: 0}[layer])
                    ffn_dve(dve, layer)
                    xadd_all(dve, 4, ACC, 4 + layer, 4)


def arrays_of(i):
    import numpy as np

    def rows(x, p=128):
        return np.ascontiguousarray(np.asarray(x).reshape(-1, p).T)

    def join(*xs):
        return np.ascontiguousarray(np.concatenate([np.asarray(x) for x in xs], 0))

    def stack(*xs):
        return np.ascontiguousarray(np.stack([np.asarray(x) for x in xs], 0))

    g = {k: np.asarray(v) for k, v in i.items()}
    mask = g["mask_BxS2_bf1"].view(np.uint8).reshape(-1)
    f2b1 = join(g["L2_ffn_sb1"], g["L2_ffn_rb1"])
    return {
        "x": g["x"].reshape(2048, 256), "ctx": g["ctx_1024"].reshape(2048, 256), "fside": g["fside_SxS2_0"],
        "mask": np.ascontiguousarray(mask), "maskT": rows(mask),
        "gates": join(g["g_xattn"], g["g_ffn"]), "ln_g0": g["L0_ffn_ln_g"], "ln_b0": g["L0_ffn_ln_b"],
        "w1": stack(g["L1_xattn_Wq"].T, g["L1_xattn_Wk"].T, g["L1_xattn_Wv"].T, g["L1_xattn_Wo"].T),
        "bv1": g["L1_xattn_bv"], "bo1": g["L1_xattn_bo"],
        "f1g": join(g["L1_ffn_shared_gate"][None], g["L1_ffn_routed_gate"]),
        "f1u": join(g["L1_ffn_shared_up"][None], g["L1_ffn_routed_up"]),
        "f1d": join(g["L1_ffn_shared_down"][None], g["L1_ffn_routed_down"]),
        "wr1": g["L1_ffn_Wr"], "rbias": g["L1_ffn_routing_bias"],
        "w2": stack(g["L2_xattn_Wq"], g["L2_xattn_Wk"], g["L2_xattn_Wv"]), "wo2": g["L2_xattn_Wo"],
        "bq2": rows(g["L2_xattn_bq"]), "bk2": rows(g["L2_xattn_bk"]), "bv2": g["L2_xattn_bv"], "bo2": g["L2_xattn_bo"],
        "ln_g2": g["L2_xattn_ln_gamma"], "ln_b2": g["L2_xattn_ln_beta"],
        "wr2": g["L2_ffn_gate_w"], "gate_b": g["L2_ffn_gate_b"],
        "f2w1": join(g["L2_ffn_sw1"], g["L2_ffn_rw1"]), "f2w2": join(g["L2_ffn_sw2"], g["L2_ffn_rw2"]),
        "f2b1": np.ascontiguousarray(f2b1.reshape(6, 8, 128).transpose(0, 2, 1)),
        "f2b2": join(g["L2_ffn_sb2"], g["L2_ffn_rb2"]),
        "w3": stack(g["L3_xattn_Wq"], g["L3_xattn_Wk"], g["L3_xattn_Wv"], g["L3_xattn_Wo"]),
        "bq3": rows(g["L3_xattn_bq"]), "bo3": g["L3_xattn_bo"],
        "smul": rows(np.repeat(g["L3_xattn_scale_mul_log"].reshape(16), 16)),
        "wr3": np.ascontiguousarray(g["L3_ffn_Wg"].T), "f3w1": g["L3_ffn_W1"], "f3w2": g["L3_ffn_W2"],
    }


def kernel(**inputs):
    import numpy as _np
    import concourse.bacc as _bacc
    from concourse import mybir as _mybir
    from concourse.bass_utils import run_bass_kernel_spmd as _run

    nc = _bacc.Bacc("TRN2", target_bir_lowering=False, num_devices=1)
    arrays, args = {}, {}
    for name, arr in arrays_of(inputs).items():
        arr = _np.ascontiguousarray(arr)
        arrays[f"in_{name}"] = arr
        args[name] = nc.dram_tensor(f"in_{name}", arr.shape, _mybir.dt.from_np(arr.dtype), kind="ExternalInput").ap()
    out = nc.dram_tensor("out_x", (TOK, D), F32, kind="ExternalOutput").ap()
    build(nc, args, out)
    r = _run(nc, [arrays], core_ids=[0])
    return r.results[0]["out_x"].reshape(BATCH, SEQ, D)
```

```python
from contextlib import ExitStack

import concourse.bass as bass
from concourse import mybir

F32 = mybir.dt.float32
U8 = mybir.dt.uint8
U32 = mybir.dt.uint32
BF16 = mybir.dt.bfloat16
ALU = mybir.AluOpType
ACT = mybir.ActivationFunctionType
AX = mybir.AxisListType

P = 128
BATCH, SEQ, D = 8, 256, 256
TOK = BATCH * SEQ
TT = TOK // P
TPB = SEQ // P
DC = D // P
CH = 512
NCH = TOK // CH
TPC = CH // P
NH = 16
WE = 8
NEG_BIAS = 999999.0
MASKED = -1.0e30
BIG = 1.0e30
EPS = 1e-5
NORM_EPS2 = 1e-24
LOG_MAX_SCALE = 4.605170185988092
RS = 4
PS = 4
TS = 8
T_LAG = 3
FIN_AT = T_LAG + 6
T_LAG2 = 2
PARTS = 3
KR = 6 * 16
QUAD = 4

F1, F1_LAST = 6, 64
F2 = 8
F3 = 4
SHARED = {1: 1, 2: 2, 3: 0}
ROUTED = {1: 7, 2: 4, 3: 8}
TOPK = 2
CAP = int(TOK * TOPK * 1.25 / ROUTED[3])
GT = 256
GTT = GT // P
TILES = {n: (TOPK * TOK + e * (GT - 1)) // GT for n, e in ROUTED.items()}
MAXT = max(TILES.values())
WROW = {1: 2 * DC * 704 + F1 * D, 2: DC * 1024 + F2 * D + F2 + D, 3: DC * 1024 + F3 * D}
SKIP = 1.0e6


def build(nc, a, out, stop_after=8):
    with ExitStack() as ctx:
        def sb(name, shape, dt=F32):
            return ctx.enter_context(nc.sbuf_tensor(name, shape, dt))

        def sem(name):
            return ctx.enter_context(nc.semaphore(name))

        X = sb("X", [P, TT, D])
        Hn = sb("Hn", [P, TT, D])
        HT = sb("HT", [P, DC, TOK])
        HTf = HT[:, :, :].rearrange("p c t -> p (c t)")
        CT = sb("CT", [P, DC, TOK])
        ACC = sb("ACC", [P, TT, D])
        arena = sb("arena", [P, 20480])
        ident = sb("ident", [P, P])
        ones = sb("ones", [P, P])
        tril = sb("tril", [P, P])
        headsel = sb("headsel", [P, 32])
        rev = sb("rev", [P, TT, WE])
        eps = sb("eps", [P, 1])
        causal0 = sb("causal0", [P, TPB, SEQ])
        biasL = sb("biasL", [P, TPB, SEQ])
        bo_bc = sb("bo_bc", [P, 3, D])
        graw = sb("graw", [P, 8])
        tg = sb("tg", [P, 8])
        lnst = sb("lnst", [P, TT, 6])
        lnmv = sb("lnmv", [P, TT, 2])
        lnsd = sb("lnsd", [P, TT])
        lnrs = sb("lnrs", [P, TT])
        lnnb = sb("lnnb", [P, TT])
        qm8 = sb("qm8", [P, TT], U8)
        qm = sb("qm", [P, TT])
        Ssb = sb("Ssb", [P, RS, TPB, SEQ])
        Pb = sb("Pb", [P, PS, TPB, SEQ])
        PTb = sb("PTb", [P, TS, TPB, SEQ])
        nmax = sb("nmax", [P, PS, TPB])
        rsum = sb("rsum", [P, BATCH, TPB, NH])
        rrec = sb("rrec", [P, TPB, NH])
        xtmp = sb("xtmp", [P, TPB, D])
        wr = sb("wr", [P, 3, DC, WE])
        rbias = sb("rbias", [P, 2, WE])
        r1 = sb("r1", [P, 4, TT])
        tileno = sb("tileno", [P, MAXT + 1])
        nrow = sb("nrow", [P, 1])
        bqk = sb("bqk", [P, 2, 8])
        bq8 = sb("bq8", [P, 8])
        bq3 = sb("bq3", [P, DC])
        smul = sb("smul", [P, DC])
        psum = ctx.enter_context(nc.psum_tensor("psum", [P, 8, 512], F32))

        Pf = Pb[:, :, :, :].rearrange("p s t k -> p (s t k)")
        rt = Pf[:, 0:4 * TT * WE].rearrange("p (i t e) -> p i t e", i=4, t=TT)
        lg, oh1, oh2, slot_f = (Pf[:, (4 + i) * TT * WE:(5 + i) * TT * WE].rearrange("p (t e) -> p t e", t=TT)
                                for i in range(4))
        pfxa, pfxb = (Pf[:, 1024 + 136 * i:1160 + 136 * i].rearrange("p (t e) -> p t e", e=WE) for i in range(2))
        rank = Pf[:, 1296:1432].rearrange("p (t e) -> p t e", e=WE)
        cmp_t = Pf[:, 1432:1496].rearrange("p (e k) -> p e k", e=WE)
        cmp_w = Pf[:, 1496:1496 + MAXT * WE].rearrange("p (w e) -> p w e", e=WE)
        small8 = Pf[:, 1700:1732].rearrange("p (i e) -> p i e", i=4)
        tile_f = Pf[:, 1732:1732 + MAXT]
        tok_f = Pf[:, 1760:1824].rearrange("p (i t) -> p i t", i=4)
        gate2 = Pf[:, 1824:1856].rearrange("p (i t) -> p i t", i=2)
        s_idx = Pf[:, 1856:1888].bitcast(U32).rearrange("p (i t) -> p i t", i=2)
        g_idx = Pf[:, 1888:1920].bitcast(U32).rearrange("p (i t) -> p i t", i=2)
        w_idx = Pf[:, 1920:1920 + MAXT].bitcast(U32)
        w_now = Pf[:, 1948:1950].bitcast(U32)

        KTa = arena[:, 0:4096].rearrange("p (c t) -> p c t", c=DC)
        Va = arena[:, 4096:8192].rearrange("p (t d) -> p t d", t=TT)
        QK = arena[:, 8192:16384].bitcast(BF16).rearrange("p (r w h t) -> p r w h t", r=2, w=2, h=NH)
        Vpad = arena[:, 16384:17408].rearrange("p (k h w) -> p k h w", k=TPB, h=NH)
        OTs = arena[:, 17408:17920].rearrange("p (c t) -> p c t", c=DC)
        Rsb = arena[:, 17920:18432].rearrange("p (c t) -> p c t", c=DC)
        Wo = arena[:, 18432:18944].rearrange("p (c n) -> p c n", c=DC)
        bv1 = arena[:, 18944:19200]
        lng = arena[:, 19200:19456]
        lnb = arena[:, 19456:19712]
        def split_bufs(layer):
            f = arena if layer == 0 else HTf
            return (f[:, 0:1536].bitcast(BF16).rearrange("p (w i c t) -> p w i c t", w=2, i=PARTS, c=DC),
                    f[:, 1536:2560].rearrange("p (w c t) -> p w c t", w=2, c=DC))
        QTa = Hn[:, :, :].rearrange("p t d -> p (t d)").rearrange("p (c t) -> p c t", c=DC)
        Wsm = PTb[:, 0:3, :, :]
        mask8 = HTf[:, 0:512].bitcast(U8)
        maskf = ACC[:, :, :].rearrange("p t d -> p (t d)")[:, 0:TOK]
        Wqkv = arena[:, 0:6144].rearrange("p (w c n) -> p w c n", w=3, c=DC)
        Wo2 = arena[:, 6144:8192].rearrange("p (c n) -> p c n", c=8)
        Q2 = arena[:, 8192:10240].rearrange("p (m t) -> p m t", m=8)
        K2 = arena[:, 10240:14336].rearrange("p (r m t) -> p r m t", r=2, m=8)
        V2 = arena[:, 14336:16384].rearrange("p (t n) -> p t n", t=TPB)
        OT2 = arena[:, 16384:18432].rearrange("p (m t) -> p m t", m=8)
        Rsb2 = arena[:, 18432:18944].rearrange("p (c t) -> p c t", c=DC)
        CTb = arena[:, 18944:19456].rearrange("p (c t) -> p c t", c=DC)
        bv2 = arena[:, 19456:20480]
        lng2 = biasL[:, 0, :]
        lnb2 = biasL[:, 1, :]
        WS = 4368
        wslot = [arena[:, s * WS:(s + 1) * WS] for s in range(2)]
        hid = arena[:, 2 * WS:2 * WS + 8192].rearrange("p (s f t) -> p s f t", s=2, f=8)
        sg = arena[:, 2 * WS + 8192:2 * WS + 9216].rearrange("p (s t) -> p s t", s=2)
        dtmp = arena[:, 2 * WS + 9216:2 * WS + 9728].rearrange("p (s d) -> p s d", s=2)
        XG = arena[:, 2 * WS + 9728:2 * WS + 10752].rearrange("p (s t d) -> p s t d", s=2, t=GTT)
        hidT = arena[:, 2 * WS:2 * WS + F2 * GT].rearrange("p (f t) -> p f t", f=F2)
        XT = arena[:, 2 * WS + 4096:2 * WS + 5120].rearrange("p (s c t) -> p s c t", s=2, c=DC)
        YO = arena[:, 2 * WS + 5120:2 * WS + 6144].rearrange("p (s t d) -> p s t d", s=2, t=GTT)
        YG = arena[:, 2 * WS + 6144:2 * WS + 8192].rearrange("p (s k d) -> p s k d", s=4, k=TOPK)
        zeros = Wo.rearrange("p c n -> p (c n)")[:, 0:D]
        xrows = nc.dram_tensor("xrows", (MAXT * GT, D), F32).ap()
        yrows = nc.dram_tensor("yrows", (MAXT * GT, D), F32).ap()
        parts = nc.dram_tensor("parts", (2, 2 * PARTS, 8, 16, DC * SEQ), BF16).ap()

        ld_x, ld_ctx, ld_small = sem("ld_x"), sem("ld_ctx"), sem("ld_small")
        ld_att = [sem(f"ld_att{i}") for i in range(4)]
        ld_wo = sem("ld_wo")
        consts, dve_consts = sem("consts"), sem("dve_consts")
        tg_done = sem("tg_done")
        st_done, ag_done, sd_done, rs_done = (sem(n) for n in ("st_done", "ag_done", "sd_done", "rs_done"))
        h_done, ha_done = sem("h_done"), sem("ha_done")
        tp_done = [sem("tp_done0"), sem("tp_done1")]
        tpe_done = [sem("tpe_done0"), sem("tpe_done1")]
        x_upd = sem("x_upd")
        chain = sem("chain")
        pj_mm = [sem("pj_mm0"), sem("pj_mm1")]
        pj_ev = [sem("pj_ev0"), sem("pj_ev1")]
        out_done = sem("out_done")

        class AttSems:
            def __init__(s, n):
                s.s, s.sm, s.p, s.t, s.pt, s.av, s.v, s.rr, s.rx, s.on, s.fin = (
                    sem(f"a{n}_{w}") for w in ("scores", "max", "probs", "ptrans", "pcopy", "pv", "values", "rsum",
                                               "widened", "onorm", "fin"))
                if n != 2:
                    s.r, s.rc, s.wo = (sem(f"a{n}_{w}") for w in ("spread", "spreadcopy", "wo"))
                s.ch = sem("a0_chain") if n == 0 else None
        att = [AttSems(n) for n in range(4)]
        split_done, parts_out, qk_rows = sem("split_done"), sem("parts_out"), [sem("qk_rows0"), sem("qk_rows1")]
        act_copied = sem("act_copied")
        nth = {0: 0, 1: 1, 3: 2}
        l2_filled = [sem("l2_filled6"), sem("l2_filled7")]
        l2_emptied = [sem("l2_emptied6"), sem("l2_emptied7")]
        spread_ready = sem("spread_ready")
        gains = sem("gains")
        ln2, ln2_sd = sem("ln2"), sem("ln2_sqrt")
        zeroed = sem("zeroed")

        class FfnSems:
            def __init__(s, n):
                s.lg, s.init = sem(f"f{n}_logits"), sem(f"f{n}_init")
                if n == 3:
                    return
                s.w = [sem(f"f{n}_w{i}") for i in range(SHARED[n])]
                s.up, s.act, s.hid, s.down, s.acc = (sem(f"f{n}_{w}") for w in ("up", "act", "hid", "down", "acc"))
                s.tmp = sem(f"f{n}_tmp") if n == 2 else None
        ffn = [None] + [FfnSems(n) for n in (1, 2, 3)]

        class MoeSems:
            def __init__(s):
                s.idx, s.sc, s.wi, s.tr, s.xt, s.up, s.act, s.hid, s.down, s.y, s.cb = (
                    sem(f"moe_{w}") for w in ("index", "scattered", "wrows", "trans", "tcopy", "up", "act", "hid",
                                              "down", "y", "combined"))
                s.w = [sem("moe_w0"), sem("moe_w1")]
                s.xg = [sem("moe_xg0"), sem("moe_xg1")]
                s.ys = [sem("moe_ystored0"), sem("moe_ystored1")]
                s.g = [sem(f"moe_gathered{i}") for i in range(4)]
        moe = MoeSems()
        zrows = sem("zero_rows")
        pfx = sem("prefix")
        waited, waited_pe, waited_pool, waited_sp = sem("waited"), sem("waited_pe"), sem("waited_pool"), sem("waited_sp")

        def x_after(layer, ff):
            return 12 * layer + (12 if ff else 8)

        block = ctx.enter_context(nc.Block())

        def bs(b, n=SEQ):
            return slice(b * n, b * n + n) if isinstance(b, int) else bass.ds(b * n, n)

        def stats_tiles(dve, m, src, lo, hi):
            for t in range(lo, hi):
                dve.bn_stats(lnst[:, t, :], src[:, t, :]).then_inc(st_done, 1)
            dve.wait_ge(st_done, TT * m + hi)
            for t in range(lo, hi):
                dve.bn_aggr(lnmv[:, t, :], lnst[:, t, :]).then_inc(ag_done, 1)

        def norm_stats(dve, m, src, ready, lo=0):
            dve.wait_ge(*ready)
            if lo < TT:
                stats_tiles(dve, m, src, lo, TT)

        def norm_sqrt(act, m):
            act.wait_ge(ag_done, TT * (m + 1))
            act.activation(lnsd[:, :], lnmv[:, :, 1], ACT.Sqrt, bias=eps[:, 0:1]).then_inc(sd_done, 1)

        def norm_apply(dve, m, src, dst):
            dve.wait_ge(sd_done, m + 1)
            dve.reciprocal(lnrs[:, :], lnsd[:, :]).then_inc(rs_done, 1)
            dve.wait_ge(rs_done, 6 * m + 1)
            dve.tensor_tensor(lnsd[:, :], lnrs[:, :], lnrs[:, :], ALU.mult).then_inc(rs_done, 1)
            dve.wait_ge(rs_done, 6 * m + 2)
            dve.scalar_tensor_tensor(out=lnsd[:, :], in0=lnmv[:, :, 1], scalar=eps[:, 0:1], in1=lnsd[:, :],
                                     op0=ALU.add, op1=ALU.mult).then_inc(rs_done, 1)
            dve.wait_ge(rs_done, 6 * m + 3)
            dve.tensor_scalar(lnsd[:, :], lnsd[:, :], -0.5, 1.5, ALU.mult, ALU.add).then_inc(rs_done, 1)
            dve.wait_ge(rs_done, 6 * m + 4)
            dve.tensor_tensor(lnrs[:, :], lnrs[:, :], lnsd[:, :], ALU.mult).then_inc(rs_done, 1)
            dve.wait_ge(rs_done, 6 * m + 5)
            dve.scalar_tensor_tensor(out=lnnb[:, :], in0=lnmv[:, :, 0], scalar=-1.0, in1=lnrs[:, :], op0=ALU.mult,
                                     op1=ALU.mult).then_inc(rs_done, 1)
            for t in range(TT):
                if t % 4 < 2:
                    dve.tensor_scalar(dst[:, t, :], src[:, t, :], lnmv[:, t, 0:1], lnrs[:, t:t + 1],
                                      ALU.subtract, ALU.mult).then_inc(h_done, 1)

        def norm_apply_act(act, m, src, dst):
            act.wait_ge(rs_done, 6 * m + 6)
            for t in range(TT):
                if t % 4 >= 2:
                    act.activation(dst[:, t, :], src[:, t, :], ACT.Identity, bias=lnnb[:, t:t + 1],
                                   scale=lnrs[:, t:t + 1]).then_inc(ha_done, 1)

        def normed(eng, m, n):
            eng.wait_ge(h_done, TT // 2 * m + n // 2)
            eng.wait_ge(ha_done, TT // 2 * m + n // 2)

        def transposes_pe(pe, n, src, ready, after=None):
            for g in range(TT // 4):
                ready(g)
                for c in range(DC):
                    if n or g:
                        pe.wait_ge(tpe_done[c], 4 * n + g)
                    for j in range(4):
                        mm = pe.transpose(psum[:, c, j * P:(j + 1) * P], src[:, 4 * g + j, c * P:(c + 1) * P],
                                          ident[:, :])
                    mm.then_inc(tp_done[c], 1)
                if after and g:
                    after(g - 1)
            if after:
                after(TT // 4 - 1)

        def transposes_copy_dve(dve, n, dst, scale=1.0):
            for g in range(TT // 4):
                dve.wait_ge(tp_done[0], 4 * n + g + 1)
                dve.tensor_scalar(dst[:, 0, g * 512:(g + 1) * 512], psum[:, 0, :], scale, None,
                                  ALU.mult).then_inc(tpe_done[0], 1)

        def transposes_copy_act(act, n, dst, scale=1.0):
            for g in range(TT // 4):
                act.wait_ge(tp_done[1], 4 * n + g + 1)
                act.activation(dst[:, 1, g * 512:(g + 1) * 512], psum[:, 1, :], ACT.Copy,
                               scale=scale).then_inc(tpe_done[1], 1)

        HEADS = [8 * m + 2 * j + n for m in range(DC) for n in range(2) for j in range(QUAD)]
        ACT_COPIES = (3, 5, 7, 10, 12, 14)
        SBANK = (0, 1)

        def tbanks(layer):
            return (2, 3) if layer == 2 else (2, 3, 5, 6)

        def tbank(layer, k):
            return tbanks(layer)[k % len(tbanks(layer))]

        def split(eng, layer, b):
            sb = nth[layer] * 10 * BATCH
            S3, R = split_bufs(layer)
            src = (HT, CT) if layer == 0 else (QTa, KTa)
            if not isinstance(b, int) or b:
                eng.wait_ge(parts_out, b * 32 + nth[layer] * 32 * BATCH)
            n = 0
            if isinstance(b, int):
                sb += 10 * b
                for w in (1, 0):
                    for i in range(PARTS):
                        left = src[w][:, :, bs(b)] if i == 0 else R[:, w]
                        if i:
                            eng.wait_ge(split_done, sb + n)
                        eng.tensor_copy(S3[:, w, i], left).then_inc(split_done, 1)
                        n += 1
                        if i < PARTS - 1:
                            eng.wait_ge(split_done, sb + n)
                            eng.tensor_tensor(R[:, w], left, S3[:, w, i], ALU.subtract).then_inc(split_done, 1)
                            n += 1
                return
            for i in range(PARTS):
                for w in range(2):
                    left = src[w][:, :, bs(b)] if i == 0 else R[:, w]
                    if i:
                        eng.wait_ge(split_done, b * 10 + (sb + n - 1))
                        if not (isinstance(b, int) and b == 0):
                            eng.sem_inc(waited_pool, 1)
                    eng.tensor_copy(S3[:, w, i], left).then_inc(split_done, 1)
                    n += 1
                if i == PARTS - 1:
                    break
                for w in range(2):
                    left = src[w][:, :, bs(b)] if i == 0 else R[:, w]
                    eng.wait_ge(split_done, b * 10 + (sb + n - 1))
                    if not (isinstance(b, int) and b == 0):
                        eng.sem_inc(waited_pool, 1)
                    eng.tensor_tensor(R[:, w], left, S3[:, w, i], ALU.subtract).then_inc(split_done, 1)
                    n += 1

        def att_load_sp(sp, layer, b, r, pair, first):
            s = att[layer]
            S3, R = split_bufs(layer)
            sb = nth[layer] * 10 * BATCH
            kb, wb = nth[layer] * 192 * BATCH // 2, nth[layer] * 32 * BATCH

            def write(w):
                sp.dma_start(parts[r, PARTS * w:PARTS * w + PARTS].rearrange("i j d x -> (j d) i x"),
                             S3[:, w].rearrange("p i c t -> p i (c t)")).then_inc(parts_out, 16)

            def read(w):
                for row, (q, k) in enumerate(((0, 0), (0, 1), (0, 2), (1, 0), (1, 1), (2, 0))):
                    sp.dma_start(QK[16 * row:16 * row + 16, r, w].rearrange("d (j m) t -> d j (m t)", j=8),
                                 parts[r, PARTS * w + (k if w else q)].rearrange("j d x -> d j x")
                                 ).then_inc(qk_rows[r], 16)
            if first:
                for n, w in enumerate((1, 0)):
                    sp.wait_ge(split_done, sb + 10 * b + 5 * (n + 1))
                    if n == 0 and kb:
                        sp.wait_ge(qk_rows[r], kb)
                    write(w)
                    if n == 0:
                        sp.wait_ge(parts_out, wb + 32 * b + 16)
                read(1)
                sp.wait_ge(parts_out, wb + 32 * b + 32)
                read(0)
                return
            sp.wait_ge(split_done, b * 10 + (sb + 10))
            sp.sem_inc(waited_sp, 1)
            sp.wait_ge(qk_rows[r], pair * 192 + kb)
            for w in range(2):
                write(w)
            sp.wait_ge(parts_out, b * 32 + (wb + 32))
            sp.sem_inc(waited_sp, 1)
            sp.wait_ge(s.s, b * NH - (NH - 1))
            for w in range(2):
                read(w)

        def att_sp(sp, layer):
            for r in range(2):
                att_load_sp(sp, layer, r, r, 0, True)
            with sp.Fori(1, BATCH // 2) as i:
                for r in range(2):
                    att_load_sp(sp, layer, i * 2 + r, r, i, False)

        def values_pool(pool, layer, b):
            s = att[layer]
            pool.wait_ge(s.av, b * QUAD + 2)
            pool.sem_inc(waited_pool, 1)
            v = Va[:, bs(b, TPB), :].rearrange("p k (a w) -> p k a w", w=32)
            o = Vpad[:, :, :, :].rearrange("p k (a n) w -> p k a n w", n=2)
            bv = bv1.rearrange("p (a w) -> p a w", w=32)
            for n in range(2):
                cols = slice(16 * n, 16 * n + 16)
                for kt in range(TPB):
                    if layer == 1:
                        ins = pool.tensor_tensor(o[:, kt, :, n, cols], v[:, kt, :, cols], bv[:, :, cols], ALU.add)
                    else:
                        ins = pool.tensor_copy(o[:, kt, :, n, cols], v[:, kt, :, cols])
            ins.then_inc(s.v, 1)

        def att_pool(pool, layer):
            with pool.Fori(0, BATCH - 2) as b:
                values_pool(pool, layer, b)
                split(pool, layer, b + 2)
            for b in (BATCH - 2, BATCH - 1):
                values_pool(pool, layer, b)

        def scores_pe(pe, layer, b, k, r=0):
            s = att[layer]
            if layer == 2:
                pe.wait_ge(s.p, b * NH + k + 1 - 2 + PS)
                bank, q, kk = k % 2, Q2[:, k // 2, :], K2[:, k % 2, k // 2, :]
            else:
                pe.wait_ge(s.sm, b * NH + k + 3)
                h = HEADS[k]
                bank, q, kk = SBANK[k % 2], QK[0:KR, r, 0, h % 8 * DC + h // 8, :], QK[0:KR, r, 1, h % 8 * DC + h // 8, :]
            for qt in range(TPB):
                mm = pe.matmul(psum[:, bank, qt * SEQ:(qt + 1) * SEQ], q[:, qt * P:(qt + 1) * P], kk,
                               start=True, stop=True)
            mm.then_inc(s.s, 1)

        def max_dve(dve, layer, b, k):
            s = att[layer]
            dve.wait_ge(s.s, b * NH + k + 2)
            if layer == 2:
                dve.wait_ge(s.p, b * NH + k + 1)
                dve.tensor_reduce(nmax[:, k % PS, :], psum[:, k % 2, :].rearrange("p (q k) -> p q k", q=TPB), AX.X,
                                  ALU.max, negate=True).then_inc(s.sm, 1)
                return
            dve.wait_ge(s.p, b * NH + k + 1 - RS + PS)
            dve.sem_inc(waited, 1)
            for qt in range(TPB):
                ins = dve.tensor_tensor_reduce(Ssb[:, k % RS, qt, :], psum[:, SBANK[k % 2], qt * SEQ:(qt + 1) * SEQ],
                                               biasL[:, qt, :], -1.0, 3.0e38, ALU.add, ALU.min,
                                               nmax[:, k % PS, qt:qt + 1])
            ins.then_inc(s.sm, 1)

        def exp_act(act, layer, b, k):
            s = att[layer]
            act.wait_ge(s.sm, b * NH + k + 1 + 4)
            act.wait_ge(s.t, b * NH + k + 1)
            h = k if layer == 2 else HEADS[k]
            for qt in range(TPB):
                src, sc = (psum[:, k % 2, qt * SEQ:(qt + 1) * SEQ], 1.0) if layer == 2 else (Ssb[:, k % RS, qt, :], -1.0)
                acc = rsum[:, b, qt, h:h + 1] if isinstance(b, int) else rsum[:, bass.ds(b, 1), qt, h:h + 1]
                ins = act.activation(Pb[:, k % PS, qt, :], src, ACT.Exp, bias=nmax[:, k % PS, qt:qt + 1], scale=sc,
                                     accum_out=acc)
            ins.then_inc(s.p, 1)

        def ptrans_pe(pe, layer, b, k):
            s = att[layer]
            pe.wait_ge(s.p, b * NH + k + 1 + PS)
            copied(pe, layer, b, k - len(tbanks(layer)))
            for kt in range(TPB):
                for qt in range(TPB):
                    mm = pe.transpose(psum[:, tbank(layer, k), kt * SEQ + qt * P:kt * SEQ + (qt + 1) * P],
                                      Pb[:, k % PS, qt, kt * P:(kt + 1) * P], ident[:, :])
            mm.then_inc(s.t, 1)

        def copied(eng, layer, b, k):
            if layer == 2:
                eng.wait_ge(att[2].pt, b * NH + k + 1 + NH)
                return
            by_act = k % NH in ACT_COPIES
            n = len(ACT_COPIES) if by_act else NH - len(ACT_COPIES)
            upto = sum((j in ACT_COPIES) == by_act for j in range(k % NH + 1)) + (n if k >= 0 else 0)
            if by_act:
                eng.wait_ge(act_copied, b * n + (nth[layer] * BATCH * n + upto))
            else:
                eng.wait_ge(att[layer].pt, b * n + upto)

        def pcopy_act(act, layer, b, k):
            s = att[layer]
            act.wait_ge(s.t, b * NH + k + 1 + PS)
            act.wait_ge(s.av, b * QUAD + k // QUAD + 1)
            act.activation(PTb[:, k % TS, :, :], psum[:, tbank(layer, k), :].rearrange("p (k q) -> p k q", k=TPB), ACT.Copy
                           ).then_inc(act_copied, 1)

        def pcopy_dve(dve, layer, b, k):
            s = att[layer]
            dve.wait_ge(s.t, b * NH + k + 1 + PS)
            dve.wait_ge(s.av, b * QUAD + k // QUAD + 1)
            dve.tensor_copy(PTb[:, k % TS, :, :], psum[:, tbank(layer, k), :].rearrange("p (k q) -> p k q", k=TPB)
                            ).then_inc(s.pt, 1)

        def pv_pe(pe, layer, b, g):
            s = att[layer]
            for by_act in (False, True):
                copied(pe, layer, b, max(k for k in range(QUAD * g, QUAD * (g + 1)) if (k in ACT_COPIES) == by_act))
            if g == 0:
                pe.wait_ge(s.v, b + 1)
                pe.wait_ge(s.on, b + 1)
            m, n = g // 2, g % 2
            for kt in range(TPB):
                for j in range(QUAD):
                    k = QUAD * g + j
                    mm = pe.matmul(psum[32 * j:32 * j + 32, 4, m * SEQ:(m + 1) * SEQ], Vpad[:, kt, HEADS[k], :],
                                   PTb[:, k % TS, kt, :], start=(n == 0 and kt == 0),
                                   stop=(n == 1 and kt == TPB - 1))
            mm.then_inc(s.av, 1)

        def rsums(b, h0, n):
            if isinstance(b, int):
                return rsum[:, b, :, h0:h0 + n]
            return rsum[:, bass.ds(b, 1), :, h0:h0 + n].rearrange("p a q h -> p (a q) h")

        def recip_dve(dve, layer, b):
            s = att[layer]
            dve.wait_ge(s.p, b * NH + NH + PS)
            if layer:
                dve.reciprocal(rrec[:, :, :], rsums(b, 0, NH)).then_inc(s.rr, 1)
                return
            dve.reciprocal(rrec[:, :, :], rsums(b, 0, NH)).then_inc(s.ch, 1)
            dve.wait_ge(s.ch, b + 1)
            dve.tensor_tensor(rrec[:, :, :], rrec[:, :, :],
                              qm[:, bs(b, TPB)].unsqueeze(2).broadcast_to([P, TPB, NH]), ALU.mult).then_inc(s.rr, 1)

        def spread_pe(pe, layer, b):
            s = att[layer]
            pe.wait_ge(s.rx, b + 1)
            pe.wait_ge(s.fin, b + 1)
            for m in range(DC):
                for qt in range(TPB):
                    mm = pe.transpose(psum[:, 7, m * SEQ + qt * P:m * SEQ + (qt + 1) * P],
                                      Rsb[:, qt, m * P:(m + 1) * P], ident[:, :])
            mm.then_inc(s.r, 1)

        def widen_act(act, layer, b):
            s = att[layer]
            act.wait_ge(s.rr, b + 1)
            act.activation(Rsb[:, :, :].rearrange("p q (h w) -> p q h w", w=16),
                           rrec[:, :, :].unsqueeze(3).broadcast_to([P, TPB, NH, 16]), ACT.Copy).then_inc(s.rx, 1)

        def spread_act(act, layer, b):
            s = att[layer]
            act.wait_ge(s.r, b + 1)
            act.activation(Rsb[:, :, :], psum[:, 7, :].rearrange("p (c t) -> p c t", c=DC), ACT.Copy).then_inc(s.rc, 1)

        def onorm_dve(dve, layer, b):
            s = att[layer]
            dve.wait_ge(s.av, b * QUAD + QUAD + 2)
            dve.wait_ge(s.rc, b + 1)
            dve.tensor_tensor(OTs[:, :, :], psum[:, 4, :].rearrange("p (c t) -> p c t", c=DC), Rsb[:, :, :],
                              ALU.mult).then_inc(s.on, 1)

        def final_pe(pe, layer, b):
            s = att[layer]
            pe.wait_ge(s.on, b + 2)
            if layer:
                pe.wait_ge(ld_wo, 16 if layer == 1 else 32)
            for qt in range(TPB):
                for c in range(DC):
                    if layer:
                        mm = pe.matmul(psum[:, 7, qt * D:(qt + 1) * D], OTs[:, c, qt * P:(qt + 1) * P], Wo[:, c, :],
                                       start=(c == 0), stop=(c == DC - 1))
                    else:
                        mm = pe.transpose(psum[:, 7, qt * D + c * P:qt * D + (c + 1) * P],
                                          OTs[:, c, qt * P:(qt + 1) * P], ident[:, :])
            mm.then_inc(s.wo, 1)

        def xadd_dve(dve, layer, b):
            s = att[layer]
            xb = X[:, bs(b, TPB), :]
            dve.wait_ge(s.wo, b + 1)
            y = psum[:, 7, :].rearrange("p (q d) -> p q d", q=TPB)
            if layer:
                bo = bo_bc[:, {1: 0, 3: 2}[layer], :]
                dve.tensor_tensor(xtmp[:, :, :], y, bo.unsqueeze(1).broadcast_to([P, TPB, D]), ALU.add
                                  ).then_inc(s.fin, 1)
                dve.wait_ge(s.fin, b + 2)
                dve.scalar_tensor_tensor(out=xb, in0=xtmp[:, :, :], scalar=tg[:, layer:layer + 1], in1=xb,
                                         op0=ALU.mult, op1=ALU.add).then_inc(x_upd, 1)
            else:
                dve.scalar_tensor_tensor(out=xb, in0=y, scalar=tg[:, 0:1], in1=xb, op0=ALU.mult,
                                         op1=ALU.add).then_inc(s.fin, 1)

        def att_step_pe(pe, layer, b, pair, r, k, cur, prev):
            if cur:
                if k == 0:
                    pe.wait_ge(qk_rows[r], pair * 192 + (nth[layer] * 192 * BATCH // 2 + 192))
                scores_pe(pe, layer, b, k, r)
            if k < T_LAG:
                if prev:
                    ptrans_pe(pe, layer, b - 1, NH + k - T_LAG)
            elif cur:
                ptrans_pe(pe, layer, b, k - T_LAG)
            g = k - T_LAG - QUAD
            if g < 0:
                g += NH
            if g % QUAD == 0:
                if k >= T_LAG + QUAD:
                    if cur:
                        pv_pe(pe, layer, b, g // QUAD)
                elif prev:
                    pv_pe(pe, layer, b - 1, g // QUAD)
            if prev and k == T_LAG + 1:
                spread_pe(pe, layer, b - 1)
            if prev and k == FIN_AT:
                final_pe(pe, layer, b - 1)

        def att_step_act(act, layer, b, pair, r, k, cur, prev):
            if k < T_LAG:
                if prev and NH + k - T_LAG in ACT_COPIES:
                    pcopy_act(act, layer, b - 1, NH + k - T_LAG)
            elif cur and k - T_LAG in ACT_COPIES:
                pcopy_act(act, layer, b, k - T_LAG)
            if cur:
                exp_act(act, layer, b, k)
            if prev and k == T_LAG - 1:
                widen_act(act, layer, b - 1)
            if prev and k == T_LAG + 1:
                spread_act(act, layer, b - 1)

        def att_step_dve(dve, layer, b, pair, r, k, cur, prev):
            if cur:
                if layer == 0 and k == 0:
                    dve.wait_ge(att[0].sm, b * NH + 4)
                    for qt in range(TPB):
                        ins = dve.tensor_tensor(biasL[:, qt, :], causal0[:, qt, :], maskf[:, bs(b)], ALU.mult)
                    ins.then_inc(own_bias, 1)
                    dve.wait_ge(own_bias, b + 1)
                max_dve(dve, layer, b, k)
            if k < T_LAG:
                if prev:
                    if NH + k - T_LAG not in ACT_COPIES:
                        pcopy_dve(dve, layer, b - 1, NH + k - T_LAG)
                    if k == T_LAG - 1:
                        recip_dve(dve, layer, b - 1)
            elif cur and k - T_LAG not in ACT_COPIES:
                pcopy_dve(dve, layer, b, k - T_LAG)
            if prev and k == T_LAG + 2:
                onorm_dve(dve, layer, b - 1)
            if prev and k == FIN_AT + 1:
                xadd_dve(dve, layer, b - 1)

        own_bias = sem("bias0")

        def att_loop(eng, layer, step, last=FIN_AT + 2, eng_stats=False):
            for r in range(2):
                for k in range(NH):
                    step(eng, layer, r, 0, r, k, True, r > 0)
            with eng.Fori(1, BATCH // 2) as i:
                for r in range(2):
                    for k in range(NH):
                        step(eng, layer, i * 2 + r, i, r, k, True, True)
            for k in range(last):
                step(eng, layer, BATCH, 0, 0, k, False, True)
                if eng_stats and 1 <= k <= TT // TPB - 1:
                    dve = eng
                    if k == 1:
                        if layer == 0:
                            dve.wait_ge(att[0].fin, BATCH)
                        else:
                            dve.wait_ge(x_upd, 12 * layer + BATCH - 1)
                    stats_tiles(dve, ST[(layer, True)], X, TPB * (k - 1), TPB * k)

        def att_pe(pe, layer):
            att_loop(pe, layer, att_step_pe)

        def att_act(act, layer):
            att_loop(act, layer, att_step_act)

        def att_dve(dve, layer):
            split(dve, layer, 0)
            split(dve, layer, 1)
            att_loop(dve, layer, att_step_dve, eng_stats=True)
            if layer == 0:
                dve.wait_ge(att[0].fin, BATCH + 1)
                dve.sem_inc(x_upd, BATCH)

        def proj_steps(part):
            if part == "q":
                return [("q", m, n) for m in range(DC) for n in range(NCH)]
            return [("k", m, n) for m in range(DC) for n in range(NCH)] + [("v", t, 0) for t in range(TT // 2)]

        N_KV, N_Q = len(proj_steps("kv")) // 2, len(proj_steps("q")) // 2
        N_PJ = N_KV + N_Q

        def pj_base(layer, part):
            return (0 if layer == 1 else N_PJ) + (0 if part == "kv" else N_KV)

        def proj_pe(pe, layer, part, lo=0, hi=None):
            pe.wait_ge(ld_att[layer], 16 * {1: 4, 3: 4}[layer])
            base = pj_base(layer, part)
            for i, (kind, m, n) in list(enumerate(proj_steps(part)))[lo:hi]:
                bk = i % 2
                if kind == "q" and m == 0:
                    for c in range(DC):
                        pe.wait_ge(tpe_done[c], 4 * tn(layer, False) + n + 1)
                if base + i // 2:
                    pe.wait_ge(pj_ev[bk], base + i // 2)
                bank = psum[:, 2 + bk, :]
                if kind == "v":
                    for j in range(2):
                        t = 2 * m + j
                        for c in range(DC):
                            mm = pe.matmul(bank[:, j * D:(j + 1) * D], CT[:, c, t * P:(t + 1) * P], Wsm[:, 2, c, :],
                                           start=(c == 0), stop=(c == DC - 1))
                else:
                    src = HT if kind == "q" else CT
                    for c in range(DC):
                        mm = pe.matmul(bank, Wsm[:, 0 if kind == "q" else 1, c, m * P:(m + 1) * P],
                                       src[:, c, n * CH:(n + 1) * CH], start=(c == 0), stop=(c == DC - 1))
                mm.then_inc(pj_mm[bk], 1)

        def proj_kv_act(act, layer, lo, hi):
            base = pj_base(layer, "kv")
            for i, (kind, m, n) in list(enumerate(proj_steps("kv")))[lo:hi]:
                bk = i % 2
                act.wait_ge(pj_mm[bk], base + i // 2 + 1)
                bank = psum[:, 2 + bk, :]
                if kind == "v":
                    act.activation(Va[:, 2 * m:2 * m + 2, :], bank.rearrange("p (t d) -> p t d", t=2), ACT.Copy
                                   ).then_inc(pj_ev[bk], 1)
                else:
                    act.activation(KTa[:, m, n * CH:(n + 1) * CH], bank, ACT.Copy).then_inc(pj_ev[bk], 1)

        def proj_q(layer, dve=None, act=None):
            base = pj_base(layer, "q")
            for i, (kind, m, n) in enumerate(proj_steps("q")):
                bk = i % 2
                eng = act if bk or layer == 3 else dve
                if eng is None:
                    continue
                eng.wait_ge(pj_mm[bk], base + i // 2 + 1)
                dst, src = QTa[:, m, n * CH:(n + 1) * CH], psum[:, 2 + bk, :]
                if layer == 3:
                    act.activation(dst, src, ACT.Identity, bias=bq3[:, m:m + 1])
                    act.wait_ge(l2_mm, 8 + i - 3)
                    act.activation(l2_slot(i), src, ACT.Square, bias=bq3[:, m:m + 1]).then_inc(pj_ev[bk], 1)
                    continue
                if bk:
                    ins = act.activation(dst, src, ACT.Copy, scale=0.25)
                else:
                    ins = dve.tensor_scalar(dst, src, 0.25, None, ALU.mult)
                ins.then_inc(pj_ev[bk], 1)

        l2_sq, l2_mm, l2_sd, l2_mx, l2_rc, l2_sp, l2_sc = (sem(n) for n in (
            "l2_sq", "l2_sum", "l2_sqrt", "l2_max", "l2_rec", "l2_spread", "l2_scaled"))
        sm_x = sem("scale_mul")

        def ACCf(i):
            return ACC[:, 2 * i:2 * i + 2, :].rearrange("p t d -> p (t d)")

        spreadm = ACCf(7).rearrange("p (n f) -> p n f", n=NCH)

        def l2_slot(i):
            return ACCf(i % 4)

        def l2_x(i):
            return (KTa if i < 8 else QTa)[:, i // 4 % 2, i % 4 * CH:(i % 4 + 1) * CH]

        def l2_keys_pool(pool):
            pool.memset(spreadm, 0.0).then_inc(zeroed, 1)
            pool.wait_ge(zeroed, 6)
            for n in range(NCH):
                v = spreadm[:, n, :].rearrange("p (h w) -> p h w", w=16)
                pool.affine_select(out=v, in_=v, compare_op=ALU.not_equal, fill=1.0, base=-32 * n,
                                   pattern=[[-1, 8], [0, 16]], channel_multiplier=1).then_inc(spread_ready, 1)
            for bk in range(2):
                pool.wait_ge(pj_ev[bk], N_PJ + N_KV)
            for i in range(8):
                if i >= 4:
                    pool.wait_ge(l2_mm, i - 3)
                pool.tensor_tensor(l2_slot(i), l2_x(i), l2_x(i), ALU.mult).then_inc(l2_sq, 1)

        def l2_sums_pe(pe, g):
            for n in range(NCH):
                i = 4 * g + n
                if g < 2:
                    pe.wait_ge(l2_sq, i + 1)
                else:
                    pe.wait_ge(pj_ev[n % 2], N_PJ + N_KV + 2 * (g - 2) + n // 2 + 1)
                if n == 0 and g >= 2:
                    pe.wait_ge(l2_mx, g - 1)
                pe.matmul(psum[32 * n:32 * n + 32, 4 + g % 2, :], headsel[:, :], l2_slot(i), start=True, stop=True
                          ).then_inc(l2_mm, 1)

        def l2_spread_pe(pe, g):
            pe.wait_ge(l2_rc, g + 1)
            for n in range(NCH):
                i = 4 * g + n
                if i >= 2:
                    pe.wait_ge(l2_sc, i - 1)
                pe.matmul(psum[:, 6 + i % 2, :], spreadm[:, n, :], ACCf(4 + g % 2), start=True, stop=True
                          ).then_inc(l2_sp, 1)

        def l2_sqrt_act(act, g):
            act.wait_ge(l2_mx, g + 1)
            act.activation(ACCf(4 + g % 2), ACCf(4 + g % 2), ACT.Sqrt).then_inc(l2_sd, 1)

        def l2_floor_dve(dve, g):
            dve.wait_ge(l2_mm, 4 * g + 4)
            if g >= 2:
                dve.wait_ge(l2_sp, 4 * g - 4)
            dve.tensor_scalar(ACCf(4 + g % 2), psum[:, 4 + g % 2, :], NORM_EPS2, None, ALU.max).then_inc(l2_mx, 1)

        def l2_recip_dve(dve, g):
            dve.wait_ge(l2_sd, g + 1)
            dve.reciprocal(ACCf(4 + g % 2), ACCf(4 + g % 2)).then_inc(l2_rc, 1)

        def l2_scale_dve(dve, g):
            for n in range(NCH):
                i = 4 * g + n
                dve.wait_ge(l2_sp, i + 1)
                x, r = l2_x(i), psum[:, 6 + i % 2, :]
                if g >= 2:
                    dve.scalar_tensor_tensor(out=x, in0=x, scalar=smul[:, g - 2:g - 1], in1=r, op0=ALU.mult,
                                             op1=ALU.mult).then_inc(l2_sc, 1)
                else:
                    dve.tensor_tensor(x, x, r, ALU.mult).then_inc(l2_sc, 1)

        def is0(b):
            return isinstance(b, int) and b == 0

        def last2(b):
            return isinstance(b, int) and b == BATCH - 1

        def base2(b, bk):
            if is0(b):
                return 4
            return b * 8 + 4 if bk else b * 9 + 3

        def fill_of(b, g):
            if g % 2 == 0:
                return 1, 2 + g // 2
            return 0, (2 if is0(b) else 3) + (0 if g == 1 else 1 if last2(b) else 5)

        def qk_fill(b, bk):
            return 3 if is0(b) and bk == 0 else 4

        def empty2(pe, b, bk, i):
            pe.wait_ge(l2_emptied[bk], base2(b, bk) + i + 1)

        def full2(eng, b, bk, i):
            eng.wait_ge(l2_filled[bk], base2(b, bk) + i + 1)

        def stage2_pool(pool, b):
            s = att[2]
            pool.wait_ge(s.s, b * NH + 1)
            pool.tensor_copy(CTb[:, :, :], CT[:, :, bs(b)]).then_inc(s.v, 1)

        def att2_pool(pool):
            with pool.Fori(0, BATCH) as b:
                stage2_pool(pool, b)

        def qk_wait(eng, sems, b, bk, n):
            if b is None:
                eng.wait_ge(sems[bk], n + 1)
            else:
                eng.wait_ge(sems[bk], base2(b, bk) + qk_fill(b, bk) + n + 1)

        def qk_pe(pe, b, n):
            w = n // 2
            cols = bs(0) if b is None else bs(b + 1)
            for bk in range(2):
                j = 2 * (n % 2) + bk
                qk_wait(pe, l2_emptied, b, bk, n)
                for h in range(2):
                    m = 2 * j + h
                    for c in range(DC):
                        mm = pe.matmul(psum[:, 6 + bk, h * SEQ:(h + 1) * SEQ], Wqkv[:, w, c, m * P:(m + 1) * P],
                                       (HT, CT)[w][:, c, cols], start=(c == 0), stop=(c == DC - 1))
                mm.then_inc(l2_filled[bk], 1)

        def qk_dve(dve, b, n):
            w, j = n // 2, 2 * (n % 2)
            qk_wait(dve, l2_filled, b, 0, n)
            if b is not None:
                dve.wait_ge(att[2].s, b * NH + NH + 1)
            src = psum[:, 6, :].rearrange("p (m t) -> p m t", m=2)
            if w == 0:
                ins = dve.scalar_tensor_tensor(
                    out=Q2[:, 2 * j:2 * j + 2, :], in0=src, scalar=0.125,
                    in1=bq8[:, 2 * j:2 * j + 2].unsqueeze(2).broadcast_to([P, 2, SEQ]), op0=ALU.mult, op1=ALU.add)
            else:
                for h in range(2):
                    q = slice(64 * h, 64 * h + 64)
                    ins = dve.tensor_tensor(
                        K2[q, h, 2 * j:2 * j + 2, :], src[q], bqk[q, 1, 2 * j:2 * j + 2].unsqueeze(2).broadcast_to(
                            [64, 2, SEQ]), ALU.add)
            ins.then_inc(l2_emptied[0], 1)

        def qk_act(act, b, n):
            w, j = n // 2, 2 * (n % 2) + 1
            qk_wait(act, l2_filled, b, 1, n)
            if b is not None:
                act.wait_ge(att[2].s, b * NH + NH + 1)
            for h in range(2):
                m = 2 * j + h
                src = psum[:, 7, h * SEQ:(h + 1) * SEQ]
                if w == 0:
                    ins = act.activation(Q2[:, m, :], src, ACT.Identity, bias=bq8[:, m:m + 1], scale=0.125)
                else:
                    for o in range(2):
                        q = slice(64 * o, 64 * o + 64)
                        ins = act.activation(K2[q, o, m, :], src[q], ACT.Identity, bias=bqk[q, 1, m:m + 1])
            ins.then_inc(l2_emptied[1], 1)

        def values2_pe(pe, b):
            s = att[2]
            pe.wait_ge(s.v, b + 1)
            for t in range(TPB):
                for bk in range(2):
                    empty2(pe, b, bk, t)
                    for c in range(DC):
                        mm = pe.matmul(psum[:, 6 + bk, :], CTb[:, c, t * P:(t + 1) * P],
                                       Wqkv[:, 2, c, bk * 512:(bk + 1) * 512], start=(c == 0), stop=(c == DC - 1))
                    mm.then_inc(l2_filled[bk], 1)
            for bk in range(2):
                empty2(pe, b, bk, 2)

        def values2_dve(dve, b):
            s = att[2]
            dve.wait_ge(s.av, b * QUAD + 2)
            for t in range(TPB):
                for bk in range(2):
                    full2(dve, b, bk, t)
                    cols = slice(bk * 512, (bk + 1) * 512)
                    dve.tensor_tensor(V2[:, t, cols], psum[:, 6 + bk, :], bv2[:, cols], ALU.add).then_inc(l2_emptied[bk], 1)

        def pv2_pe(pe, b, g):
            s = att[2]
            copied(pe, 2, b, QUAD * g + QUAD - 1)
            pe.wait_ge(s.on, b * QUAD + g + 1)
            for m in range(2):
                for kt in range(TPB):
                    for n in range(2):
                        k = QUAD * g + 2 * m + n
                        mm = pe.matmul(psum[64 * n:64 * n + 64, 4 + g % 2, m * SEQ:(m + 1) * SEQ],
                                       V2[:, kt, 64 * k:64 * k + 64], PTb[:, k % TS, kt, :], start=(kt == 0),
                                       stop=(kt == TPB - 1))
            mm.then_inc(s.av, 1)

        def recip2_dve(dve, b, g):
            s = att[2]
            dve.wait_ge(s.p, b * NH + QUAD * (g + 1) + PS)
            dve.reciprocal(rrec[:, :, QUAD * g:QUAD * (g + 1)], rsums(b, QUAD * g, QUAD)).then_inc(s.rr, 1)

        def spread2_pe(pe, b, g):
            s = att[2]
            bk, i = fill_of(b, g)
            pe.wait_ge(s.rx, b * QUAD + g + 1)
            empty2(pe, b, bk, i)
            for m in range(2):
                for qt in range(TPB):
                    mm = pe.transpose(psum[:, 6 + bk, m * SEQ + qt * P:m * SEQ + (qt + 1) * P],
                                      Rsb2[:, qt, m * P:(m + 1) * P], ident[:, :])
            mm.then_inc(l2_filled[bk], 1)

        def widen2_act(act, b, g):
            s = att[2]
            act.wait_ge(s.rr, b * QUAD + g + 1)
            act.activation(Rsb2[:, :, :].rearrange("p q (h w) -> p q h w", w=64),
                           rrec[:, :, QUAD * g:QUAD * (g + 1)].unsqueeze(3).broadcast_to([P, TPB, QUAD, 64]), ACT.Copy
                           ).then_inc(s.rx, 1)

        def spread2_act(act, b, g):
            s = att[2]
            bk, i = fill_of(b, g)
            full2(act, b, bk, i)
            act.activation(Rsb2[:, :, :], psum[:, 6 + bk, :].rearrange("p (c t) -> p c t", c=DC), ACT.Copy
                           ).then_inc(l2_emptied[bk], 1)

        def onorm2_dve(dve, b, g):
            s = att[2]
            bk, i = fill_of(b, g)
            dve.wait_ge(s.av, b * QUAD + g + 3)
            dve.wait_ge(l2_emptied[bk], base2(b, bk) + i + 2)
            dve.tensor_tensor(OT2[:, 2 * g:2 * g + 2, :], psum[:, 4 + g % 2, :].rearrange("p (c t) -> p c t", c=DC),
                              Rsb2[:, :, :], ALU.mult).then_inc(s.on, 1)

        def wo2_pe(pe, nb, i):
            s = att[2]
            pe.wait_ge(s.on, nb * QUAD + 2)
            empty2(pe, nb, 0, i)
            for qt in range(TPB):
                for m in range(8):
                    mm = pe.matmul(psum[:, 6, qt * D:(qt + 1) * D], OT2[:, m, qt * P:(qt + 1) * P], Wo2[:, m, :],
                                   start=(m == 0), stop=(m == 7))
            mm.then_inc(l2_filled[0], 1)

        L2N = slice(TT - TPB, TT)

        def y2_wait(dve, nb, n):
            dve.wait_ge(ln2, nb * 14 + (n - 14))
            dve.sem_inc(waited, 1)

        def y2_dve(dve, nb, i):
            full2(dve, nb, 0, i)
            dve.tensor_tensor(xtmp[:, :, :], psum[:, 6, :].rearrange("p (q d) -> p q d", q=TPB),
                              bo_bc[:, 1, :].unsqueeze(1).broadcast_to([P, TPB, D]), ALU.add).then_inc(l2_emptied[0], 1)
            dve.wait_ge(l2_emptied[0], base2(nb, 0) + i + 2)
            dve.tensor_tensor(xtmp[:, :, :], xtmp[:, :, :], Hn[:, bs(nb - 1, TPB), :], ALU.add).then_inc(ln2, 1)

        def y2_stats_dve(dve, nb):
            y2_wait(dve, nb, 1)
            for q in range(TPB):
                dve.bn_stats(lnst[:, TT - TPB + q, :], xtmp[:, q, :]).then_inc(ln2, 1)

        def y2_aggr_dve(dve, nb):
            y2_wait(dve, nb, 3)
            for q in range(TPB):
                dve.bn_aggr(lnmv[:, TT - TPB + q, :], lnst[:, TT - TPB + q, :]).then_inc(ln2, 1)

        def y2_act(act, nb):
            act.wait_ge(ln2, nb * 14 + (5 - 14))
            act.activation(lnsd[:, L2N], lnmv[:, L2N, 1], ACT.Sqrt, bias=eps[:, 0:1]).then_inc(ln2_sd, 1)

        def y2_rstd_dve(dve, nb):
            dve.wait_ge(ln2_sd, nb * 1)
            dve.reciprocal(lnrs[:, L2N], lnsd[:, L2N]).then_inc(ln2, 1)
            y2_wait(dve, nb, 6)
            dve.tensor_tensor(lnsd[:, L2N], lnrs[:, L2N], lnrs[:, L2N], ALU.mult).then_inc(ln2, 1)
            y2_wait(dve, nb, 7)
            dve.scalar_tensor_tensor(out=lnsd[:, L2N], in0=lnmv[:, L2N, 1], scalar=eps[:, 0:1], in1=lnsd[:, L2N],
                                     op0=ALU.add, op1=ALU.mult).then_inc(ln2, 1)
            y2_wait(dve, nb, 8)
            dve.tensor_scalar(lnsd[:, L2N], lnsd[:, L2N], -0.5, 1.5, ALU.mult, ALU.add).then_inc(ln2, 1)
            y2_wait(dve, nb, 9)
            dve.tensor_tensor(lnrs[:, L2N], lnrs[:, L2N], lnsd[:, L2N], ALU.mult).then_inc(ln2, 1)

        def y2_apply_dve(dve, nb):
            y2_wait(dve, nb, 10)
            for q in range(TPB):
                t = TT - TPB + q
                dve.tensor_scalar(xtmp[:, q, :], xtmp[:, q, :], lnmv[:, t, 0:1], lnrs[:, t:t + 1],
                                  ALU.subtract, ALU.mult).then_inc(ln2, 1)

        def y2_affine_dve(dve, nb):
            for n, (vec, op) in enumerate(((lng2, ALU.mult), (lnb2, ALU.add))):
                y2_wait(dve, nb, 12 + n)
                dve.tensor_tensor(xtmp[:, :, :], xtmp[:, :, :], vec.unsqueeze(1).broadcast_to([P, TPB, D]), op
                                  ).then_inc(ln2, 1)

        def y2_xadd_dve(dve, nb):
            y2_wait(dve, nb, 14)
            xb = X[:, bs(nb - 1, TPB), :]
            dve.scalar_tensor_tensor(out=xb, in0=xtmp[:, :, :], scalar=tg[:, 2:3], in1=xb, op0=ALU.mult, op1=ALU.add
                                     ).then_inc(x_upd, 1)

        TAIL = NH + 5
        LAST_WO = -4
        Y2_STEPS = {1: y2_stats_dve, 2: y2_aggr_dve, 6: y2_rstd_dve, 7: y2_apply_dve, 10: y2_affine_dve, 11: y2_xadd_dve}

        def att2_body_pe(pe, b, first):
            values2_pe(pe, b)
            if not first:
                wo2_pe(pe, b, 2)
            for k in range(TAIL):
                if k < NH:
                    scores_pe(pe, 2, b, k)
                if T_LAG2 <= k < NH + T_LAG2:
                    ptrans_pe(pe, 2, b, k - T_LAG2)
                if k >= 6 and (k - 6) % 4 == 0:
                    pv2_pe(pe, b, (k - 6) // 4)
                if NH <= k < NH + 4 and not last2(b):
                    qk_pe(pe, b, k - NH)
                if k >= 7 and (k - 7) % 4 == 0:
                    spread2_pe(pe, b, (k - 7) // 4)

        def att2_body_act(act, b, first):
            for k in range(TAIL):
                if not first and k == 5:
                    y2_act(act, b)
                if k < NH:
                    exp_act(act, 2, b, k)
                if k >= 5 and (k - 5) % 4 == 0 and k < NH + 4:
                    widen2_act(act, b, (k - 5) // 4)
                if NH <= k < NH + 4 and not last2(b):
                    qk_act(act, b, k - NH)
                if k >= 7 and (k - 7) % 4 == 0:
                    spread2_act(act, b, (k - 7) // 4)

        def att2_body_dve(dve, b, first):
            values2_dve(dve, b)
            for k in range(TAIL):
                if k < NH:
                    max_dve(dve, 2, b, k)
                if T_LAG2 <= k < NH + T_LAG2:
                    pcopy_dve(dve, 2, b, k - T_LAG2)
                if k >= 5 and (k - 5) % 4 == 0 and k < NH + 4:
                    recip2_dve(dve, b, (k - 5) // 4)
                if NH <= k < NH + 4 and not last2(b):
                    qk_dve(dve, b, k - NH)
                if k >= 8 and (k - 8) % 4 == 0:
                    onorm2_dve(dve, b, (k - 8) // 4)
                if first:
                    continue
                if k == 0:
                    y2_dve(dve, b, 2)
                elif k in Y2_STEPS:
                    Y2_STEPS[k](dve, b)

        def att2_pe(pe, layer):
            for n in range(4):
                qk_pe(pe, None, n)
            att2_body_pe(pe, 0, True)
            with pe.Fori(1, BATCH - 1) as b:
                att2_body_pe(pe, b, False)
            att2_body_pe(pe, BATCH - 1, False)
            wo2_pe(pe, BATCH, LAST_WO)

        def att2_act(act, layer):
            for n in range(4):
                qk_act(act, None, n)
            att2_body_act(act, 0, True)
            with act.Fori(1, BATCH - 1) as b:
                att2_body_act(act, b, False)
            att2_body_act(act, BATCH - 1, False)
            y2_act(act, BATCH)

        def att2_dve(dve, layer):
            for n in range(4):
                qk_dve(dve, None, n)
            att2_body_dve(dve, 0, True)
            with dve.Fori(1, BATCH - 1) as b:
                att2_body_dve(dve, b, False)
            att2_body_dve(dve, BATCH - 1, False)
            dve.wait_ge(x_upd, x_after(1, True) + BATCH - 1)
            stats_tiles(dve, ST[(2, True)], X, 0, TT - TPB)
            y2_dve(dve, BATCH, LAST_WO)
            for k in sorted(Y2_STEPS):
                Y2_STEPS[k](dve, BATCH)

        def logits_pe(pe, layer, n, g):
            f = ffn[layer]
            for c in range(DC):
                pe.wait_ge(tpe_done[c], 4 * tn(layer, True) + g + 1)
            for t in range(4 * g, 4 * g + 4):
                for c in range(DC):
                    mm = pe.matmul(psum[:, 4, t * WE:t * WE + n], HT[:, c, t * P:(t + 1) * P], wr[:, layer - 1, c, 0:n],
                                   start=(c == 0), stop=(c == DC - 1))
            mm.then_inc(f.lg, 1)

        steps = [0]

        def routing_dve(dve, layer, n):
            f = ffn[layer]

            def link(ins):
                steps[0] += 1
                ins.then_inc(chain, 1)
                dve.wait_ge(chain, steps[0])

            def row(x):
                return x.unsqueeze(2).broadcast_to([P, TT, n])

            if layer == 1:
                dve.wait_ge(consts, N_CONST + MAXT + 1)
            z = lg[:, :, 0:n]
            t0, t1, pr, msk = (rt[:, i, :, 0:n] for i in range(4))
            o1, o2, rv = oh1[:, :, 0:n], oh2[:, :, 0:n], rev[:, :, 0:n]
            link(dve.memset(rt[:, 3, :, :], 0.0))
            dve.wait_ge(f.lg, 4)
            ps = psum[:, 4, 0:TT * WE].rearrange("p (t e) -> p t e", e=WE)[:, :, 0:n]
            if layer == 1:
                link(dve.tensor_tensor(z, ps, rbias[:, 0, 0:n].unsqueeze(1).broadcast_to([P, TT, n]), ALU.mult))
                dve.sem_inc(rt_in, 1)
                dve.wait_ge(rt_out, 1)
                val = pr
            elif layer == 2:
                link(dve.tensor_tensor(z, ps, rbias[:, 1, 0:n].unsqueeze(1).broadcast_to([P, TT, n]), ALU.add))
                link(dve.tensor_reduce(r1[:, 0, :], z, AX.X, ALU.max))
                link(dve.tensor_tensor(z, z, row(r1[:, 0, :]), ALU.subtract))
                dve.sem_inc(rt_in, 1)
                dve.wait_ge(rt_out, 2)
                link(dve.tensor_reduce(r1[:, 0, :], pr, AX.X, ALU.add))
                link(dve.reciprocal(r1[:, 1, :], r1[:, 0, :]))
                link(dve.tensor_tensor(pr, pr, row(r1[:, 1, :]), ALU.mult))
                val = pr
            else:
                link(dve.tensor_copy(z, ps))
                val = z

            def pick(values, best, onehot):
                link(dve.tensor_reduce(best, values, AX.X, ALU.max))
                link(dve.tensor_tensor(t0, values, row(best), ALU.is_equal))
                link(dve.tensor_tensor(t0, t0, rv, ALU.mult))
                link(dve.tensor_reduce(r1[:, 3, :], t0, AX.X, ALU.max))
                link(dve.tensor_tensor(onehot, t0, row(r1[:, 3, :]), ALU.is_equal))

            pick(val, r1[:, 0, :], o1)
            link(dve.scalar_tensor_tensor(out=t1, in0=o1, scalar=-BIG, in1=val, op0=ALU.mult, op1=ALU.add))
            pick(t1, r1[:, 1, :], o2)
            link(dve.tensor_tensor(msk, o1, o2, ALU.add))
            if layer == 1:
                link(dve.tensor_tensor(r1[:, 2, :], r1[:, 0, :], r1[:, 1, :], ALU.add))
                link(dve.reciprocal(r1[:, 3, :], r1[:, 2, :]))
                link(dve.tensor_tensor(gate2[:, :, :], r1[:, 0:2, :], r1[:, 3, :].unsqueeze(1).broadcast_to([P, 2, TT]),
                                       ALU.mult))
            elif layer == 2:
                link(dve.tensor_copy(gate2[:, :, :], r1[:, 0:2, :]))
            else:
                link(dve.tensor_tensor(r1[:, 2, :], r1[:, 1, :], r1[:, 0, :], ALU.subtract))
                dve.sem_inc(rt_in, 1)
                dve.wait_ge(rt_out, 3)
                link(dve.tensor_scalar(r1[:, 2, :], r1[:, 1, :], 1.0, None, ALU.add))
                link(dve.reciprocal(gate2[:, 0, :], r1[:, 2, :]))
                link(dve.tensor_tensor(gate2[:, 1, :], r1[:, 1, :], gate2[:, 0, :], ALU.mult))
            link(dve.tensor_scalar(gate2[:, :, :], gate2[:, :, :], tg[:, 4 + layer:5 + layer], None, ALU.mult))
            link(dve.memset(pfxa[:, :, :], 0.0))
            link(dve.tensor_copy(pfxa[:, 1:TT + 1, 0:n], msk))
            src, dst = pfxa, pfxb
            for d in (1, 2, 4, 8):
                dve.tensor_copy(dst[:, 0:d, :], src[:, 0:d, :]).then_inc(chain, 1)
                steps[0] += 1
                link(dve.tensor_tensor(dst[:, d:, :], src[:, d:, :], src[:, 0:TT + 1 - d, :], ALU.add))
                src, dst = dst, src
            dve.sem_inc(pfx, 1)
            dve.wait_ge(pfx, 3 * layer - 1)
            link(dve.tensor_copy(rank[:, :, 0:n], psum[:, 5, 0:(TT + 1) * WE].rearrange("p (t e) -> p t e", e=WE)[:, :, 0:n]))
            dve.sem_inc(pfx, 1)
            tot, ntl, base, base2_ = (small8[:, i, :] for i in range(4))
            link(dve.memset(small8[:, :, :], 0.0))
            if layer == 3:
                link(dve.tensor_scalar(tot[:, 0:n], rank[:, TT, 0:n], float(CAP), None, ALU.min))
            else:
                link(dve.tensor_copy(tot[:, 0:n], rank[:, TT, 0:n]))
            link(dve.scalar_tensor_tensor(
                out=cmp_t[:, :, :], in0=tileno[:, 0:8].unsqueeze(1).broadcast_to([P, WE, 8]), scalar=float(GT),
                in1=tot.unsqueeze(2).broadcast_to([P, WE, 8]), op0=ALU.mult, op1=ALU.is_lt))
            link(dve.tensor_reduce(ntl, cmp_t[:, :, :], AX.X, ALU.add))
            link(dve.tensor_copy(base[:, 1:WE], ntl[:, 0:WE - 1]))
            src, dst = base, base2_
            for d in (1, 2, 4):
                dve.tensor_copy(dst[:, 0:d], src[:, 0:d]).then_inc(chain, 1)
                steps[0] += 1
                link(dve.tensor_tensor(dst[:, d:], src[:, d:], src[:, 0:WE - d], ALU.add))
                src, dst = dst, src
            first = src
            nt = TILES[layer]
            link(dve.tensor_tensor(cmp_w[:, 0:nt, 0:n], first[:, 0:n].unsqueeze(1).broadcast_to([P, nt, n]),
                                   tileno[:, 0:nt].unsqueeze(2).broadcast_to([P, nt, n]), ALU.is_le))
            link(dve.tensor_reduce(tile_f[:, 0:nt], cmp_w[:, 0:nt, 0:n], AX.X, ALU.add))
            link(dve.tensor_scalar(tile_f[:, 0:nt], tile_f[:, 0:nt], float(P), nrow[:, 0:1], ALU.mult, ALU.add))
            link(dve.tensor_copy(w_idx[:, 0:nt], tile_f[:, 0:nt]))
            link(dve.tensor_scalar(first, first, float(GT), -1.0, ALU.mult, ALU.add))
            link(dve.tensor_tensor(slot_f[:, :, 0:n], rank[:, 0:TT, 0:n],
                                   first[:, 0:n].unsqueeze(1).broadcast_to([P, TT, n]), ALU.add))
            for k, one in enumerate((o1, o2)):
                link(dve.tensor_tensor(t0, one, slot_f[:, :, 0:n], ALU.mult))
                link(dve.tensor_reduce(tok_f[:, k, :], t0, AX.X, ALU.add))
            if layer == 3:
                link(dve.tensor_scalar(t1, rank[:, 0:TT, 0:n], CAP + 0.5, None, ALU.is_lt))
                for k, one in enumerate((o1, o2)):
                    link(dve.tensor_tensor(t0, one, t1, ALU.mult))
                    link(dve.tensor_reduce(tok_f[:, 2 + k, :], t0, AX.X, ALU.add))
                keep = tok_f[:, 2:4, :]
                link(dve.tensor_tensor(gate2[:, :, :], gate2[:, :, :], keep, ALU.mult))
                link(dve.tensor_tensor(tok_f[:, 0:2, :], tok_f[:, 0:2, :], keep, ALU.mult))
                link(dve.tensor_copy(g_idx[:, :, :], tok_f[:, 0:2, :]))
                link(dve.tensor_scalar(keep, keep, -SKIP, SKIP, ALU.mult, ALU.add))
                link(dve.tensor_tensor(tok_f[:, 0:2, :], tok_f[:, 0:2, :], keep, ALU.add))
            else:
                link(dve.tensor_copy(g_idx[:, :, :], tok_f[:, 0:2, :]))
            link(dve.tensor_copy(s_idx[:, :, :], tok_f[:, 0:2, :]))
            dve.sem_inc(moe.idx, 1)

        def routing_act(act, layer):
            if layer == 1:
                act.wait_ge(rt_in, 1)
                act.activation(rt[:, 2, :, 0:7], lg[:, :, 0:7], ACT.Sigmoid).then_inc(rt_out, 1)
            elif layer == 2:
                act.wait_ge(rt_in, 2)
                act.activation(rt[:, 2, :, 0:4], lg[:, :, 0:4], ACT.Exp).then_inc(rt_out, 1)
            else:
                act.wait_ge(rt_in, 3)
                act.activation(r1[:, 1, :], r1[:, 2, :], ACT.Exp).then_inc(rt_out, 1)

        def ranks_pe(pe, layer):
            pe.wait_ge(pfx, 3 * layer - 2)
            pe.matmul(psum[:, 5, 0:(TT + 1) * WE], ones[:, :], pfxa[:, :, :].rearrange("p t e -> p (t e)"),
                      start=True, stop=False, skip_group_check=True)
            pe.matmul(psum[:, 5, 0:TT * WE], tril[:, :], rt[:, 3, :, :].rearrange("p t e -> p (t e)"),
                      start=False, stop=True, skip_group_check=True).then_inc(pfx, 1)

        def ffn_shape(layer):
            return {1: (F1, F1_LAST, True), 2: (F2, P, False), 3: (F3, P, True)}[layer]

        def wviews(layer, s):
            w = wslot[s]
            if layer == 1:
                g = w[:, 0:1408].rearrange("p (c n) -> p c n", c=DC)
                u = w[:, 1408:2816].rearrange("p (c n) -> p c n", c=DC)
                return g, u, w[:, 2816:4352].rearrange("p (f n) -> p f n", f=F1)
            if layer == 2:
                return (w[:, 0:2048].rearrange("p (c n) -> p c n", c=DC), None,
                        w[:, 2048:4096].rearrange("p (f n) -> p f n", f=F2))
            w1 = w[:, 0:2048].rearrange("p (c n) -> p c n", c=DC)
            return w1[:, :, 0:512], w1[:, :, 512:1024], w[:, 2048:3072].rearrange("p (f n) -> p f n", f=F3)

        def b1c(s, k):
            return wslot[s][:, 4096 + k:4097 + k]

        def b2c(s):
            return wslot[s][:, 4104:4104 + D]

        def wsl(layer, e):
            return 1 if layer == 1 else e

        def ffn_loads(sp, layer):
            f = ffn[layer]
            sp.wait_ge(x_upd, x_after(layer, False))
            for e in range(SHARED[layer]):
                sp.dma_start(wslot[wsl(layer, e)][:, 0:WROW[layer]], a[f"f{layer}s"][e * P:(e + 1) * P, :]
                             ).then_inc(f.w[e], 16)

        def ffn_pe(pe, layer):
            f = ffn[layer]
            nf, last_w, gated = ffn_shape(layer)
            for e in range(SHARED[layer]):
                g, u, d = wviews(layer, wsl(layer, e))
                pe.wait_ge(f.w[e], 16)
                def chunk(i, c, first=False):
                    at = bass.ds(i * (2 * CH) + c * CH, CH) if not isinstance(i, int) else slice(
                        (2 * i + c) * CH, (2 * i + c + 1) * CH)
                    for k in range(nf):
                        w = last_w if k == nf - 1 else P
                        n = (e * NCH + c) * nf + k
                        pe.wait_ge(f.hid, i * (2 * nf) + (n + 1))
                        if w < P:
                            pe.sem_inc(waited_pe, 1)
                        for wv, bank in ((g, 0), (u, 2)):
                            if wv is None:
                                continue
                            for kc in range(DC):
                                mm = pe.matmul(psum[0:w, bank + n % 2, :], wv[:, kc, k * P:k * P + w], HT[:, kc, at],
                                               start=(kc == 0), stop=(kc == DC - 1))
                        mm.then_inc(f.up, 1)
                    if first:
                        ranks_pe(pe, layer)
                    if (e, c) == (0, 0):
                        pe.wait_ge(pfx, 3 * layer)
                    for tt in range(TPC):
                        pe.wait_ge(f.acc, i * 8 + ((e * NCH + c) * 4 + tt + 1))
                        for k in range(nf):
                            if tt == 0:
                                pe.wait_ge(f.hid, i * (2 * nf) + ((e * NCH + c) * nf + k + 3))
                            w = last_w if k == nf - 1 else P
                            mm = pe.matmul(psum[:, 4 + tt, 0:D], hid[0:w, c, k, tt * P:(tt + 1) * P], d[0:w, k, :],
                                           start=(k == 0), stop=(k == nf - 1))
                        mm.then_inc(f.down, 1)
                if layer == 2 and e == 0:
                    for i in range(NCH // 2):
                        for c in range(2):
                            chunk(i, c, (i, c) == (0, 0))
                else:
                    with pe.Fori(0, NCH // 2) as i:
                        for c in range(2):
                            chunk(i, c)

        def ffn_act(act, layer):
            f = ffn[layer]
            nf, last_w, gated = ffn_shape(layer)
            for e in range(SHARED[layer]):
                if layer == 2:
                    act.wait_ge(f.w[e], 16)
                with act.Fori(0, NCH // 2) as i:
                    for c in range(2):
                        if layer == 2:
                            act.wait_ge(f.down, i * 8 + (4 * (e * NCH + c) + 4))
                        for k in range(nf):
                            w = last_w if k == nf - 1 else P
                            n = (e * NCH + c) * nf + k
                            act.wait_ge(f.up, i * (2 * nf) + (n + 1))
                            if layer == 2:
                                act.activation(hid[:, c, k, :], psum[:, n % 2, :], ACT.Relu,
                                               bias=b1c(wsl(layer, e), k)).then_inc(f.hid, 1)
                            else:
                                act.wait_ge(f.hid, i * (2 * nf) + (n + 1))
                                act.activation(sg[0:w, n % 2, :], psum[0:w, n % 2, :], ACT.Silu).then_inc(f.act, 1)

        def ffn_dve(dve, layer):
            f = ffn[layer]
            nf, last_w, gated = ffn_shape(layer)
            dve.wait_ge(f.init, 1)
            for e in range(SHARED[layer]):
                if layer == 2:
                    dve.wait_ge(f.w[e], 16)
                with dve.Fori(0, NCH // 2) as i:
                    for c in range(2):
                        if gated:
                            dve.wait_ge(f.down, i * 8 + (4 * (e * NCH + c) + 4))
                            for k in range(nf):
                                w = last_w if k == nf - 1 else P
                                n = (e * NCH + c) * nf + k
                                dve.wait_ge(f.act, i * (2 * nf) + (n + 1))
                                dve.tensor_tensor(hid[0:w, c, k, :], sg[0:w, n % 2, :], psum[0:w, 2 + n % 2, :],
                                                  ALU.mult).then_inc(f.hid, 1)
                        for tt in range(TPC):
                            n = 4 * (e * NCH + c) + tt
                            dve.wait_ge(f.down, i * 8 + (n + 9))
                            y = psum[:, 4 + tt, 0:D]
                            if layer == 2:
                                dve.tensor_tensor(dtmp[:, tt % 2, :], y, b2c(e), ALU.add).then_inc(f.tmp, 1)
                                dve.wait_ge(f.tmp, i * 8 + (n + 1))
                                y = dtmp[:, tt % 2, :]
                            row = ACC[:, bass.ds(i * 8 + (c * TPC + tt), 1), :].squeeze(1)
                            dve.scalar_tensor_tensor(out=row, in0=y, scalar=1.0 / SHARED[layer], in1=row,
                                                     op0=ALU.mult, op1=ALU.add).then_inc(f.acc, 1)
            dve.wait_ge(f.acc, 16 * SHARED[layer] + 4)

        def t_base(layer):
            return sum(TILES[n] for n in range(1, layer))

        def h_base(layer):
            return sum(TILES[n] * ffn_shape(n)[0] for n in range(1, layer))

        def p_base(layer, s):
            return sum((TILES[n] + 1 - s) // 2 for n in range(1, layer))

        def moe_loop(eng, layer, body, ahead=1, start=0):
            nt = TILES[layer]
            pairs = (nt - ahead) // 2
            with eng.Fori(start, pairs) as i:
                for s in range(2):
                    body(i, s, True)
            for w in range(2 * pairs, nt):
                body(w // 2, w % 2, w + ahead < nt)

        def tiles_of(rows, i, s):
            v = rows.rearrange("(w t p) d -> w p t d", t=GTT, p=P)
            w = i * 2 + s
            return v[w] if isinstance(w, int) else v[bass.ds(w, 1)].squeeze(0)

        def moe_sp(sp, layer):
            tb = t_base(layer)

            def load(i, s):
                sp.wait_ge(moe.tr, i * 2 + (tb + s + 1))
                sp.dma_start(XG[:, s, :, :], tiles_of(xrows, i, s)).then_inc(moe.xg[s], 16)

            def body(i, s, more):
                if more:
                    load(i + 1, s)
                sp.wait_ge(moe.y, i * 2 + (tb + s + 3))
                sp.dma_start(tiles_of(yrows, i, s), YO[:, s, :, :]).then_inc(moe.ys[s], 16)
            sp.wait_ge(moe.sc, 16 * TOPK * TT * layer)
            for s in range(2):
                load(0, s)
            moe_loop(sp, layer, body, ahead=2)

        def moe_pool(pool, layer):
            tb = t_base(layer)
            nt = TILES[layer]
            rows = nt * GT
            pool.wait_ge(moe.idx, layer)
            if layer == 1:
                pool.wait_ge(zrows, 16)
            for t in range(TT):
                for k in range(TOPK):
                    pool.indirect_dma_start(xrows[:, :], bass.IndirectOffsetOnAxis(s_idx[:, k, t:t + 1], 0), Hn[:, t, :],
                                            None, bounds_check=MAXT * GT - 1, oob_is_err=False).then_inc(moe.sc, 16)

            def weights(i, s, more):
                pool.wait_ge(moe.y, i * 2 + (tb + s + 1))
                src = w_idx[:, 2 * i + s:2 * i + s + 1] if isinstance(i, int) else w_idx[:, bass.ds(i * 2 + s, 1)]
                pool.tensor_copy(w_now[:, s:s + 1], src).then_inc(moe.wi, 1)
                pool.wait_ge(moe.wi, i * 2 + (tb + s + 1))
                pool.sem_inc(waited_pool, 1)
                pool.indirect_dma_start(wslot[s][:, 0:WROW[layer]], None, a[f"f{layer}r"],
                                        bass.IndirectOffsetOnAxis(w_now[:, s:s + 1], 0)).then_inc(moe.w[s], 16)
            for s in range(2):
                if layer == 1 and s == 1 or layer == 2:
                    pool.wait_ge(ffn[layer].acc, 16 * (s + 1 if layer == 2 else 1) + 4)
                weights(0, s, True)
            moe_loop(pool, layer, weights, start=1)
            for s in range(2):
                pool.wait_ge(moe.ys[s], 16 * (p_base(layer, s) + (nt + 1 - s) // 2) + 16)
            for t in range(TT):
                if t >= 4:
                    pool.wait_ge(moe.cb, 2 * TT * (layer - 1) + cb_second(t - 4))
                for k in range(TOPK):
                    pool.indirect_dma_start(YG[:, t % 4, k, :], None, yrows[0:rows, :],
                                            bass.IndirectOffsetOnAxis(g_idx[:, k, t:t + 1], 0)).then_inc(moe.g[t % 4], 16)

        def moe_pe(pe, layer):
            nf, last_w, gated = ffn_shape(layer)
            tb, hb = t_base(layer), h_base(layer)

            def transposes(i, s, pb):
                pe.wait_ge(moe.xg[s], i * 16 + 16 * (pb + 1))
                for t in range(GTT):
                    for c in range(DC):
                        mm = pe.transpose(psum[:, 6 + s, c * GT + t * P:c * GT + (t + 1) * P],
                                          XG[:, s, t, c * P:(c + 1) * P], ident[:, :])
                mm.then_inc(moe.tr, 1)

            def body(i, s, more):
                g, u, d = wviews(layer, s)
                pe.wait_ge(moe.w[s], i * 16 + 16 * (p_base(layer, s) + 1))
                pe.wait_ge(moe.xt, i * 2 + (tb + s + 1))
                for k in range(nf):
                    w = last_w if k == nf - 1 else P
                    n = s * nf + k
                    pe.wait_ge(moe.hid, i * (2 * nf) + (hb + n + 1))
                    for wv, bank in ((g, 0), (u, 2)):
                        if wv is None:
                            continue
                        for kc in range(DC):
                            mm = pe.matmul(psum[0:w, bank + n % 2, 0:GT], wv[:, kc, k * P:k * P + w], XT[:, s, kc, :],
                                           start=(kc == 0), stop=(kc == DC - 1))
                    mm.then_inc(moe.up, 1)
                if more:
                    transposes(i + s, 1 - s, p_base(layer, 1 - s))
                pe.wait_ge(moe.y, i * 2 + (tb + s + 1))
                for t in range(GTT):
                    for k in range(nf):
                        if t == 0:
                            pe.wait_ge(moe.hid, i * (2 * nf) + (hb + s * nf + k + 3))
                        w = last_w if k == nf - 1 else P
                        mm = pe.matmul(psum[:, 4 + s, t * D:(t + 1) * D], hidT[0:w, k, t * P:(t + 1) * P], d[0:w, k, :],
                                       start=(k == 0), stop=(k == nf - 1))
                mm.then_inc(moe.down, 1)
            if SHARED[layer]:
                pe.wait_ge(ffn[layer].acc, 16 * SHARED[layer] + 4)
            transposes(0, 0, p_base(layer, 0))
            moe_loop(pe, layer, body)

        def store_free(eng, layer, i, s):
            eng.wait_ge(moe.ys[s], i * 16 + 16 * (p_base(layer, s) + 1) - 0)

        def y_act(act, layer, i, s):
            act.wait_ge(moe.down, i * 2 + (t_base(layer) + s + 1))
            store_free(act, layer, i, s)
            act.activation(YO[:, s, :, :], psum[:, 4 + s, :].rearrange("p (t d) -> p t d", t=GTT), ACT.Copy
                           ).then_inc(moe.y, 1)

        def moe_act(act, layer):
            nf, last_w, gated = ffn_shape(layer)
            hb = h_base(layer)

            def body(i, s, more):
                if layer == 2:
                    act.wait_ge(moe.w[s], i * 16 + 16 * (p_base(layer, s) + 1))
                for k in range(nf):
                    w = last_w if k == nf - 1 else P
                    n = s * nf + k
                    act.wait_ge(moe.up, i * (2 * nf) + (hb + n + 1))
                    if layer == 2:
                        act.activation(hidT[:, k, :], psum[:, n % 2, 0:GT], ACT.Relu, bias=b1c(s, k)
                                       ).then_inc(moe.hid, 1)
                    else:
                        act.wait_ge(moe.hid, i * (2 * nf) + (hb + n + 1))
                        act.activation(sg[0:w, n % 2, 0:GT], psum[0:w, n % 2, 0:GT],
                                       ACT.Silu if layer == 1 else ACT.Gelu).then_inc(moe.act, 1)
                if gated:
                    y_act(act, layer, i, s)
            moe_loop(act, layer, body)

        def moe_dve(dve, layer):
            nf, last_w, gated = ffn_shape(layer)
            tb, hb = t_base(layer), h_base(layer)
            ab = {1: 0, 2: 0, 3: TILES[1] * F1}[layer]

            def copy(i, s):
                dve.wait_ge(moe.tr, i * 2 + (tb + s + 3))
                dve.tensor_copy(XT[:, s, :, :], psum[:, 6 + s, :].rearrange("p (c t) -> p c t", c=DC)
                                ).then_inc(moe.xt, 1)

            def body(i, s, more):
                if gated:
                    for k in range(nf):
                        w = last_w if k == nf - 1 else P
                        n = s * nf + k
                        dve.wait_ge(moe.act, i * (2 * nf) + (ab + n + 1))
                        dve.tensor_tensor(hidT[0:w, k, :], sg[0:w, n % 2, 0:GT], psum[0:w, 2 + n % 2, 0:GT],
                                          ALU.mult).then_inc(moe.hid, 1)
                if more:
                    copy(i + s, 1 - s)
                if not gated:
                    dve.wait_ge(moe.down, i * 2 + (tb + s + 1))
                    store_free(dve, layer, i, s)
                    dve.tensor_tensor(YO[:, s, :, :], psum[:, 4 + s, :].rearrange("p (t d) -> p t d", t=GTT),
                                      b2c(s).unsqueeze(1).broadcast_to([P, GTT, D]), ALU.add).then_inc(moe.y, 1)
            copy(0, 0)
            moe_loop(dve, layer, body)

        def cb_first(t):
            return 2 * t if t else 1

        def cb_second(t):
            return 2 * t + 3 if t < TT - 1 else 2 * TT

        def combine_dve(dve, layer):
            base = 2 * TT * (layer - 1)

            def add(t, k):
                dve.scalar_tensor_tensor(out=X[:, t, :], in0=YG[:, t % 4, k, :], scalar=gate2[:, k, t:t + 1],
                                         in1=X[:, t, :], op0=ALU.mult, op1=ALU.add).then_inc(moe.cb, 1)
            m = ST[(layer + 1, False)] if layer < 3 else None
            for t in range(TT + 2):
                if t < TT:
                    dve.wait_ge(moe.g[t % 4], 32 * (4 * (layer - 1) + t // 4 + 1))
                    add(t, 0)
                if 1 <= t <= TT:
                    dve.wait_ge(moe.cb, base + cb_first(t - 1))
                    add(t - 1, 1)
                if t >= 2 and m is not None:
                    dve.wait_ge(moe.cb, base + cb_second(t - 2))
                    stats_tiles(dve, m, X, t - 2, t - 1)
            dve.wait_ge(moe.cb, base + 2 * TT)
            dve.sem_inc(x_upd, 4)

        def xadd_all(dve, n, src, gate, per, signal=x_upd):
            for g in range(n):
                t = slice(g * per, (g + 1) * per)
                dve.scalar_tensor_tensor(out=X[:, t, :], in0=src[:, t, :], scalar=tg[:, gate:gate + 1], in1=X[:, t, :],
                                         op0=ALU.mult, op1=ALU.add).then_inc(signal, 1)

        def gains_dve(dve):
            for v in (lng, lnb):
                ins = dve.tensor_scalar(v, v, tg[:, 4:5], None, ALU.mult)
            ins.then_inc(gains, 1)

        def bias0_pool(pool):
            pool.wait_ge(gains, 1)
            normed(pool, 1, TT)
            for q in range(8):
                t = slice(2 * q, 2 * q + 2)
                pool.tensor_tensor(X[:, t, :], X[:, t, :], lnb.unsqueeze(1).broadcast_to([P, 2, D]), ALU.add
                                   ).then_inc(gains, 1)

        def update0_dve(dve):
            for q in range(4):
                t = slice(4 * q, 4 * q + 4)
                normed(dve, 2, 4 * q + 4)
                dve.tensor_tensor(ACC[:, t, :], ACC[:, t, :], lng.unsqueeze(1).broadcast_to([P, 4, D]), ALU.mult
                                  ).then_inc(chain, 1)
            steps[0] += 4
            for q in range(4):
                t = slice(4 * q, 4 * q + 4)
                dve.wait_ge(chain, steps[0] - 3 + q)
                dve.wait_ge(gains, 1 + 2 * (q + 1))
                dve.tensor_tensor(X[:, t, :], X[:, t, :], ACC[:, t, :], ALU.add).then_inc(x_upd, 1)

        def tn(layer, ff):
            return {(0, False): 1, (1, False): 2, (1, True): 3, (2, False): 4, (2, True): 5, (3, False): 6, (3, True): 7}[
                (layer, ff)]
        ST = {(0, False): 0, (0, True): 1, (1, False): 3, (1, True): 4, (2, False): 5, (2, True): 6, (3, False): 7,
              (3, True): 8}

        rt_in, rt_out = sem("rt_in"), sem("rt_out")
        mask1 = sem("mask1")
        shared_in = sem("shared_in")
        SUB = [(l, ff) for l in range(4) for ff in (False, True)][:stop_after]

        def more(layer):
            return len(SUB) > 2 * layer + 2
        N_SMALL = 17
        N_CONST = 20

        def att_weights(sp, layer):
            for w in range(3):
                sp.dma_start(Wsm[:, w, :, :], a[f"w{layer}"][w].rearrange("(c p) n -> p c n", p=P)
                             ).then_inc(ld_att[layer], 16)
            if layer == 1:
                sp.dma_start(bv1, a["bv1"].partition_broadcast(P)).then_inc(ld_att[1], 16)
            else:
                sp.dma_start(biasL[:, :, :], a["fside"].rearrange("(t p) k -> p t k", p=P)).then_inc(ld_att[3], 16)

        def wo_load(sp, layer):
            sp.dma_start(Wo[:, :, :], a[f"w{layer}"][3].rearrange("(c p) n -> p c n", p=P)).then_inc(ld_wo, 16)

        @block.sync
        def _(sp):
            xv = a["x"].rearrange("(t p) d -> p t d", p=P)
            for s in range(2):
                sp.sem_inc(moe.ys[s], 16)
            sp.dma_start(X[:, :, :], xv).then_inc(ld_x, 16)
            sp.dma_start(Va[:, :, :], a["ctx"].rearrange("(t p) d -> p t d", p=P)).then_inc(ld_ctx, 16)
            small = [(mask8[:, 0:TOK], a["mask"].partition_broadcast(P)), (qm8[:, :], a["maskT"]),
                     (graw[:, :], a["gates"].partition_broadcast(P)),
                     (lng, a["ln_g0"].partition_broadcast(P)), (lnb, a["ln_b0"].partition_broadcast(P)),
                     (bo_bc[:, 0, :], a["bo1"].partition_broadcast(P)), (bo_bc[:, 1, :], a["bo2"].partition_broadcast(P)),
                     (bo_bc[:, 2, :], a["bo3"].partition_broadcast(P)),
                     (rbias[:, 0, 0:7], a["rbias"].partition_broadcast(P)),
                     (rbias[:, 1, 0:4], a["gate_b"].partition_broadcast(P)),
                     (wr[:, 0, :, 0:7], a["wr1"].rearrange("(c p) e -> p c e", p=P)),
                     (wr[:, 1, :, 0:4], a["wr2"].rearrange("(c p) e -> p c e", p=P)),
                     (wr[:, 2, :, 0:8], a["wr3"].rearrange("(c p) e -> p c e", p=P)),
                     (bqk[:, 0, :], a["bq2"]), (bqk[:, 1, :], a["bk2"]), (bq3[:, :], a["bq3"]), (smul[:, :], a["smul"])]
            assert len(small) == N_SMALL
            for dst, src in small:
                sp.dma_start(dst, src).then_inc(ld_small, 16)

            for layer, ff in SUB:
                if ff and layer:
                    if SHARED[layer]:
                        ffn_loads(sp, layer)
                    if layer == 2:
                        att_weights(sp, 3)
                    moe_sp(sp, layer)
                elif ff:
                    sp.wait_ge(x_upd, x_after(0, False))
                    att_weights(sp, 1)
                    sp.wait_ge(zrows, 16)
                    wo_load(sp, 1)
                elif layer == 2:
                    sp.wait_ge(moe.y, t_base(2) + 2)
                    for w in range(3):
                        for c in range(DC):
                            sp.wait_ge(moe.cb, 4 * (DC * w + c) + 2)
                            sp.dma_start(Wqkv[:, w, c, :], a["w2"][w][c * P:(c + 1) * P, :]).then_inc(ld_att[2], 16)
                    for c in range(2):
                        sp.wait_ge(moe.cb, 26 + 4 * c)
                        sp.dma_start(Wo2[:, 4 * c:4 * c + 4, :],
                                     a["wo2"][4 * c * P:4 * (c + 1) * P, :].rearrange("(c p) n -> p c n", p=P)
                                     ).then_inc(ld_att[2], 16)
                    for dst, name in ((bv2, "bv2"), (lng2, "ln_g2"), (lnb2, "ln_b2")):
                        sp.dma_start(dst, a[name].partition_broadcast(P)).then_inc(ld_att[2], 16)
                else:
                    if layer == 3:
                        sp.wait_ge(moe.y, t_base(3) + 2)
                        wo_load(sp, 3)
                    att_sp(sp, layer)
                    if layer == 0:
                        sp.wait_ge(zeroed, 1)
                        sp.dma_start(xrows.rearrange("(t p) d -> p t d", p=P),
                                     zeros.unsqueeze(1).broadcast_to([P, MAXT * GTT, D])).then_inc(zrows, 16)
            ov = out.rearrange("(t p) d -> p t d", p=P)
            if SUB[-1] == (3, True):
                for q in range(4):
                    sp.wait_ge(moe.cb, 4 * TT + cb_second(4 * q + 3))
                    sp.dma_start(ov[:, 4 * q:4 * q + 4, :], X[:, 4 * q:4 * q + 4, :]).then_inc(out_done, 16)
                sp.wait_ge(out_done, 64)
            else:
                sp.wait_ge(x_upd, x_after(*SUB[-1]))
                sp.dma_start(ov, X[:, :, :]).then_inc(out_done, 16)
                sp.wait_ge(out_done, 16)

        @block.gpsimd
        def _(pool):
            n = [0]
            pool.memset(zeros, 0.0).then_inc(zeroed, 1)

            def step(ins, wait=True):
                n[0] += 1
                ins.then_inc(consts, 1)
                if wait:
                    pool.wait_ge(consts, n[0])
            pool.memset(ident[:, :], 0.0).then_inc(consts, 1)
            pool.memset(ones[:, :], 1.0).then_inc(consts, 1)
            pool.memset(tril[:, :], 1.0).then_inc(consts, 1)
            pool.memset(headsel[:, :], 1.0).then_inc(consts, 1)
            pool.memset(causal0[:, :, :], -NEG_BIAS).then_inc(consts, 1)
            n[0] = 5
            for e in range(WE):
                step(pool.memset(rev[:, :, e], float(WE - e)), wait=False)
            step(pool.memset(eps[:, :], EPS))
            step(pool.affine_select(out=ident[:, :], in_=ident[:, :], compare_op=ALU.not_equal, fill=1.0, base=0,
                                    pattern=[[-1, P]], channel_multiplier=1))
            step(pool.affine_select(out=tril[:, :], in_=tril[:, :], compare_op=ALU.is_ge, fill=0.0, base=0,
                                    pattern=[[1, P]], channel_multiplier=-1))
            step(pool.affine_select(out=headsel[:, :], in_=headsel[:, :], compare_op=ALU.is_ge, fill=0.0, base=0,
                                    pattern=[[-16, 32]], channel_multiplier=1))
            step(pool.affine_select(out=headsel[:, :], in_=headsel[:, :], compare_op=ALU.is_ge, fill=0.0, base=15,
                                    pattern=[[16, 32]], channel_multiplier=-1))
            for qt in range(TPB):
                step(pool.affine_select(out=causal0[:, qt, :], in_=causal0[:, qt, :], compare_op=ALU.is_ge, fill=0.0,
                                        base=P * qt, pattern=[[-1, SEQ]], channel_multiplier=1))
            for w in range(MAXT + 1):
                pool.memset(tileno[:, w:w + 1], float(w)).then_inc(consts, 1)

            for layer, ff in SUB:
                if not ff:
                    if layer == 2:
                        pool.wait_ge(x_upd, x_after(1, True))
                        pool.memset(K2[:, :, :, :], 0.0).then_inc(zeroed, 1)
                        att2_pool(pool)
                        continue
                    if layer != 1:
                        if layer:
                            pool.wait_ge(x_upd, x_after(layer - 1, True))
                        pool.memset(Vpad[:, :, :, :], 0.0).then_inc(zeroed, 1)
                    if layer == 1:
                        pool.wait_ge(x_upd, x_after(0, False))
                        pool.memset(biasL[:, :, :], 0.0).then_inc(zeroed, 1)
                        pool.wait_ge(zeroed, 3)
                        for qt in range(TPB):
                            ins = pool.affine_select(out=biasL[:, qt, :], in_=biasL[:, qt, :], compare_op=ALU.is_ge,
                                                     fill=MASKED, base=P * qt - 1, pattern=[[-1, SEQ]],
                                                     channel_multiplier=1)
                            ins.then_inc(mask1, 1)
                        pool.wait_ge(mask1, 2)
                        pool.memset(biasL[0:1, 0, 0:1], 0.0).then_inc(mask1, 1)
                    if layer == 0:
                        pool.wait_ge(ld_ctx, 16)
                        for c in range(DC):
                            pool.wait_ge(tpe_done[c], 4 * tn(0, False) + 4)
                    else:
                        if layer == 3:
                            l2_keys_pool(pool)
                        for bk in range(2):
                            pool.wait_ge(pj_ev[bk], N_PJ * (1 if layer == 1 else 2))
                        if layer == 3:
                            pool.wait_ge(l2_sc, 16)
                    pool.wait_ge(zeroed, {0: 2, 1: 3, 3: 5}[layer])
                    att_pool(pool, layer)
                elif not layer:
                    bias0_pool(pool)
                elif layer:
                    if SHARED[layer]:
                        pool.wait_ge(x_upd, x_after(layer, False))
                        pool.memset(ACC[:, :, :], 0.0).then_inc(ffn[layer].init, 1)
                    moe_pool(pool, layer)

        @block.tensor
        def _(pe):
            pe.sem_inc(moe.tr, 2)
            pe.wait_ge(consts, N_CONST)
            for n in range(4):
                pe.sem_inc(att[n].s, 1)
                pe.sem_inc(att[n].t, PS)
                pe.sem_inc(att[n].av, 2)
            for n in range(1, 3):
                pe.sem_inc(ffn[n].down, 8)
            pe.wait_ge(ld_ctx, 16)
            transposes_pe(pe, 0, Va, lambda g: None)
            for layer, ff in SUB:
                if (layer, ff) == (3, False):
                    pe.wait_ge(moe.y, t_base(3) + 2)
                    pe.wait_ge(spread_ready, NCH)
                    for g in range(2):
                        l2_sums_pe(pe, g)
                if (layer, ff) != (0, True):
                    m = ST[(layer, ff)]
                    transposes_pe(pe, tn(layer, ff), Hn, lambda g: normed(pe, m, 4 * g + 4),
                                  (lambda g: logits_pe(pe, layer, ROUTED[layer], g)) if ff else None)
                if not ff:
                    if layer == 1:
                        proj_pe(pe, layer, "q")
                    if layer == 3:
                        proj_pe(pe, layer, "q", 0, 4)
                        l2_spread_pe(pe, 0)
                        l2_sums_pe(pe, 2)
                        proj_pe(pe, layer, "q", 4, 8)
                        for g in (1, 2, 3):
                            if g == 2:
                                l2_sums_pe(pe, 3)
                            l2_spread_pe(pe, g)
                    if layer == 2:
                        pe.wait_ge(ld_att[2], 16 * 11)
                        for c in range(DC):
                            pe.wait_ge(tpe_done[c], 4 * tn(2, False) + 4)
                    (att2_pe if layer == 2 else att_pe)(pe, layer)
                elif layer:
                    if layer != 2:
                        ranks_pe(pe, layer)
                    ffn_pe(pe, layer)
                    moe_pe(pe, layer)
                    if layer == 2 and more(layer):
                        proj_pe(pe, 3, "kv")
                elif more(layer):
                    proj_pe(pe, 1, "kv")

        @block.scalar
        def _(act):
            for n in range(4):
                act.sem_inc(att[n].p, PS)
            act.sem_inc(act_copied, len(ACT_COPIES))
            act.wait_ge(consts, N_CONST)
            norm_sqrt(act, 0)
            transposes_copy_act(act, 0, CT)
            norm_apply_act(act, 0, X, Hn)
            act.wait_ge(ld_small, 16 * N_SMALL)
            act.activation(tg[:, :], graw[:, :], ACT.Tanh).then_inc(tg_done, 1)
            act.mul(bq8[:, :], bqk[:, 0, :], 0.125).then_inc(tg_done, 1)
            act.wait_ge(sm_x, 1)
            act.activation(smul[:, :], smul[:, :], ACT.Exp).then_inc(sm_x, 1)
            act.wait_ge(tg_done, 2)
            for layer, ff in SUB:
                if (layer, ff) != (0, False):
                    norm_sqrt(act, ST[(layer, ff)])
                    norm_apply_act(act, ST[(layer, ff)], X, Hn)
                if (layer, ff) == (0, True):
                    if more(layer):
                        act.wait_ge(x_upd, x_after(0, False))
                        proj_kv_act(act, 1, 0, N_KV)
                    norm_sqrt(act, 2)
                    norm_apply_act(act, 2, Hn, ACC)
                    if more(layer):
                        proj_kv_act(act, 1, N_KV, 2 * N_KV)
                else:
                    transposes_copy_act(act, tn(layer, ff), HT, 0.25 if (layer, ff) == (0, False) else 1.0)
                if not ff:
                    if layer == 3:
                        for g in range(2):
                            l2_sqrt_act(act, g)
                    if layer in (1, 3):
                        proj_q(layer, act=act)
                    if layer == 3:
                        for g in (2, 3):
                            l2_sqrt_act(act, g)
                    if layer == 2:
                        act.wait_ge(zeroed, 4)
                    (att2_act if layer == 2 else att_act)(act, layer)
                elif layer:
                    routing_act(act, layer)
                    ffn_act(act, layer)
                    moe_act(act, layer)
                    if layer == 2 and more(layer):
                        act.wait_ge(moe.y, t_base(3) + 2)
                        proj_kv_act(act, 3, 0, 2 * N_KV)

        @block.vector
        def _(dve):
            for n in range(4):
                dve.sem_inc(att[n].sm, 4)
                dve.sem_inc(att[n].pt, NH if n == 2 else NH - len(ACT_COPIES))
                dve.sem_inc(att[n].on, 1 if n != 2 else 2)
                dve.sem_inc(att[n].fin, 1)
            for bk in range(2):
                dve.sem_inc(l2_emptied[bk], 1)
            for n in range(1, 3):
                dve.sem_inc(ffn[n].hid, 2)
                dve.sem_inc(ffn[n].acc, 4)
            dve.sem_inc(moe.hid, 2)
            dve.sem_inc(moe.y, 2)
            norm_stats(dve, 0, X, (ld_x, 16))
            transposes_copy_dve(dve, 0, CT)
            norm_apply(dve, 0, X, Hn)
            dve.wait_ge(consts, N_CONST)
            dve.wait_ge(ld_small, 16 * N_SMALL)
            dve.tensor_reduce(nrow[:, :], tril[:, :], AX.X, ALU.add, negate=True).then_inc(dve_consts, 1)
            dve.tensor_scalar(smul[:, :], smul[:, :], LOG_MAX_SCALE, None, ALU.min).then_inc(sm_x, 1)
            dve.tensor_copy(maskf, mask8[:, 0:TOK])
            dve.tensor_copy(qm[:, :], qm8[:, :]).then_inc(dve_consts, 1)
            dve.wait_ge(dve_consts, 2)
            for layer, ff in SUB:
                m = ST[(layer, ff)]
                if m:
                    ahead = {(0, True): TT - TPB, (1, False): 0, (1, True): TT - TPB, (2, False): TT, (2, True): TT - TPB,
                             (3, False): TT, (3, True): TT - TPB}[(layer, ff)]
                    last = x_after(*SUB[2 * layer + int(ff) - 1])
                    norm_stats(dve, m, X, (x_upd, last), ahead)
                    norm_apply(dve, m, X, Hn)
                if (layer, ff) == (0, True):
                    gains_dve(dve)
                    normed(dve, 1, TT)
                    norm_stats(dve, 2, Hn, (h_done, TT))
                    norm_apply(dve, 2, Hn, ACC)
                    update0_dve(dve)
                    continue
                transposes_copy_dve(dve, tn(layer, ff), HT, 0.25 if (layer, ff) == (0, False) else 1.0)
                if not ff:
                    if layer == 0:
                        dve.wait_ge(tg_done, 2)
                        for c in range(DC):
                            dve.wait_ge(tpe_done[c], 4 * tn(0, False) + 4)
                    if layer == 3:
                        dve.wait_ge(sm_x, 2)
                        for part, g in ((l2_floor_dve, 0), (l2_floor_dve, 1), (l2_recip_dve, 0), (l2_recip_dve, 1),
                                        (l2_scale_dve, 0), (l2_floor_dve, 2), (l2_scale_dve, 1), (l2_recip_dve, 2),
                                        (l2_floor_dve, 3), (l2_recip_dve, 3), (l2_scale_dve, 2), (l2_scale_dve, 3)):
                            part(dve, g)
                        dve.wait_ge(l2_sc, 16)
                    if layer == 1:
                        proj_q(layer, dve=dve)
                        for bk in range(2):
                            dve.wait_ge(pj_ev[bk], N_PJ)
                        dve.wait_ge(mask1, 3)
                    if layer == 2:
                        dve.wait_ge(ld_att[2], 16 * 11)
                        dve.wait_ge(zeroed, 4)
                    (att2_dve if layer == 2 else att_dve)(dve, layer)
                else:
                    routing_dve(dve, layer, ROUTED[layer])
                    if SHARED[layer]:
                        ffn_dve(dve, layer)
                    moe_dve(dve, layer)
                    if SHARED[layer]:
                        xadd_all(dve, 4, ACC, 4 + layer, 4, shared_in)
                        dve.wait_ge(shared_in, 4 * layer)
                    combine_dve(dve, layer)


def arrays_of(i):
    import numpy as np

    def rows(x, p=128):
        return np.ascontiguousarray(np.asarray(x).reshape(-1, p).T)

    def join(*xs):
        return np.ascontiguousarray(np.concatenate([np.asarray(x) for x in xs], 0))

    def stack(*xs):
        return np.ascontiguousarray(np.stack([np.asarray(x) for x in xs], 0))

    g = {k: np.asarray(v) for k, v in i.items()}
    mask = g["mask_BxS2_bf1"].view(np.uint8).reshape(-1)

    def experts(*mats, biases=None):
        e = mats[0].shape[0]
        parts = []
        for m in mats:
            k = -(-m.shape[1] // 128)
            full = np.zeros((e, k * 128, m.shape[2]), m.dtype)
            full[:, :m.shape[1]] = m
            parts.append(full.reshape(e, k, 128, m.shape[2]).transpose(0, 2, 1, 3).reshape(e, 128, -1))
        if biases:
            b1, b2 = biases
            parts.append(b1.reshape(e, -1, 128).transpose(0, 2, 1))
            parts.append(np.broadcast_to(b2[:, None, :], (e, 128, b2.shape[1])))
        return np.ascontiguousarray(np.concatenate(parts, 2).reshape(e * 128, -1))

    return {
        "x": g["x"].reshape(2048, 256), "ctx": g["ctx_1024"].reshape(2048, 256), "fside": g["fside_SxS2_0"],
        "mask": np.ascontiguousarray(mask), "maskT": rows(mask),
        "gates": join(g["g_xattn"], g["g_ffn"]), "ln_g0": g["L0_ffn_ln_g"], "ln_b0": g["L0_ffn_ln_b"],
        "w1": stack(g["L1_xattn_Wq"].T, g["L1_xattn_Wk"].T, g["L1_xattn_Wv"].T, g["L1_xattn_Wo"].T),
        "bv1": g["L1_xattn_bv"], "bo1": g["L1_xattn_bo"],
        "f1s": experts(g["L1_ffn_shared_gate"][None], g["L1_ffn_shared_up"][None], g["L1_ffn_shared_down"][None]),
        "f1r": experts(g["L1_ffn_routed_gate"], g["L1_ffn_routed_up"], g["L1_ffn_routed_down"]),
        "wr1": g["L1_ffn_Wr"], "rbias": g["L1_ffn_routing_bias"],
        "w2": stack(g["L2_xattn_Wq"], g["L2_xattn_Wk"], g["L2_xattn_Wv"]), "wo2": g["L2_xattn_Wo"],
        "bq2": rows(g["L2_xattn_bq"]), "bk2": rows(g["L2_xattn_bk"]), "bv2": g["L2_xattn_bv"], "bo2": g["L2_xattn_bo"],
        "ln_g2": g["L2_xattn_ln_gamma"], "ln_b2": g["L2_xattn_ln_beta"],
        "wr2": g["L2_ffn_gate_w"], "gate_b": g["L2_ffn_gate_b"],
        "f2s": experts(g["L2_ffn_sw1"], g["L2_ffn_sw2"], biases=(g["L2_ffn_sb1"], g["L2_ffn_sb2"])),
        "f2r": experts(g["L2_ffn_rw1"], g["L2_ffn_rw2"], biases=(g["L2_ffn_rb1"], g["L2_ffn_rb2"])),
        "w3": stack(g["L3_xattn_Wq"], g["L3_xattn_Wk"], g["L3_xattn_Wv"], g["L3_xattn_Wo"]),
        "bq3": rows(g["L3_xattn_bq"]), "bo3": g["L3_xattn_bo"],
        "smul": rows(np.repeat(g["L3_xattn_scale_mul_log"].reshape(16), 16)),
        "wr3": np.ascontiguousarray(g["L3_ffn_Wg"].T), "f3r": experts(g["L3_ffn_W1"], g["L3_ffn_W2"]),
    }


def kernel(**inputs):
    import numpy as _np
    import concourse.bacc as _bacc
    from concourse import mybir as _mybir
    from concourse.bass_utils import run_bass_kernel_spmd as _run

    nc = _bacc.Bacc("TRN2", target_bir_lowering=False, num_devices=1)
    arrays, args = {}, {}
    for name, arr in arrays_of(inputs).items():
        arr = _np.ascontiguousarray(arr)
        arrays[f"in_{name}"] = arr
        args[name] = nc.dram_tensor(f"in_{name}", arr.shape, _mybir.dt.from_np(arr.dtype), kind="ExternalInput").ap()
    out = nc.dram_tensor("out_x", (TOK, D), F32, kind="ExternalOutput").ap()
    build(nc, args, out)
    r = _run(nc, [arrays], core_ids=[0])
    return r.results[0]["out_x"].reshape(BATCH, SEQ, D)
```
